# Optimizing a Trainium2 kernel written in Bass

```python
import numpy as np
import jax
import jax.numpy as jnp

def _softmax(x, axis=-1):
    return jax.nn.softmax(x, axis=axis)

def _gelu(x):
    return jax.nn.gelu(x, approximate=True)

def _silu(x):
    return jax.nn.silu(x)

def _sigmoid(x):
    return jax.nn.sigmoid(x)

def _layernorm(x, axis=-1, eps=1e-05):
    m = jnp.mean(x, axis=axis, keepdims=True)
    v = jnp.var(x, axis=axis, keepdims=True)
    return (x - m) / jnp.sqrt(v + eps)

def _scatter_add(tgt, idx, src, axis=0):
    return tgt.at[idx].add(src)

def _segment_sum(src, seg, n):
    return jax.ops.segment_sum(src, seg, n)
kernel_name = 'mk_seq_preln_d2_jaxref_r8_7b863f'

def setup_inputs(seed: int=0):
    np.random.seed(seed)
    _w = jnp.asarray

    def _L0_attn_setup():
        import math
        import jax, jax.numpy as jnp
        import numpy as np

        def get_alibi_slopes(n_heads: int) -> jnp.ndarray:

            def _pow2_slopes(n):
                i = jnp.arange(1, n + 1, dtype=jnp.float32)
                return jnp.power(2.0, -8.0 * i / n)
            if n_heads & n_heads - 1 == 0:
                return _pow2_slopes(n_heads)
            nearest = 2 ** math.ceil(math.log2(n_heads))
            full = _pow2_slopes(nearest)
            half = nearest // 2
            half_slopes = _pow2_slopes(half)
            extra = full[jnp.arange(half) * 2 + 1]
            return jnp.concatenate([half_slopes, extra])[:n_heads]

        def build_alibi_bias(n_heads: int, T: int, causal: bool=True) -> jnp.ndarray:
            slopes = get_alibi_slopes(n_heads)
            idx = jnp.arange(T)
            rel = jnp.abs(idx[:, None] - idx[None, :]).astype(jnp.float32)
            bias = -slopes[:, None, None] * rel[None]
            if causal:
                future = idx[None, :] > idx[:, None]
                bias = jnp.where(future[None], -jnp.inf, bias)
            return bias
        key = jax.random.key(seed)
        ks = jax.random.split(key, 5)
        B, T, C = (2, 256, 128)
        s = 0.02
        return {'x': jax.random.normal(ks[0], (B, T, C), dtype=jnp.float32), 'Wq': jax.random.normal(ks[1], (C, C), dtype=jnp.float32) * s, 'Wk': jax.random.normal(ks[2], (C, C), dtype=jnp.float32) * s, 'Wv': jax.random.normal(ks[3], (C, C), dtype=jnp.float32) * s, 'Wo': jax.random.normal(ks[4], (C, C), dtype=jnp.float32) * s}
    _L0_attn_in = _L0_attn_setup()

    def _L0_ffn_setup():
        import jax, jax.numpy as jnp
        import numpy as np
        D = 128
        HD = 128
        EA = 8
        KA = 2
        EF = 16
        KF = 2
        FH = 64
        MAXP = 64
        B, S = (4, 128)
        EPS = 1e-05

        def _layer_norm(x, w, b):
            mu = x.mean(-1, keepdims=True)
            var = ((x - mu) ** 2).mean(-1, keepdims=True)
            return (x - mu) * jax.lax.rsqrt(var + EPS) * w + b

        def _topk_gates(logits, k):
            top_vals, top_idx = jax.lax.top_k(logits, k)
            g = jax.nn.softmax(top_vals, axis=-1)
            onehot = jax.nn.one_hot(top_idx, logits.shape[-1], dtype=logits.dtype)
            return jnp.einsum('...k,...ke->...e', g, onehot)

        def _moa(x, gate_w, q_w, q_b, k_w, k_b, v_w, v_b, o_w, o_b, rel_table):
            S_ = x.shape[1]
            gates = _topk_gates(x @ gate_w, KA)
            q = (jnp.einsum('bsd,edh->bseh', x, q_w) + q_b) * HD ** (-0.5)
            k = x @ k_w + k_b
            v = x @ v_w + v_b
            scores = jnp.einsum('bqeh,bkh->beqk', q, k)
            rel_s = jnp.einsum('bqeh,rh->beqr', q, rel_table)
            pos = jnp.arange(S_)
            rel_idx = jnp.clip(pos[None, :] - pos[:, None], -MAXP, MAXP) + MAXP
            scores = scores + jnp.take_along_axis(rel_s, rel_idx[None, None], axis=-1)
            p = jax.nn.softmax(scores, axis=-1)
            ctx = jnp.einsum('beqk,bkh->bqeh', p, v)
            out = jnp.einsum('bqeh,ehd,bqe->bqd', ctx, o_w, gates)
            return out + jnp.einsum('bqe,ed->bqd', gates, o_b)

        def _moe_ffn(x, gate_w, w1, b1, w2, b2):
            gates = _topk_gates(x @ gate_w, KF)
            h = jax.nn.relu(jnp.einsum('bsd,edh->bseh', x, w1) + b1)
            out = jnp.einsum('bseh,ehd,bse->bsd', h, w2, gates)
            return out + jnp.einsum('bse,ed->bsd', gates, b2)
        key = jax.random.key(seed)
        ks = jax.random.split(key, 12)
        r = lambda i, shape, scale=0.02: jax.random.normal(ks[i], shape, jnp.float32) * scale
        return {'src': jax.random.normal(ks[0], (B, S, D), jnp.float32), 'ln1_w': jnp.ones((D,), jnp.float32), 'ln1_b': jnp.zeros((D,), jnp.float32), 'ln2_w': jnp.ones((D,), jnp.float32), 'ln2_b': jnp.zeros((D,), jnp.float32), 'attn_gate_w': r(1, (D, EA)), 'q_w': r(2, (EA, D, HD)), 'q_b': jnp.zeros((EA, HD), jnp.float32), 'k_w': r(3, (D, HD)), 'k_b': jnp.zeros((HD,), jnp.float32), 'v_w': r(4, (D, HD)), 'v_b': jnp.zeros((HD,), jnp.float32), 'o_w': r(5, (EA, HD, D)), 'o_b': jnp.zeros((EA, D), jnp.float32), 'rel_table': r(6, (2 * MAXP + 1, HD)), 'ff_gate_w': r(7, (D, EF)), 'ff_w1': r(8, (EF, D, FH)), 'ff_b1': jnp.zeros((EF, FH), jnp.float32), 'ff_w2': r(9, (EF, FH, D)), 'ff_b2': jnp.zeros((EF, D), jnp.float32)}
    _L0_ffn_in = _L0_ffn_setup()

    def _L1_attn_setup():
        import jax, jax.numpy as jnp
        import numpy as np
        B, T, C = (2, 256, 128)
        N_HEAD = 16
        HEAD_DIM = C // N_HEAD
        ATTN_MODE = 'local'
        LOCAL_ATTN_CTX = 32

        def build_mask(n, attn_mode, local_attn_ctx):
            i = jnp.arange(n)[:, None]
            j = jnp.arange(n)[None, :]
            causal = j <= i
            if attn_mode == 'all':
                return causal
            if attn_mode == 'local':
                return causal & (j >= i - local_attn_ctx)
            if attn_mode == 'strided':
                return causal & (j % local_attn_ctx == 0)
            raise ValueError(attn_mode)
        key = jax.random.key(seed)
        k1, k2, k3 = jax.random.split(key, 3)
        s = 0.02
        return {'x': jax.random.normal(k1, (B, T, C), dtype=jnp.float32), 'W_attn': jax.random.normal(k2, (C, 3 * C), dtype=jnp.float32) * s, 'b_attn': jnp.zeros((3 * C,), dtype=jnp.float32), 'W_proj': jax.random.normal(k3, (C, C), dtype=jnp.float32) * s, 'b_proj': jnp.zeros((C,), dtype=jnp.float32)}
    _L1_attn_in = _L1_attn_setup()

    def _L1_ffn_setup():
        import jax, jax.numpy as jnp
        import numpy as np
        D, F, E, K = (128, 344, 8, 2)
        key = jax.random.key(seed)
        k0, k1, k2, k3, k4 = jax.random.split(key, 5)
        s = 0.02
        x = jax.random.normal(k0, (2, 64, D), jnp.float32)
        Ws = jax.random.normal(k1, (D, E), jnp.float32) * s
        bs = jnp.zeros((E,), jnp.float32)
        Wg = jax.random.normal(k2, (E, D, F), jnp.float32) * s
        Wu = jax.random.normal(k3, (E, D, F), jnp.float32) * s
        Wd = jax.random.normal(k4, (E, F, D), jnp.float32) * s
        return {'x': x, 'Ws': Ws, 'bs': bs, 'Wg': Wg, 'Wu': Wu, 'Wd': Wd}
    _L1_ffn_in = _L1_ffn_setup()
    _d = {'L0_attn_x': _L0_attn_in['x'], 'L0_attn_Wq': _L0_attn_in['Wq'], 'L0_attn_Wk': _L0_attn_in['Wk'], 'L0_attn_Wv': _L0_attn_in['Wv'], 'L0_attn_Wo': _L0_attn_in['Wo'], 'L0_ffn_ln1_w': _L0_ffn_in['ln1_w'], 'L0_ffn_ln1_b': _L0_ffn_in['ln1_b'], 'L0_ffn_ln2_w': _L0_ffn_in['ln2_w'], 'L0_ffn_ln2_b': _L0_ffn_in['ln2_b'], 'L0_ffn_attn_gate_w': _L0_ffn_in['attn_gate_w'], 'L0_ffn_q_w': _L0_ffn_in['q_w'], 'L0_ffn_q_b': _L0_ffn_in['q_b'], 'L0_ffn_k_w': _L0_ffn_in['k_w'], 'L0_ffn_k_b': _L0_ffn_in['k_b'], 'L0_ffn_v_w': _L0_ffn_in['v_w'], 'L0_ffn_v_b': _L0_ffn_in['v_b'], 'L0_ffn_o_w': _L0_ffn_in['o_w'], 'L0_ffn_o_b': _L0_ffn_in['o_b'], 'L0_ffn_rel_table': _L0_ffn_in['rel_table'], 'L0_ffn_ff_gate_w': _L0_ffn_in['ff_gate_w'], 'L0_ffn_ff_w1': _L0_ffn_in['ff_w1'], 'L0_ffn_ff_b1': _L0_ffn_in['ff_b1'], 'L0_ffn_ff_w2': _L0_ffn_in['ff_w2'], 'L0_ffn_ff_b2': _L0_ffn_in['ff_b2'], 'L1_attn_W_attn': _L1_attn_in['W_attn'], 'L1_attn_b_attn': _L1_attn_in['b_attn'], 'L1_attn_W_proj': _L1_attn_in['W_proj'], 'L1_attn_b_proj': _L1_attn_in['b_proj'], 'L1_ffn_Ws': _L1_ffn_in['Ws'], 'L1_ffn_bs': _L1_ffn_in['bs'], 'L1_ffn_Wg': _L1_ffn_in['Wg'], 'L1_ffn_Wu': _L1_ffn_in['Wu'], 'L1_ffn_Wd': _L1_ffn_in['Wd']}
    _x0 = _d['L0_attn_x']
    _d['L0_attn_x'] = jax.random.normal(jax.random.fold_in(jax.random.key(seed), 1), (16, 256, 128), dtype=_x0.dtype)
    del _x0
    return _d

def reference(L0_attn_x, L0_attn_Wq, L0_attn_Wk, L0_attn_Wv, L0_attn_Wo, L0_ffn_ln1_w, L0_ffn_ln1_b, L0_ffn_ln2_w, L0_ffn_ln2_b, L0_ffn_attn_gate_w, L0_ffn_q_w, L0_ffn_q_b, L0_ffn_k_w, L0_ffn_k_b, L0_ffn_v_w, L0_ffn_v_b, L0_ffn_o_w, L0_ffn_o_b, L0_ffn_rel_table, L0_ffn_ff_gate_w, L0_ffn_ff_w1, L0_ffn_ff_b1, L0_ffn_ff_w2, L0_ffn_ff_b2, L1_attn_W_attn, L1_attn_b_attn, L1_attn_W_proj, L1_attn_b_proj, L1_ffn_Ws, L1_ffn_bs, L1_ffn_Wg, L1_ffn_Wu, L1_ffn_Wd):

    def _L0_attn_ref(x, Wq, Wk, Wv, Wo):
        import math
        import jax, jax.numpy as jnp
        import numpy as np

        def get_alibi_slopes(n_heads: int) -> jnp.ndarray:

            def _pow2_slopes(n):
                i = jnp.arange(1, n + 1, dtype=jnp.float32)
                return jnp.power(2.0, -8.0 * i / n)
            if n_heads & n_heads - 1 == 0:
                return _pow2_slopes(n_heads)
            nearest = 2 ** math.ceil(math.log2(n_heads))
            full = _pow2_slopes(nearest)
            half = nearest // 2
            half_slopes = _pow2_slopes(half)
            extra = full[jnp.arange(half) * 2 + 1]
            return jnp.concatenate([half_slopes, extra])[:n_heads]

        def build_alibi_bias(n_heads: int, T: int, causal: bool=True) -> jnp.ndarray:
            slopes = get_alibi_slopes(n_heads)
            idx = jnp.arange(T)
            rel = jnp.abs(idx[:, None] - idx[None, :]).astype(jnp.float32)
            bias = -slopes[:, None, None] * rel[None]
            if causal:
                future = idx[None, :] > idx[:, None]
                bias = jnp.where(future[None], -jnp.inf, bias)
            return bias
        B, T, C = x.shape
        H = 16
        D = C // H
        scale = D ** (-0.5)

        def proj_split(W):
            t = jnp.einsum('btc,dc->btd', x, W)
            return t.reshape(B, T, H, D).transpose(0, 2, 1, 3)
        q, k, v = (proj_split(Wq), proj_split(Wk), proj_split(Wv))
        scores = jnp.einsum('bhtd,bhsd->bhts', q, k) * scale
        bias = build_alibi_bias(H, T, causal=True)
        scores = scores + bias[None]
        attn = jax.nn.softmax(scores, axis=-1)
        out = jnp.einsum('bhts,bhsd->bhtd', attn, v)
        out = out.transpose(0, 2, 1, 3).reshape(B, T, C)
        return jnp.einsum('btc,dc->btd', out, Wo)

    def _L0_ffn_ref(src, ln1_w, ln1_b, ln2_w, ln2_b, attn_gate_w, q_w, q_b, k_w, k_b, v_w, v_b, o_w, o_b, rel_table, ff_gate_w, ff_w1, ff_b1, ff_w2, ff_b2):
        import jax, jax.numpy as jnp
        import numpy as np
        D = 128
        HD = 128
        EA = 8
        KA = 2
        EF = 16
        KF = 2
        FH = 64
        MAXP = 64
        B, S = (4, 128)
        EPS = 1e-05

        def _layer_norm(x, w, b):
            mu = x.mean(-1, keepdims=True)
            var = ((x - mu) ** 2).mean(-1, keepdims=True)
            return (x - mu) * jax.lax.rsqrt(var + EPS) * w + b

        def _topk_gates(logits, k):
            top_vals, top_idx = jax.lax.top_k(logits, k)
            g = jax.nn.softmax(top_vals, axis=-1)
            onehot = jax.nn.one_hot(top_idx, logits.shape[-1], dtype=logits.dtype)
            return jnp.einsum('...k,...ke->...e', g, onehot)

        def _moa(x, gate_w, q_w, q_b, k_w, k_b, v_w, v_b, o_w, o_b, rel_table):
            S_ = x.shape[1]
            gates = _topk_gates(x @ gate_w, KA)
            q = (jnp.einsum('bsd,edh->bseh', x, q_w) + q_b) * HD ** (-0.5)
            k = x @ k_w + k_b
            v = x @ v_w + v_b
            scores = jnp.einsum('bqeh,bkh->beqk', q, k)
            rel_s = jnp.einsum('bqeh,rh->beqr', q, rel_table)
            pos = jnp.arange(S_)
            rel_idx = jnp.clip(pos[None, :] - pos[:, None], -MAXP, MAXP) + MAXP
            scores = scores + jnp.take_along_axis(rel_s, rel_idx[None, None], axis=-1)
            p = jax.nn.softmax(scores, axis=-1)
            ctx = jnp.einsum('beqk,bkh->bqeh', p, v)
            out = jnp.einsum('bqeh,ehd,bqe->bqd', ctx, o_w, gates)
            return out + jnp.einsum('bqe,ed->bqd', gates, o_b)

        def _moe_ffn(x, gate_w, w1, b1, w2, b2):
            gates = _topk_gates(x @ gate_w, KF)
            h = jax.nn.relu(jnp.einsum('bsd,edh->bseh', x, w1) + b1)
            out = jnp.einsum('bseh,ehd,bse->bsd', h, w2, gates)
            return out + jnp.einsum('bse,ed->bsd', gates, b2)
        res = src
        xn = _layer_norm(src, ln1_w, ln1_b)
        x = res + _moa(xn, attn_gate_w, q_w, q_b, k_w, k_b, v_w, v_b, o_w, o_b, rel_table)
        res = x
        xn = _layer_norm(x, ln2_w, ln2_b)
        return res + _moe_ffn(xn, ff_gate_w, ff_w1, ff_b1, ff_w2, ff_b2)

    def _L1_attn_ref(x, W_attn, b_attn, W_proj, b_proj):
        import jax, jax.numpy as jnp
        import numpy as np
        B, T, C = (2, 256, 128)
        N_HEAD = 16
        HEAD_DIM = C // N_HEAD
        ATTN_MODE = 'local'
        LOCAL_ATTN_CTX = 32

        def build_mask(n, attn_mode, local_attn_ctx):
            i = jnp.arange(n)[:, None]
            j = jnp.arange(n)[None, :]
            causal = j <= i
            if attn_mode == 'all':
                return causal
            if attn_mode == 'local':
                return causal & (j >= i - local_attn_ctx)
            if attn_mode == 'strided':
                return causal & (j % local_attn_ctx == 0)
            raise ValueError(attn_mode)
        b, t, c = x.shape
        qkv = x @ W_attn + b_attn
        q, k, v = jnp.split(qkv, 3, axis=-1)

        def heads(a):
            return a.reshape(b, t, N_HEAD, HEAD_DIM).transpose(0, 2, 1, 3)
        q, k, v = (heads(q), heads(k), heads(v))
        scale = 1.0 / np.sqrt(HEAD_DIM)
        scores = jnp.einsum('bhtd,bhsd->bhts', q, k) * scale
        mask = build_mask(t, ATTN_MODE, LOCAL_ATTN_CTX)
        scores = jnp.where(mask[None, None], scores, -jnp.inf)
        attn = jax.nn.softmax(scores, axis=-1)
        out = jnp.einsum('bhts,bhsd->bhtd', attn, v)
        out = out.transpose(0, 2, 1, 3).reshape(b, t, c)
        return out @ W_proj + b_proj

    def _L1_ffn_ref(x, Ws, bs, Wg, Wu, Wd):
        import jax, jax.numpy as jnp
        import numpy as np
        D, F, E, K = (128, 344, 8, 2)
        b, n, d = x.shape
        xt = x.reshape(-1, d)
        logits = xt @ Ws + bs
        topk_w, topk_idx = jax.lax.top_k(logits, K)
        topk_w = jax.nn.softmax(topk_w, axis=-1)
        combine = jnp.sum(jax.nn.one_hot(topk_idx, E, dtype=xt.dtype) * topk_w[..., None], axis=1)
        g = jnp.einsum('td,edf->tef', xt, Wg)
        u = jnp.einsum('td,edf->tef', xt, Wu)
        h = jax.nn.silu(g) * u
        y = jnp.einsum('tef,efd->ted', h, Wd)
        out = jnp.einsum('ted,te->td', y, combine)
        return out.reshape(b, n, d)
    x = L0_attn_x
    x = x + _L0_attn_ref(_layernorm(x, axis=-1), L0_attn_Wq, L0_attn_Wk, L0_attn_Wv, L0_attn_Wo)
    x = x + _L0_ffn_ref(_layernorm(x, axis=-1), L0_ffn_ln1_w, L0_ffn_ln1_b, L0_ffn_ln2_w, L0_ffn_ln2_b, L0_ffn_attn_gate_w, L0_ffn_q_w, L0_ffn_q_b, L0_ffn_k_w, L0_ffn_k_b, L0_ffn_v_w, L0_ffn_v_b, L0_ffn_o_w, L0_ffn_o_b, L0_ffn_rel_table, L0_ffn_ff_gate_w, L0_ffn_ff_w1, L0_ffn_ff_b1, L0_ffn_ff_w2, L0_ffn_ff_b2)
    x = x + _L1_attn_ref(_layernorm(x, axis=-1), L1_attn_W_attn, L1_attn_b_attn, L1_attn_W_proj, L1_attn_b_proj)
    x = x + _L1_ffn_ref(_layernorm(x, axis=-1), L1_ffn_Ws, L1_ffn_bs, L1_ffn_Wg, L1_ffn_Wu, L1_ffn_Wd)
    return x

_drawn_inputs = setup_inputs


def setup_inputs(seed=0):
    import zlib

    import numpy as np

    out = dict(_drawn_inputs(seed))
    spreads = {'L0_ffn_ln1_w': (1.0, 0.6),
     'L0_ffn_ln1_b': (0.0, 0.699),
     'L0_ffn_ln2_w': (1.0, 0.6),
     'L0_ffn_ln2_b': (0.0, 0.562),
     'L0_ffn_q_b': (0.0, 0.8),
     'L0_ffn_k_b': (0.0, 0.8),
     'L0_ffn_v_b': (0.0, 0.8),
     'L0_ffn_o_b': (0.0, 0.1),
     'L0_ffn_ff_b1': (0.0, 0.8),
     'L0_ffn_ff_b2': (0.0, 0.1),
     'L1_attn_b_attn': (0.0, 0.745),
     'L1_attn_b_proj': (0.0, 0.1),
     'L1_ffn_bs': (0.0, 0.8)}
    factors = {'L0_attn_Wq': 8.0,
     'L0_attn_Wk': 8.0,
     'L0_attn_Wv': 3.473,
     'L0_attn_Wo': 3.529,
     'L0_ffn_q_w': 8.0,
     'L0_ffn_k_w': 8.0,
     'L0_ffn_v_w': 8.0,
     'L0_ffn_o_w': 6.219,
     'L0_ffn_rel_table': 8.0,
     'L0_ffn_ff_w1': 7.009,
     'L0_ffn_ff_w2': 5.456,
     'L1_attn_W_attn': 8.0,
     'L1_attn_W_proj': 4.808,
     'L1_ffn_Ws': 8.0,
     'L1_ffn_Wg': 8.0,
     'L1_ffn_Wu': 8.0,
     'L1_ffn_Wd': 8.0}
    for name, (base, spread) in spreads.items():
        noise = np.random.default_rng([zlib.crc32(name.encode()), seed]).standard_normal(out[name].shape)
        drawn = base * np.exp(spread * noise) if base else spread * noise
        out[name] = jnp.asarray(drawn.astype(out[name].dtype))
    for name, factor in factors.items():
        out[name] = (out[name] * factor).astype(out[name].dtype)
    return out
```

```python
import math
from contextlib import ExitStack

import concourse.bass as bass
from concourse import mybir
import numpy as np

F32 = mybir.dt.float32
F32R = mybir.dt.float32r
BF16 = mybir.dt.bfloat16
U8 = mybir.dt.uint8
ALU = mybir.AluOpType
ACT = mybir.ActivationFunctionType
AX = mybir.AxisListType

P = 128
BATCH, SEQ, DIM = 16, 256, 128
HALVES = SEQ // P
TILES = BATCH * HALVES
EPS = 1e-5
MASKED = -1e30
LOWEST = -3e38

HEADS, HEAD_DIM = 16, 8
GROUP = 4
GROUPS = HEADS // GROUP
STRIP = P // GROUP
ROW_SLOPE_HI, ROW_MAX_HI, ROW_SLOPE_LO, ROW_MAX_LO = 0, 1, 2, 3
ROW_A, ROW_B, ROW_C = 4, 12, 20
LOCAL_WINDOW = 32


class Attention:

    def __init__(self, name, alibi):
        self.name = name
        self.alibi = alibi
        self.late_keys = 0 if alibi else P - LOCAL_WINDOW
        self.early_queries = SEQ if alibi else P + LOCAL_WINDOW


def cleared_at_exit(nc, ctx, semaphores):
    def clear():
        with nc.Block() as block:
            @block.sync
            def _(sp):
                for semaphore in semaphores:
                    sp.sem_clear(semaphore)

    ctx.callback(clear)



def attention(nc, cfg, x_sb, weights, consts, loaded, loads):
    wq_stack, wk_stack, wv, wo, const_rows, bias_rows = weights
    ident, ident_bf, mask_rows, mask_cols, row_masks, ramp, half_pow = consts
    n0 = cfg.name
    ctx = ExitStack()
    with ctx:
        def sb(name, shape, dt=F32):
            return ctx.enter_context(nc.sbuf_tensor(f"{n0}_{name}", shape, dt))

        def pb(name, shape):
            return ctx.enter_context(nc.psum_tensor(f"{n0}_{name}", shape, F32))

        semaphores = []

        def sem(name):
            semaphores.append(ctx.enter_context(nc.semaphore(f"{n0}_{name}")))
            return semaphores[-1]

        w_hi = {k: sb(f"w{k}_hi", [P, HEADS * STRIP], F32R) for k in "qk"}
        w_lo = {k: sb(f"w{k}_lo", [P, HEADS * STRIP], F32R) for k in "qk"}
        c_rows = {k: sb(f"c{k}", [P, HEADS * STRIP], F32R) for k in "qk"}
        c_tmp = sb("c_tmp", [P, 2 * HEADS * STRIP], F32R)
        stats = sb("stats", [P, HALVES, 6])
        moments = sb("moments", [P, HALVES, 2])
        var_eps = sb("var_eps", [P, HALVES])
        rstd = sb("rstd", [P, HALVES])
        xn = sb("xn", [P, HALVES, DIM])
        xt = sb("xt", [P, SEQ])
        xt_hi = sb("xt_hi", [P, SEQ], F32R)
        xt_lo = sb("xt_lo", [P, SEQ], F32R)
        qk_hi = sb("qk_hi", [P, 2 * SEQ], F32R)
        q_max_hi = sb("q_max_hi", [P, SEQ], F32R)
        k_stack = [sb(f"k_stack{i}", [P, SEQ], F32R) for i in range(2)]
        q_stack = [sb(f"q_stack{i}", [P, SEQ], F32R) for i in range(2)]
        q_full = sb("q_full", [P, SEQ + P], F32R)
        row_max = sb("row_max", [P, HALVES, GROUP])
        neg_max = sb("neg_max", [P, HALVES, P])
        if cfg.alibi:
            pieces, width = 1, SEQ + P
        else:
            pieces, width = 2, P + LOCAL_WINDOW
        probs = sb("probs", [P, GROUP, pieces * width])
        v_aug = sb("v_aug", [P, HALVES, HEADS, STRIP])
        o_t = [sb(f"o_t{i}", [P, SEQ]) for i in range(2)]
        inv_sum = sb("inv_sum", [P, HALVES * GROUP])
        attn = sb("attn", [P, HALVES, DIM])
        attn_t = sb("attn_t", [P, SEQ])

        qk_ps = [pb(f"qk_ps{i}", [P, 2 * SEQ]) for i in range(2)]
        score_ps = pb("score_ps", [P, GROUP, 2 * SEQ])
        o_ps = pb("o_ps", [P, 2 * SEQ])
        misc = pb("misc", [P, 2 * SEQ])

        zeroed = sem("zeroed")
        waited = sem("waited")
        halved = sem("halved")
        split = sem("split")
        stats_done = sem("stats_done")
        var_ready = sem("var_ready")
        eps_added = sem("eps_added")
        rstd_ready = sem("rstd_ready")
        xn_ready = sem("xn_ready")
        xn_turned = sem("xn_turned")
        xt_hi_ready = sem("xt_hi_ready")
        xt_ready = sem("xt_ready")
        v_done = sem("v_done")
        v_ready = sem("v_ready")
        qk_done = sem("qk_done")
        qk_hi_ready = sem("qk_hi_ready")
        stacks_ready = sem("stacks_ready")
        scores_done = sem("scores_done")
        max_part = sem("max_part")
        max_ready = sem("max_ready")
        max_added = sem("max_added")
        q_hi_ready = sem("q_hi_ready")
        q_full_ready = sem("q_full_ready")
        scores_t_done = sem("scores_t_done")
        probs_ready = sem("probs_ready")
        pv_done = sem("pv_done")
        o_t_ready = sem("o_t_ready")
        out_turned = sem("out_turned")
        inv_ready = sem("inv_ready")
        attn_ready = sem("attn_ready")
        attn_turned = sem("attn_turned")
        attn_t_ready = sem("attn_t_ready")
        projected = sem("projected")
        x_added = sem("x_added")
        x_biased = sem("x_biased")

        def over_batches(eng, body):
            body(0)
            with eng.Fori(1, BATCH - 1) as b:
                body(b)
            body(BATCH - 1)

        def is_first(b):
            return isinstance(b, int) and b == 0

        def is_last(b):
            return isinstance(b, int) and b == BATCH - 1

        def x_half(b, h):
            return x_sb[:, bass.ds((b * HALVES + h) * DIM, DIM)]

        cleared_at_exit(nc, ctx, semaphores)
        block = ctx.enter_context(nc.Block())

        @block.gpsimd
        def _(pool):
            for k in "qk":
                pool.memset(c_rows[k][:, :].bitcast(F32), 0.0).then_inc(zeroed, 1)
            pool.memset(q_full[:, SEQ:].bitcast(F32), 0.0).then_inc(zeroed, 1)
            pool.memset(neg_max[:, :, :], 0.0).then_inc(zeroed, 1)
            pool.memset(v_aug[:, :, :, :], 0.0).then_inc(zeroed, 1)
            pool.wait_ge(zeroed, 5)
            pool.memset(v_aug[:, :, :, HEAD_DIM:HEAD_DIM + 1], 1.0).then_inc(zeroed, 1)

            def inverse_deviation(b):
                pool.wait_ge(var_ready, b + 1)
                pool.sem_inc(waited, 1)
                pool.tensor_scalar(var_eps[:, :], moments[:, :, 1], EPS, None, ALU.add).then_inc(eps_added, 1)
                pool.wait_ge(eps_added, b + 1)
                pool.tensor_tensor(rstd[:, :], var_eps[:, :], half_pow[:, :], ALU.pow).then_inc(rstd_ready, 1)

            inverse_deviation(0)
            with pool.Fori(1, BATCH) as b:
                inverse_deviation(b)

        @block.scalar
        def _(act):
            act.wait_ge(loaded, loads)
            scale = HEAD_DIM ** -0.5
            act.activation(w_hi["q"][:, :], wq_stack[:, :], ACT.Copy, scale=scale).then_inc(halved, 1)
            act.activation(w_hi["k"][:, :], wk_stack[:, :], ACT.Copy).then_inc(halved, 1)
            act.wait_ge(zeroed, 6)
            row_scale = 1.0 if cfg.alibi else scale
            for j, k in enumerate("qk"):
                cols = slice(j * 512, j * 512 + 512)
                s = row_scale if k == "q" else 1.0
                act.activation(c_rows[k][0:1, :], const_rows[0:1, cols], ACT.Copy, scale=s).then_inc(halved, 1)
                act.activation(c_tmp[32:33, cols], const_rows[32:33, cols], ACT.Copy, scale=s).then_inc(halved, 1)
                act.activation(c_rows[k][64:65, :], const_rows[64:65, cols], ACT.Copy).then_inc(halved, 1)

            def turned_x(b):
                act.wait_ge(xn_turned, b + 1)
                act.activation(xt[:, :], misc[:, 0:SEQ], ACT.Copy)
                act.activation(xt_hi[:, :], misc[:, 0:SEQ], ACT.Copy).then_inc(xt_hi_ready, 1)

            def high_half(u, parity):
                act.wait_ge(qk_done, u + 1)
                if not (isinstance(u, int) and u == 0):
                    act.wait_ge(stacks_ready, u)
                act.activation(qk_hi[:, :], qk_ps[parity][:, :], ACT.Copy).then_inc(qk_hi_ready, 1)

            def high_half_with_max(u, parity):
                act.wait_ge(max_added, u + 1)
                act.activation(q_max_hi[:, :], qk_ps[parity][:, 0:SEQ], ACT.Copy).then_inc(q_hi_ready, 1)

            turned_x(0)
            high_half(0, 0)
            high_half(1, 1)
            high_half_with_max(0, 0)

            def unit(b, g):
                u = b * GROUPS + g
                for pair in range(GROUP // 2):
                    act.wait_ge(scores_t_done, u * GROUP + 2 * pair + 2)
                    banks = score_ps[:, 2 * pair:2 * pair + 2, :]
                    if pieces == 1:
                        src, dst = banks[:, :, 0:width], probs[:, 2 * pair:2 * pair + 2, :]
                    else:
                        src = banks.rearrange("p h (k q) -> p h k q", k=2)[:, :, :, 0:width]
                        dst = probs[:, 2 * pair:2 * pair + 2, :].rearrange("p h (k q) -> p h k q", k=2)
                    act.activation(dst, src, ACT.Exp).then_inc(probs_ready, 1)
                if not (is_last(b) and g >= 2):
                    high_half(u + 2, g % 2)
                if g == 0 and not is_first(b):
                    attention_turned(b - 1)
                if g == 1 and not is_last(b):
                    turned_x(b + 1)
                act.wait_ge(pv_done, u + 1)
                act.activation(o_t[g % 2][:, :], o_ps[:, 0:SEQ], ACT.Copy).then_inc(o_t_ready, 1)
                if not (is_last(b) and g == 3):
                    high_half_with_max(u + 1, (g + 1) % 2)

            def attention_turned(b):
                act.wait_ge(attn_turned, b + 1)
                act.activation(attn_t[:, :], misc[:, 0:SEQ], ACT.Copy).then_inc(attn_t_ready, 1)

            def batch(b):
                for g in range(GROUPS):
                    unit(b, g)

            over_batches(act, batch)
            attention_turned(BATCH - 1)

        @block.vector
        def _(dve):
            dve.wait_ge(loaded, loads)
            scale = HEAD_DIM ** -0.5
            dve.wait_ge(halved, 8)
            for k, src, s in (("q", wq_stack, scale), ("k", wk_stack, 1.0)):
                dve.scalar_tensor_tensor(out=w_lo[k][:, :], in0=src[:, :], scalar=s,
                                         in1=w_hi[k][:, :].bitcast(F32), op0=ALU.mult,
                                         op1=ALU.subtract).then_inc(split, 1)
            row_scale = 1.0 if cfg.alibi else scale
            for j, k in enumerate("qk"):
                cols = slice(j * 512, j * 512 + 512)
                dve.scalar_tensor_tensor(out=c_rows[k][32:33, :], in0=const_rows[32:33, cols],
                                         scalar=row_scale if k == "q" else 1.0,
                                         in1=c_tmp[32:33, cols].bitcast(F32), op0=ALU.mult,
                                         op1=ALU.subtract).then_inc(split, 1)

            def moments_of(b):
                for h in range(HALVES):
                    dve.bn_stats(stats[:, h, :], x_half(b, h)).then_inc(stats_done, 1)
                dve.wait_ge(stats_done, b * HALVES + HALVES)
                dve.sem_inc(waited, 1)
                for h in range(HALVES):
                    ins = dve.bn_aggr(moments[:, h, :], stats[:, h, :])
                ins.then_inc(var_ready, 1)

            def normalise(b):
                dve.wait_ge(rstd_ready, b + 1)
                dve.wait_ge(var_ready, b + 1)
                for h in range(HALVES):
                    ins = dve.tensor_scalar(xn[:, h, :], x_half(b, h), moments[:, h, 0:1], rstd[:, h:h + 1],
                                            ALU.subtract, ALU.mult)
                ins.then_inc(xn_ready, 1)

            def turned_x_low(b):
                dve.wait_ge(xt_hi_ready, b + 1)
                dve.tensor_tensor(xt_lo[:, :], misc[:, 0:SEQ], xt_hi[:, :].bitcast(F32),
                                  ALU.subtract).then_inc(xt_ready, 1)

            def stacks(u, parity):
                dve.wait_ge(qk_hi_ready, u + 1)
                ps = qk_ps[parity]
                for dst, at, mask in ((q_stack[parity], 0, 0), (k_stack[parity], SEQ, 1)):
                    ins = dve.scalar_tensor_tensor(
                        out=dst[:, :], in0=qk_hi[:, at:at + SEQ].bitcast(F32), scalar=row_masks[:, mask:mask + 1],
                        in1=ps[:, at:at + SEQ], op0=ALU.mult, op1=ALU.add)
                ins.then_inc(stacks_ready, 1)

            def maxima(u, parity):
                for i in range(GROUP):
                    dve.wait_ge(scores_done, u * GROUP + i + 1)
                    dve.sem_inc(waited, 1)
                    for h in range(HALVES):
                        lo = 0 if h == 0 else cfg.late_keys
                        hi = P if h == 0 else SEQ
                        ins = dve.tensor_tensor_reduce(
                            score_ps[:, i, h * SEQ + lo:h * SEQ + hi], score_ps[:, i, h * SEQ + lo:h * SEQ + hi],
                            mask_rows[:, h, lo:hi], 1.0, LOWEST, ALU.add, ALU.max,
                            row_max[:, h, i:i + 1])
                    ins.then_inc(max_part, 1)
                dve.wait_ge(max_part, u * GROUP + GROUP)
                cols = neg_max[:, :, :].rearrange("q h (i r two) -> q (h i) r two", r=STRIP // 2, two=2)
                src = row_max[:, :, :].rearrange("q h i -> q (h i)").unsqueeze(2).broadcast_to([P, HALVES * GROUP, 2])
                dve.tensor_scalar(cols[:, :, 0:2, 1], src, -1.0, None, ALU.mult).then_inc(max_ready, 1)

            def queries_with_max(u, parity):
                dve.wait_ge(q_hi_ready, u + 1)
                dve.scalar_tensor_tensor(
                    out=q_full[:, 0:SEQ], in0=q_max_hi[:, :].bitcast(F32), scalar=row_masks[:, 0:1],
                    in1=qk_ps[parity][:, 0:SEQ], op0=ALU.mult, op1=ALU.add).then_inc(q_full_ready, 1)

            def output_rows(u, g):
                dve.wait_ge(out_turned, u + 1)
                o = misc[:, 0:SEQ].rearrange("q (i r) -> q i r", r=STRIP)
                dve.reciprocal(inv_sum[:, :], o[:, :, HEAD_DIM]).then_inc(inv_ready, 1)
                dve.wait_ge(inv_ready, u + 1)
                for h in range(HALVES):
                    ins = dve.tensor_tensor(
                        attn[:, h, g * GROUP * HEAD_DIM:(g + 1) * GROUP * HEAD_DIM].rearrange("q (i d) -> q i d", d=HEAD_DIM),
                        o[:, h * GROUP:(h + 1) * GROUP, 0:HEAD_DIM],
                        inv_sum[:, h * GROUP:(h + 1) * GROUP].unsqueeze(2).broadcast_to([P, GROUP, HEAD_DIM]), ALU.mult)
                    if h == HALVES - 1:
                        ins.then_inc(attn_ready, 1)

            def add_to_x(b):
                dve.wait_ge(projected, b + 1)
                dst = x_sb[:, bass.ds(b * SEQ, SEQ)]
                dve.tensor_tensor(dst, dst, misc[:, 0:SEQ], ALU.add).then_inc(x_added, 1)
                if bias_rows is not None:
                    dve.wait_ge(x_added, b + 1)
                    dve.tensor_tensor(dst.rearrange("p (h c) -> p h c", h=HALVES), dst.rearrange("p (h c) -> p h c", h=HALVES),
                                      bias_rows[:, DIM:2 * DIM].unsqueeze(1).broadcast_to([P, HALVES, DIM]),
                                      ALU.add).then_inc(x_biased, 1)

            dve.wait_ge(zeroed, 6)
            moments_of(0)
            normalise(0)
            turned_x_low(0)
            stacks(0, 0)
            stacks(1, 1)
            maxima(0, 0)
            queries_with_max(0, 0)

            def unit(b, g):
                u = b * GROUPS + g
                if g == 0:
                    dve.wait_ge(v_done, b + 1)
                    src = misc[:, 0:SEQ].rearrange("p (n d) -> p n d", d=HEAD_DIM)
                    dst = v_aug[:, :, :, :].rearrange("p k h r -> p (k h) r")[:, :, 0:HEAD_DIM]
                    if bias_rows is None:
                        dve.tensor_copy(dst, src).then_inc(v_ready, 1)
                    else:
                        for h in range(HALVES):
                            ins = dve.tensor_tensor(dst[:, h * HEADS:(h + 1) * HEADS, :], src[:, h * HEADS:(h + 1) * HEADS, :],
                                                    bias_rows[:, 0:DIM].rearrange("p (n d) -> p n d", d=HEAD_DIM), ALU.add)
                        ins.then_inc(v_ready, 1)
                if g == 1 and not is_last(b):
                    normalise(b + 1)
                if not (is_first(b) and g == 0):
                    output_rows(u - 1, (g - 1) % GROUPS)
                if not (is_last(b) and g >= 2):
                    stacks(u + 2, g % 2)
                if not (is_last(b) and g == 3):
                    maxima(u + 1, (g + 1) % 2)
                if g == 0 and not is_last(b):
                    moments_of(b + 1)
                if g == 1 and not is_last(b):
                    turned_x_low(b + 1)
                if g == 2 and not is_first(b):
                    add_to_x(b - 1)
                if not (is_last(b) and g == 3):
                    queries_with_max(u + 1, (g + 1) % 2)

            def batch(b):
                for g in range(GROUPS):
                    unit(b, g)

            over_batches(dve, batch)
            output_rows(BATCH * GROUPS - 1, GROUPS - 1)
            add_to_x(BATCH - 1)

        @block.tensor
        def _(pe):
            pe.wait_ge(loaded, loads)

            def turn_x(b):
                pe.wait_ge(xn_ready, b + 1)
                for h in range(HALVES):
                    mm = pe.transpose(misc[:, h * P:(h + 1) * P], xn[:, h, :], ident[:, :])
                mm.then_inc(xn_turned, 1)

            def values(b):
                for h in range(HALVES):
                    mm = pe.matmul(misc[:, h * DIM:(h + 1) * DIM], xt[:, h * P:(h + 1) * P], wv[:, :],
                                   start=True, stop=True)
                mm.then_inc(v_done, 1)

            def queries_keys(g, parity):
                for k, at, ramp_or_one in (("q", 0, 0), ("k", SEQ, 0)):
                    out = qk_ps[parity][:, at:at + SEQ]
                    cols = slice(g * P, (g + 1) * P)
                    pe.matmul(out, c_rows[k][:, cols], ramp[:, :], start=(k == "q"), stop=False, skip_group_check=True)
                    pe.matmul(out, w_hi[k][:, cols], xt_lo[:, :], start=False, stop=False, skip_group_check=True)
                    pe.matmul(out, w_lo[k][:, cols], xt_hi[:, :], start=False, stop=False, skip_group_check=True)
                    mm = pe.matmul(out, w_hi[k][:, cols], xt_hi[:, :], start=False, stop=True, skip_group_check=True)
                mm.then_inc(qk_done, 1)

            def scores(u, parity):
                pe.wait_ge(stacks_ready, u + 1)
                if not (isinstance(u, int) and u == 0):
                    pe.wait_ge(probs_ready, u * (GROUP // 2))
                for h in range(HALVES):
                    for i in range(GROUP):
                        rows = slice(i * STRIP, (i + 1) * STRIP)
                        mm = pe.matmul(score_ps[:, i, h * SEQ:(h + 1) * SEQ], q_stack[parity][rows, h * P:(h + 1) * P],
                                       k_stack[parity][rows, :], start=True, stop=True)
                        if h == HALVES - 1:
                            mm.then_inc(scores_done, 1)

            def add_max(u, parity):
                pe.wait_ge(max_ready, u + 1)
                for h in range(HALVES):
                    mm = pe.matmul(qk_ps[parity][:, h * P:(h + 1) * P], neg_max[:, h, :], ident[:, :],
                                   start=False, stop=True, skip_group_check=True)
                mm.then_inc(max_added, 1)

            def scores_turned(u, parity):
                pe.wait_ge(q_full_ready, u + 1)
                for i in range(GROUP):
                    for h in range(HALVES):
                        n = (P if cfg.alibi else P + LOCAL_WINDOW) if h == 0 else P
                        pe.matmul(score_ps[:, i, h * SEQ:h * SEQ + n], ident_bf[:, :], mask_cols[:, 0:n],
                                  start=(h == 0), stop=False, skip_group_check=True)
                for h in range(HALVES):
                    for i in range(GROUP):
                        rows = slice(i * STRIP, (i + 1) * STRIP)
                        mm = pe.matmul(score_ps[:, i, h * SEQ:(h + 1) * SEQ], k_stack[parity][rows, h * P:(h + 1) * P],
                                       q_full[rows, h * P:h * P + SEQ], start=False, stop=True, skip_group_check=True)
                        if h == HALVES - 1:
                            mm.then_inc(scores_t_done, 1)

            def probs_values(u, g):
                pe.wait_ge(probs_ready, (u + 1) * (GROUP // 2))
                if not (isinstance(u, int) and u == 0):
                    pe.wait_ge(o_t_ready, u)
                for h in range(HALVES):
                    n = cfg.early_queries if h == 0 else P
                    at = 0 if h == 0 else (SEQ if cfg.alibi else width)
                    for i in range(GROUP):
                        mm = pe.matmul(o_ps[i * STRIP:(i + 1) * STRIP, h * P:h * P + n],
                                       v_aug[:, h, g * GROUP + i, :], probs[:, i, at:at + n],
                                       start=(h == 0), stop=(h == HALVES - 1), skip_group_check=True)
                mm.then_inc(pv_done, 1)

            def turn_output(u, parity):
                pe.wait_ge(o_t_ready, u + 1)
                for h in range(HALVES):
                    mm = pe.transpose(misc[:, h * P:(h + 1) * P], o_t[parity][:, h * P:(h + 1) * P], ident[:, :])
                mm.then_inc(out_turned, 1)

            def turn_attention(b):
                pe.wait_ge(attn_ready, (b + 1) * GROUPS)
                for h in range(HALVES):
                    mm = pe.transpose(misc[:, h * P:(h + 1) * P], attn[:, h, :], ident[:, :])
                mm.then_inc(attn_turned, 1)

            def project(b):
                pe.wait_ge(attn_t_ready, b + 1)
                for h in range(HALVES):
                    mm = pe.matmul(misc[:, h * DIM:(h + 1) * DIM], attn_t[:, h * P:(h + 1) * P], wo[:, :],
                                   start=True, stop=True)
                mm.then_inc(projected, 1)

            pe.wait_ge(split, 4)
            pe.wait_ge(halved, 8)
            turn_x(0)
            pe.wait_ge(xt_ready, 1)
            queries_keys(0, 0)
            queries_keys(1, 1)
            scores(0, 0)
            add_max(0, 0)

            def unit(b, g):
                u = b * GROUPS + g
                if g == 0:
                    if is_first(b):
                        pe.wait_ge(xt_ready, 1)
                    else:
                        pe.wait_ge(attn_ready, u - 1)
                    values(b)
                scores_turned(u, g % 2)
                if not (is_first(b) and g == 0):
                    if g == 0:
                        pe.wait_ge(v_ready, b + 1)
                    elif g == 1:
                        if is_first(b):
                            pe.wait_ge(v_ready, 1)
                        else:
                            pe.wait_ge(attn_t_ready, b)
                    elif g == 2:
                        if is_last(b):
                            pe.wait_ge(attn_ready, u - 1)
                        else:
                            pe.wait_ge(xt_ready, b + 2)
                    else:
                        if is_first(b):
                            pe.wait_ge(attn_ready, u - 1)
                        else:
                            pe.wait_ge(x_added, b)
                    turn_output(u - 1, (g - 1) % 2)
                if not (is_last(b) and g >= 2):
                    if g == 2:
                        pe.wait_ge(xt_ready, b + 2)
                    queries_keys((g + 2) % GROUPS, g % 2)
                if not (is_last(b) and g == 3):
                    scores(u + 1, (g + 1) % 2)
                if g == 0 and not is_first(b):
                    turn_attention(b - 1)
                if g == 1 and not is_last(b):
                    pe.wait_ge(attn_ready, u)
                    turn_x(b + 1)
                if g == 2 and not is_first(b):
                    pe.wait_ge(attn_ready, u)
                    project(b - 1)
                if g == 0:
                    pe.wait_ge(v_ready, b + 1)
                probs_values(u, g)
                if not (is_last(b) and g == 3):
                    add_max(u + 1, (g + 1) % 2)

            def batch(b):
                for g in range(GROUPS):
                    unit(b, g)

            over_batches(pe, batch)
            pe.wait_ge(attn_ready, BATCH * GROUPS - 1)
            turn_output(BATCH * GROUPS - 1, 1)
            turn_attention(BATCH - 1)
            project(BATCH - 1)



def route_logits(dve, t, count, n_tiles, logits_ps, bias, done):
    if bias is None:
        dve.tensor_copy(t.logits[:, :, :], logits_ps).then_inc(t.logits_ready, 1)
    else:
        dve.tensor_tensor(t.logits[:, :, :], logits_ps, bias, ALU.add).then_inc(t.logits_ready, 1)
    dve.wait_ge(t.logits_ready, count + 1)
    dve.sem_inc(t.waited, 1)
    for n in range(n_tiles):
        ins = dve.max(t.top[:, n, :], t.logits[:, n, :])
    ins.then_inc(t.top_ready, 1)
    dve.wait_ge(t.top_ready, count + 1)
    dve.tensor_tensor(t.gap[:, :], t.top[:, :, 1], t.top[:, :, 0], ALU.subtract).then_inc(t.gap_ready, 1)
    for n in range(n_tiles):
        ins = dve.max_index(t.index[:, n, :], t.top[:, n, :], t.logits[:, n, :])
    ins.then_inc(t.index_ready, 1)
    dve.wait_ge(t.index_ready, count + 1)
    dve.tensor_copy(t.chosen[:, :, :], t.index[:, :, 0:2]).then_inc(t.chosen_ready, 1)


def route_gates(dve, t, count, n_tiles, gates):
    dve.wait_ge(t.gap_exp_ready, count + 1)
    dve.tensor_scalar(t.total[:, :], t.gap_exp[:, :], 1.0, None, ALU.add).then_inc(t.total_ready, 1)
    dve.wait_ge(t.total_ready, count + 1)
    dve.reciprocal(t.share[:, :, 0], t.total[:, :]).then_inc(t.first_ready, 1)
    dve.wait_ge(t.first_ready, count + 1)
    dve.tensor_tensor(t.share[:, :, 1], t.gap_exp[:, :], t.share[:, :, 0], ALU.mult).then_inc(t.share_ready, 1)
    dve.wait_ge(t.share_ready, count + 1)
    dve.wait_ge(t.chosen_ready, count + 1)
    for n in range(n_tiles):
        for k in range(2):
            ins = dve.tensor_scalar(t.placed[:, n, k, :], t.experts[:, :], t.chosen[:, n, k:k + 1],
                                    t.share[:, n, k:k + 1], ALU.is_equal, ALU.mult)
    ins.then_inc(t.placed_ready, 1)
    dve.wait_ge(t.placed_ready, count + 1)
    first, second = t.placed[:, :, 0, :], t.placed[:, :, 1, :]
    return dve.tensor_tensor(gates, first, second, ALU.add)


class Router:

    def __init__(self, sb, sem, n_tiles, n_experts, experts):
        self.experts = experts
        self.logits = sb("logits", [P, n_tiles, n_experts])
        self.top = sb("top", [P, n_tiles, 8])
        self.index = sb("index", [P, n_tiles, 8], mybir.dt.uint32)
        self.chosen = sb("chosen", [P, n_tiles, 2])
        self.gap = sb("gap", [P, n_tiles])
        self.gap_exp = sb("gap_exp", [P, n_tiles])
        self.total = sb("total", [P, n_tiles])
        self.share = sb("share", [P, n_tiles, 2])
        self.placed = sb("placed", [P, n_tiles, 2, n_experts])
        self.waited = sem("waited")
        self.logits_ready = sem("logits_ready")
        self.top_ready = sem("top_ready")
        self.gap_ready = sem("gap_ready")
        self.index_ready = sem("index_ready")
        self.chosen_ready = sem("chosen_ready")
        self.gap_exp_ready = sem("gap_exp_ready")
        self.total_ready = sem("total_ready")
        self.first_ready = sem("first_ready")
        self.share_ready = sem("share_ready")
        self.placed_ready = sem("placed_ready")


HD = 128
EA = 8
MAXP = 64
QUAD = 4
STEPS = (EA // QUAD) * HALVES
SLAB = P * (SEQ + 1)


def mixture_of_heads(nc, x_sb, y_sb, w, consts, scratch, loaded, loads):
    ident, half_pow, experts, far_mask = consts
    ctx = ExitStack()
    with ctx:
        def sb(name, shape, dt=F32):
            return ctx.enter_context(nc.sbuf_tensor(f"moa_{name}", shape, dt))

        def pb(name, shape):
            return ctx.enter_context(nc.psum_tensor(f"moa_{name}", shape, F32))

        semaphores = []

        def sem(name):
            semaphores.append(ctx.enter_context(nc.semaphore(f"moa_{name}")))
            return semaphores[-1]

        qw = [sb("qw_hi", [P, EA * HD], F32R), sb("qw_lo", [P, EA * HD], F32R)]
        kw = [sb("kw_hi", [P, HD], F32R), sb("kw_lo", [P, HD], F32R)]
        rel = [sb("rel_hi", [P, 2 * P], F32R), sb("rel_lo", [P, 2 * P], F32R)]
        rel_near = sb("rel_near", [P, 2 * P])
        k_bias = sb("k_bias", [P, 2])
        stats = sb("stats", [P, HALVES, 6])
        stats2 = sb("stats2", [P, HALVES, 6])
        moments = sb("moments", [P, HALVES, 2])
        moments2 = sb("moments2", [P, HALVES, 2])
        var_eps = sb("var_eps", [P, HALVES])
        var_eps2 = sb("var_eps2", [P, HALVES])
        rstd = sb("rstd", [P, HALVES])
        rstd2 = sb("rstd2", [P, HALVES])
        tn = sb("tn", [P, HALVES, DIM])
        xt = sb("xt", [P, SEQ])
        xt_hi = sb("xt_hi", [P, SEQ], F32R)
        xt_lo = sb("xt_lo", [P, SEQ], F32R)
        router = Router(lambda n, s, d=F32: sb("r_" + n, s, d), lambda n: sem("r_" + n), HALVES, EA, experts)
        gates = sb("gates", [P, BATCH, HALVES, EA])
        gates_now = sb("gates_now", [P, HALVES, EA])
        gates_t = sb("gates_t", [EA, SEQ])
        q_hi = [sb(f"q_hi{i}", [P, QUAD, SEQ], F32R) for i in range(2)]
        q_lo = [sb(f"q_lo{i}", [P, QUAD, SEQ], F32R) for i in range(2)]
        keys = sb("keys", [P, HALVES, SEQ])
        keys_hi = sb("keys_hi", [P, HALVES, SEQ], F32R)
        keys_lo = sb("keys_lo", [P, HALVES, SEQ], F32R)
        v_next = sb("v_next", [P, HALVES, HD])
        v = sb("v", [P, HALVES, HD])
        band = [sb(f"band{i}", [P, QUAD, P]) for i in range(2)]
        band_in = [sb(f"band_in{i}", [P, QUAD, SEQ]) for i in range(STEPS)]
        row_max = sb("row_max", [P, QUAD])
        neg_max = sb("neg_max", [P, QUAD])
        sums = sb("sums", [P, QUAD])
        inv = sb("inv", [P, QUAD])
        factor = [sb(f"factor{i}", [P, QUAD]) for i in range(2)]
        probs = [sb(f"probs{i}", [P, QUAD, SEQ]) for i in range(2)]
        weighted = [sb(f"weighted{i}", [P, QUAD, SEQ]) for i in range(2)]
        probs_t = sb("probs_t", [P, HALVES, QUAD * P])
        heads_t = sb("heads_t", [P, QUAD * P])

        rel_ps = pb("rel_ps", [P, 2, 2 * P])
        score_ps = pb("score_ps", [P, QUAD, SEQ])
        turn_ps = pb("turn_ps", [P, HALVES, QUAD * P])
        heads_ps = pb("heads_ps", [P, QUAD * P])
        out_ps = pb("out_ps", [P, 4 * P])
        misc = pb("misc", [P, 4 * P])

        names = """waited cleared rel_ready halved split stats_ready var_ready eps_added rstd_ready s_ready stats2_ready
            var2_ready eps2_added rstd2_ready tn_ready tn_turned xt_ready xt_hi_ready xt_lo_ready
            q_done q_hi_ready q_ready v_done v_next_ready v_ready keys_done keys_added keys_hi_ready keys_ready
            logits_done gates_ready gates_kept gates_turned gates_t_ready rel_done band_left_ready band_ready
            band_written band_read scores_done max_found neg_max_ready probs_ready inv_ready factor_ready
            weighted_ready turned probs_t_left probs_t_right heads_done heads_ready out_done y_ready""".split()
        s = {n: sem(n) for n in names}
        scale = HD ** -0.5

        def over_batches(eng, body):
            body(0)
            with eng.Fori(1, BATCH - 1) as b:
                body(b)
            body(BATCH - 1)

        def first(b):
            return isinstance(b, int) and b == 0

        def last(b):
            return isinstance(b, int) and b == BATCH - 1

        def started(u):
            return not isinstance(u, int) or 0 <= u < BATCH * STEPS

        def tile(t, b, h):
            return t[:, bass.ds((b * HALVES + h) * DIM, DIM)]

        cleared_at_exit(nc, ctx, semaphores)
        block = ctx.enter_context(nc.Block())

        @block.sync
        def _(sp):
            def shift_band(u, j):
                sp.wait_ge(s["band_ready"], (u + 1) * 2)
                half = j % HALVES
                slab = scratch[j]
                rows = slab[:, :].rearrange("e (q w) -> q e w", w=SEQ + 1)
                sp.dma_start(rows[:, :, 0:P], band[j % 2][:, :, :]).then_inc(s["band_written"], 16)
                sp.wait_ge(s["band_written"], (u + 1) * 16)
                rows = slab[:, 0:P * SEQ].rearrange("e (q w) -> q e w", w=SEQ)
                if half == 0:
                    dst, src = band_in[j][:, :, 0:SEQ - MAXP], rows[:, :, MAXP:SEQ]
                else:
                    dst, src = band_in[j][:, :, MAXP:SEQ], rows[:, :, 0:SEQ - MAXP]
                sp.dma_start(dst, src).then_inc(s["band_read"], 16)

            sp.wait_ge(s["cleared"], STEPS)
            shift_band(0, 0)
            shift_band(1, 1)

            def batch(b):
                for j in range(STEPS):
                    if not (last(b) and j >= 2):
                        shift_band(b * STEPS + j + 2, (j + 2) % STEPS)

            over_batches(sp, batch)
            sp.wait_ge(s["band_read"], BATCH * STEPS * 16)

        @block.gpsimd
        def _(pool):
            for j in range(STEPS):
                gone = slice(SEQ - MAXP, SEQ) if j % HALVES == 0 else slice(0, MAXP)
                pool.memset(band_in[j][:, :, gone], 0.0).then_inc(s["cleared"], 1)

            def deviations(b):
                for m, ve, r, ready, added, done in ((moments, var_eps, rstd, "var_ready", "eps_added", "rstd_ready"),
                                                     (moments2, var_eps2, rstd2, "var2_ready", "eps2_added", "rstd2_ready")):
                    pool.wait_ge(s[ready], b + 1)
                    pool.sem_inc(s["waited"], 1)
                    pool.tensor_scalar(ve[:, :], m[:, :, 1], EPS, None, ALU.add).then_inc(s[added], 1)
                    pool.wait_ge(s[added], b + 1)
                    pool.tensor_tensor(r[:, :], ve[:, :], half_pow[:, :], ALU.pow).then_inc(s[done], 1)

            deviations(0)

            def batch(b):
                for j in range(STEPS):
                    u = b * STEPS + j
                    if j == 0 and not last(b):
                        deviations(b + 1)
                    pool.wait_ge(s["factor_ready"], u + 1)
                    if not (first(b) and j < 2):
                        pool.wait_ge(s["turned"], u - 1)
                    pool.tensor_tensor(weighted[j % 2][:, :, :], probs[j % 2][:, :, :],
                                       factor[j % 2][:, :].unsqueeze(2).broadcast_to([P, QUAD, SEQ]),
                                       ALU.mult).then_inc(s["weighted_ready"], 1)
                    if j == 1:
                        pool.wait_ge(s["v_next_ready"], b + 1)
                        if not first(b):
                            pool.wait_ge(s["heads_done"], b * STEPS)
                        pool.sem_inc(s["waited"], 1)
                        pool.tensor_copy(v[:, :, :], v_next[:, :, :]).then_inc(s["v_ready"], 1)

            over_batches(pool, batch)

        @block.scalar
        def _(act):
            act.wait_ge(loaded, loads)
            act.wait_ge(s["rel_ready"], 4)
            act.activation(qw[0][:, :], w["q_w"][:, :], ACT.Copy).then_inc(s["halved"], 1)
            act.activation(kw[0][:, :], w["k_w"][:, :], ACT.Copy).then_inc(s["halved"], 1)
            act.activation(rel[0][:, :], rel_near[:, :], ACT.Copy).then_inc(s["halved"], 1)

            def turned_x(b):
                act.wait_ge(s["tn_turned"], b + 1)
                act.activation(xt[:, :], misc[:, 0:SEQ], ACT.Identity, bias=w["ln1_b"][:, 0:1],
                               scale=w["ln1_w"][:, 0:1]).then_inc(s["xt_ready"], 1)
                act.wait_ge(s["xt_ready"], b + 1)
                act.activation(xt_hi[:, :], xt[:, :], ACT.Copy).then_inc(s["xt_hi_ready"], 1)

            def queries_high(n, e0):
                act.wait_ge(s["q_done"], n + 1)
                for i in range(2):
                    e = e0 + i
                    ins = act.activation(q_hi[e // QUAD][:, e % QUAD, :], misc[:, i * SEQ:(i + 1) * SEQ], ACT.Identity,
                                         bias=w["q_b"][:, e:e + 1])
                ins.then_inc(s["q_hi_ready"], 1)

            def band_left(u, j, part):
                act.wait_ge(s["rel_done"], u * 2 + part + 1)
                if started(u - 2) and part == 0:
                    act.wait_ge(s["band_written"], (u - 1) * 16)
                act.activation(band[j % 2][:, 2 * part:2 * part + 2, :], rel_ps[:, :, 0:P],
                               ACT.Copy).then_inc(s["band_left_ready"], 1)

            def keys_high(b):
                act.wait_ge(s["keys_added"], b + 1)
                act.wait_ge(s["scores_done"], b * STEPS + 0) if not first(b) else None
                act.activation(keys_hi[:, :, :], keys[:, :, :], ACT.Copy).then_inc(s["keys_hi_ready"], 1)

            def gap(b):
                act.wait_ge(router.gap_ready, b + 1)
                act.activation(router.gap_exp[:, :], router.gap[:, :], ACT.Exp).then_inc(router.gap_exp_ready, 1)

            turned_x(0)
            queries_high(0, 0)
            queries_high(1, 2)
            gap(0)
            keys_high(0)
            queries_high(2, 4)
            queries_high(3, 6)
            for u in range(2):
                for part in range(2):
                    band_left(u, u, part)

            def batch(b):
                for j in range(STEPS):
                    u = b * STEPS + j
                    act.wait_ge(s["neg_max_ready"], u + 1)
                    if not (first(b) and j < 2):
                        act.wait_ge(s["weighted_ready"], u - 1)
                    for e in range(QUAD):
                        ins = act.activation(probs[j % 2][:, e, :], score_ps[:, e, :], ACT.Exp, bias=neg_max[:, e:e + 1],
                                             scale=scale, accum_out=sums[:, e:e + 1])
                    ins.then_inc(s["probs_ready"], 1)
                    if j == 1 and not last(b):
                        turned_x(b + 1)
                    if j == 3 and not last(b):
                        keys_high(b + 1)
                        queries_high(b * 4 + 6, 4)
                    if started(u + 2) and not (last(b) and j >= 2):
                        band_left(u + 2, j, 0)
                    if j == 1 and not last(b):
                        queries_high(b * 4 + 4, 0)
                    if j == 2 and not last(b):
                        gap(b + 1)
                    if j == 3 and not last(b):
                        queries_high(b * 4 + 7, 6)
                    if not (first(b) and j < 2):
                        act.wait_ge(s["turned"], u - 1)
                        act.activation(probs_t[:, 0, :], turn_ps[:, 0, :], ACT.Copy).then_inc(s["probs_t_left"], 1)
                    if started(u + 2) and not (last(b) and j >= 2):
                        band_left(u + 2, j, 1)
                    if j == 1 and not last(b):
                        queries_high(b * 4 + 5, 2)
                    if not (first(b) and j < 2):
                        heads_out(u - 2)

            def heads_out(u):
                act.wait_ge(s["heads_done"], u + 1)
                act.activation(heads_t[:, :], heads_ps[:, :], ACT.Copy).then_inc(s["heads_ready"], 1)

            over_batches(act, batch)
            for u in range(BATCH * STEPS - 2, BATCH * STEPS):
                act.wait_ge(s["turned"], u + 1)
                act.activation(probs_t[:, 0, :], turn_ps[:, 0, :], ACT.Copy).then_inc(s["probs_t_left"], 1)
                heads_out(u)

        @block.vector
        def _(dve):
            dve.wait_ge(loaded, loads)
            for i, at in enumerate((0, 2 * MAXP)):
                dve.tensor_scalar(rel_near[:, i * P:(i + 1) * P], w["rel_t"][:, 0:P], w["rel_t"][:, at:at + 1], None,
                                  ALU.subtract).then_inc(s["rel_ready"], 1)
                dve.tensor_tensor(k_bias[:, i:i + 1], w["k_b"][:, 0:1], w["rel_t"][:, at:at + 1],
                                  ALU.add).then_inc(s["rel_ready"], 1)
            dve.wait_ge(s["halved"], 3)
            dve.wait_ge(s["rel_ready"], 4)
            for full, (hi, lo) in ((w["q_w"], qw), (w["k_w"], kw), (rel_near, rel)):
                dve.tensor_tensor(lo[:, :], full[:, :], hi[:, :].bitcast(F32), ALU.subtract).then_inc(s["split"], 1)

            def norm_x(b):
                for h in range(HALVES):
                    ins = dve.bn_stats(stats[:, h, :], tile(x_sb, b, h))
                ins.then_inc(s["stats_ready"], 1)
                dve.wait_ge(s["stats_ready"], b + 1)
                dve.sem_inc(s["waited"], 1)
                for h in range(HALVES):
                    ins = dve.bn_aggr(moments[:, h, :], stats[:, h, :])
                ins.then_inc(s["var_ready"], 1)

            def norm_s(b):
                dve.wait_ge(s["rstd_ready"], b + 1)
                dve.wait_ge(s["var_ready"], b + 1)
                for h in range(HALVES):
                    ins = dve.tensor_scalar(tile(y_sb, b, h), tile(x_sb, b, h), moments[:, h, 0:1], rstd[:, h:h + 1],
                                            ALU.subtract, ALU.mult)
                ins.then_inc(s["s_ready"], 1)
                dve.wait_ge(s["s_ready"], b + 1)
                dve.sem_inc(s["waited"], 1)
                for h in range(HALVES):
                    ins = dve.bn_stats(stats2[:, h, :], tile(y_sb, b, h))
                ins.then_inc(s["stats2_ready"], 1)
                dve.wait_ge(s["stats2_ready"], b + 1)
                dve.sem_inc(s["waited"], 1)
                for h in range(HALVES):
                    ins = dve.bn_aggr(moments2[:, h, :], stats2[:, h, :])
                ins.then_inc(s["var2_ready"], 1)

            def norm_out(b):
                dve.wait_ge(s["rstd2_ready"], b + 1)
                dve.wait_ge(s["var2_ready"], b + 1)
                for h in range(HALVES):
                    ins = dve.tensor_scalar(tn[:, h, :], tile(y_sb, b, h), moments2[:, h, 0:1], rstd2[:, h:h + 1],
                                            ALU.subtract, ALU.mult)
                ins.then_inc(s["tn_ready"], 1)

            def turned_x_low(b):
                dve.wait_ge(s["xt_hi_ready"], b + 1)
                dve.tensor_tensor(xt_lo[:, :], xt[:, :], xt_hi[:, :].bitcast(F32), ALU.subtract).then_inc(s["xt_lo_ready"], 1)

            def queries_low(n, e0):
                dve.wait_ge(s["q_hi_ready"], n + 1)
                for i in range(2):
                    e = e0 + i
                    ins = dve.scalar_tensor_tensor(
                        out=q_lo[e // QUAD][:, e % QUAD, :], in0=misc[:, i * SEQ:(i + 1) * SEQ], scalar=w["q_b"][:, e:e + 1],
                        in1=q_hi[e // QUAD][:, e % QUAD, :].bitcast(F32), op0=ALU.add, op1=ALU.subtract)
                ins.then_inc(s["q_ready"], 1)

            def values(b):
                dve.wait_ge(s["v_done"], b + 1)
                if not first(b):
                    dve.wait_ge(s["v_ready"], b)
                dve.tensor_tensor(v_next[:, :, :], misc[:, 0:SEQ].rearrange("p (h d) -> p h d", h=HALVES),
                                  w["v_b"][:, :].unsqueeze(1).broadcast_to([P, HALVES, HD]),
                                  ALU.add).then_inc(s["v_next_ready"], 1)

            def keys_in(b):
                dve.wait_ge(s["keys_done"], b + 1)
                if not first(b):
                    dve.wait_ge(s["keys_ready"], b)
                for half, cut in ((0, MAXP), (1, SEQ - MAXP)):
                    for side, (lo, hi) in enumerate(((0, cut), (cut, SEQ))):
                        ins = dve.tensor_scalar(keys[:, half, lo:hi], misc[:, lo:hi], k_bias[:, side:side + 1], None, ALU.add)
                ins.then_inc(s["keys_added"], 1)

            def keys_low(b):
                dve.wait_ge(s["keys_hi_ready"], b + 1)
                dve.tensor_tensor(keys_lo[:, :, :], keys[:, :, :], keys_hi[:, :, :].bitcast(F32),
                                  ALU.subtract).then_inc(s["keys_ready"], 1)

            def logits(b):
                dve.wait_ge(s["logits_done"], b + 1)
                route_logits(dve, router, b, HALVES, misc[:, 0:HALVES * EA].rearrange("p (h e) -> p h e", h=HALVES), None, None)

            def gates_of(b):
                route_gates(dve, router, b, HALVES, gates_now[:, :, :]).then_inc(s["gates_ready"], 1)
                dve.wait_ge(s["gates_ready"], b + 1)
                dst = gates[:, bass.ds(b, 1), :, :].rearrange("p a h e -> p (a h) e")
                dve.tensor_copy(dst, gates_now[:, :, :]).then_inc(s["gates_kept"], 1)

            def band_right(u, j, part):
                dve.wait_ge(s["band_left_ready"], u * 2 + part + 1)
                dve.sem_inc(s["waited"], 1)
                dve.copy_predicated(band[j % 2][:, 2 * part:2 * part + 2, :],
                                    far_mask[:, :].unsqueeze(1).broadcast_to([P, 2, P]),
                                    rel_ps[:, :, P:2 * P]).then_inc(s["band_ready"], 1)

            norm_x(0)
            norm_s(0)
            norm_out(0)
            turned_x_low(0)
            queries_low(0, 0)
            queries_low(1, 2)
            values(0)
            logits(0)
            gates_of(0)
            keys_in(0)
            keys_low(0)
            queries_low(2, 4)
            queries_low(3, 6)
            for u in range(2):
                for part in range(2):
                    band_right(u, u, part)

            def turned_right(u):
                dve.wait_ge(s["turned"], u + 1)
                dve.tensor_copy(probs_t[:, 1, :], turn_ps[:, 1, :]).then_inc(s["probs_t_right"], 1)

            def add_to_y(b):
                dve.wait_ge(s["out_done"], b + 1)
                dst = y_sb[:, bass.ds(b * SEQ, SEQ)]
                dve.tensor_tensor(dst, dst, out_ps[:, 0:SEQ], ALU.add).then_inc(s["y_ready"], 1)

            def batch(b):
                for j in range(STEPS):
                    u = b * STEPS + j
                    dve.wait_ge(s["scores_done"], u + 1)
                    dve.wait_ge(s["band_read"], (u + 1) * 16)
                    dve.sem_inc(s["waited"], 1)
                    for e in range(QUAD):
                        ins = dve.tensor_tensor_reduce(score_ps[:, e, :], score_ps[:, e, :], band_in[j][:, e, :], 1.0, LOWEST,
                                                       ALU.add, ALU.max, row_max[:, e:e + 1])
                    ins.then_inc(s["max_found"], 1)
                    dve.wait_ge(s["max_found"], u + 1)
                    dve.tensor_scalar(neg_max[:, :], row_max[:, :], -scale, None, ALU.mult).then_inc(s["neg_max_ready"], 1)
                    if j == 0:
                        dve.wait_ge(s["gates_turned"], b + 1)
                        dve.tensor_copy(gates_t[:, :], misc[0:EA, 0:SEQ]).then_inc(s["gates_t_ready"], 1)
                        if not last(b):
                            norm_x(b + 1)
                    if j == 1 and not last(b):
                        turned_x_low(b + 1)
                    if j == 2 and not last(b):
                        values(b + 1)
                    if j == 3 and not last(b):
                        keys_low(b + 1)
                        queries_low(b * 4 + 6, 4)
                    if not (last(b) and j >= 2):
                        band_right(u + 2, j, 0)
                    if j == 0 and not last(b):
                        norm_s(b + 1)
                    if j == 1 and not last(b):
                        queries_low(b * 4 + 4, 0)
                    if j == 2 and not last(b):
                        logits(b + 1)
                    if j == 3 and not last(b):
                        queries_low(b * 4 + 7, 6)
                    if not (first(b) and j < 2):
                        turned_right(u - 2)
                    if not (last(b) and j >= 2):
                        band_right(u + 2, j, 1)
                    if j == 1 and not last(b):
                        queries_low(b * 4 + 5, 2)
                    if j == 2 and not last(b):
                        keys_in(b + 1)
                        gates_of(b + 1)
                    dve.wait_ge(s["probs_ready"], u + 1)
                    dve.reciprocal(inv[:, :], sums[:, :]).then_inc(s["inv_ready"], 1)
                    dve.wait_ge(s["inv_ready"], u + 1)
                    dve.wait_ge(s["gates_kept"], b + 1)
                    eg, half = j // HALVES, j % HALVES
                    g = gates[:, bass.ds(b, 1), half, eg * QUAD:(eg + 1) * QUAD].rearrange("p a e -> p (a e)")
                    dve.tensor_tensor(factor[j % 2][:, :], inv[:, :], g, ALU.mult).then_inc(s["factor_ready"], 1)
                    if j == 0 and not last(b):
                        norm_out(b + 1)
                    if j == 2 and not first(b):
                        add_to_y(b - 1)

            over_batches(dve, batch)
            for u in range(BATCH * STEPS - 2, BATCH * STEPS):
                turned_right(u)
            add_to_y(BATCH - 1)

        @block.tensor
        def _(pe):
            pe.wait_ge(loaded, loads)
            pe.wait_ge(s["split"], 3)

            def turn_x(b):
                pe.wait_ge(s["tn_ready"], b + 1)
                for h in range(HALVES):
                    mm = pe.transpose(misc[:, h * P:(h + 1) * P], tn[:, h, :], ident[:, :])
                mm.then_inc(s["tn_turned"], 1)

            def three(out, lhs, rhs, begin, end):
                pe.matmul(out, lhs[1], rhs[0], start=begin, stop=False)
                pe.matmul(out, lhs[0], rhs[1], start=False, stop=False)
                return pe.matmul(out, lhs[0], rhs[0], start=False, stop=end)

            def queries(n, e0):
                for i in range(2):
                    cols = slice((e0 + i) * HD, (e0 + i + 1) * HD)
                    mm = three(misc[:, i * SEQ:(i + 1) * SEQ], [t[:, cols] for t in qw], [xt_hi[:, :], xt_lo[:, :]], True, True)
                mm.then_inc(s["q_done"], 1)

            def values(b):
                for h in range(HALVES):
                    mm = pe.matmul(misc[:, h * HD:(h + 1) * HD], xt[:, h * P:(h + 1) * P], w["v_w"][:, :],
                                   start=True, stop=True)
                mm.then_inc(s["v_done"], 1)

            def keys_of(b):
                three(misc[:, 0:SEQ], [t[:, :] for t in kw], [xt_hi[:, :], xt_lo[:, :]], True, True).then_inc(s["keys_done"], 1)

            def logits(b):
                for h in range(HALVES):
                    mm = pe.matmul(misc[:, h * EA:(h + 1) * EA], xt[:, h * P:(h + 1) * P], w["gate_w"][:, :],
                                   start=True, stop=True)
                mm.then_inc(s["logits_done"], 1)

            def turn_gates(b):
                for h in range(HALVES):
                    mm = pe.transpose(misc[0:EA, h * P:(h + 1) * P], gates_now[:, h, :], ident[:, :])
                mm.then_inc(s["gates_turned"], 1)

            def near(u, j, part):
                if not (isinstance(u, int) and u == 0 and part == 0):
                    pe.wait_ge(s["band_ready"], u * 2 + part)
                eg, half = j // HALVES, j % HALVES
                for i in range(2):
                    e = 2 * part + i
                    cols = slice(half * P, (half + 1) * P)
                    mm = three(rel_ps[:, i, :], [q_hi[eg][:, e, cols], q_lo[eg][:, e, cols]], [rel[0][:, :], rel[1][:, :]],
                               True, True)
                mm.then_inc(s["rel_done"], 1)

            def scores(u, j):
                if not (isinstance(u, int) and u == 0):
                    pe.wait_ge(s["probs_ready"], u)
                eg, half = j // HALVES, j % HALVES
                for e in range(QUAD):
                    cols = slice(half * P, (half + 1) * P)
                    mm = three(score_ps[:, e, :], [q_hi[eg][:, e, cols], q_lo[eg][:, e, cols]],
                               [keys_hi[:, half, :], keys_lo[:, half, :]], True, True)
                mm.then_inc(s["scores_done"], 1)

            def turn_probs(u, parity):
                pe.wait_ge(s["weighted_ready"], u + 1)
                if not (isinstance(u, int) and u == 0):
                    pe.wait_ge(s["probs_t_left"], u)
                    pe.wait_ge(s["probs_t_right"], u)
                for h in range(HALVES):
                    for e in range(QUAD):
                        mm = pe.transpose(turn_ps[:, h, e * P:(e + 1) * P], weighted[parity][:, e, h * P:(h + 1) * P], ident[:, :])
                mm.then_inc(s["turned"], 1)

            def heads(u):
                pe.wait_ge(s["probs_t_left"], u + 1)
                pe.wait_ge(s["probs_t_right"], u + 1)
                if not (isinstance(u, int) and u == 0):
                    pe.wait_ge(s["heads_ready"], u)
                for h in range(HALVES):
                    mm = pe.matmul(heads_ps[:, :], v[:, h, :], probs_t[:, h, :], start=(h == 0), stop=(h == HALVES - 1))
                mm.then_inc(s["heads_done"], 1)

            def project(b, u, j):
                pe.wait_ge(s["heads_ready"], u + 1)
                eg, half = j // HALVES, j % HALVES
                if j == 0:
                    pe.wait_ge(s["gates_t_ready"], b + 1)
                    if not first(b):
                        pe.wait_ge(s["y_ready"], b)
                    for h in range(HALVES):
                        pe.matmul(out_ps[:, h * P:(h + 1) * P], gates_t[:, h * P:(h + 1) * P], w["o_b"][:, :],
                                  start=(h == 0), stop=False, skip_group_check=True)
                for e in range(QUAD):
                    n = eg * QUAD + e
                    mm = pe.matmul(out_ps[:, half * P:(half + 1) * P], heads_t[:, e * P:(e + 1) * P],
                                   w["o_w"][:, n * DIM:(n + 1) * DIM], start=False, stop=(eg == 1 and e == QUAD - 1),
                                   skip_group_check=True)
                if j == STEPS - 1:
                    mm.then_inc(s["out_done"], 1)

            turn_x(0)
            pe.wait_ge(s["xt_lo_ready"], 1)
            queries(0, 0)
            pe.wait_ge(s["q_ready"], 1)
            queries(1, 2)
            pe.wait_ge(s["q_ready"], 2)
            values(0)
            pe.wait_ge(s["v_next_ready"], 1)
            logits(0)
            pe.wait_ge(router.logits_ready, 1)
            keys_of(0)
            pe.wait_ge(s["keys_added"], 1)
            queries(2, 4)
            pe.wait_ge(s["q_ready"], 3)
            queries(3, 6)
            pe.wait_ge(s["keys_ready"], 1)
            for u in range(2):
                for part in range(2):
                    near(u, u, part)

            def batch(b):
                for j in range(STEPS):
                    u = b * STEPS + j
                    if j == 0:
                        pe.wait_ge(s["keys_ready"], b + 1)
                    scores(u, j)
                    if j == 0:
                        pe.wait_ge(s["q_ready"], b * 4 + 4)
                        pe.wait_ge(s["gates_ready"], b + 1)
                        turn_gates(b)
                    if j == 1 and not last(b):
                        pe.wait_ge(s["gates_t_ready"], b + 1)
                        turn_x(b + 1)
                    if j == 2 and not last(b):
                        pe.wait_ge(s["q_ready"], b * 4 + 6)
                        values(b + 1)
                    if j == 3 and not last(b):
                        pe.wait_ge(s["keys_added"], b + 2)
                        queries(b * 4 + 6, 4)
                    if not (first(b) and j < 3):
                        project(b if j == 3 else b - 1, u - 3, (j - 3) % STEPS)
                    if not (last(b) and j >= 2):
                        near(u + 2, (j + 2) % STEPS, 0)
                    if j == 1 and not last(b):
                        pe.wait_ge(s["xt_lo_ready"], b + 2)
                        queries(b * 4 + 4, 0)
                    if j == 2 and not last(b):
                        pe.wait_ge(s["v_next_ready"], b + 2)
                        logits(b + 1)
                    if j == 3 and not last(b):
                        pe.wait_ge(s["q_ready"], b * 4 + 7)
                        queries(b * 4 + 7, 6)
                    if not (first(b) and j < 2):
                        turn_probs(u - 2, j % 2)
                    if not (last(b) and j >= 2):
                        near(u + 2, (j + 2) % STEPS, 1)
                    if j == 1 and not last(b):
                        pe.wait_ge(s["q_ready"], b * 4 + 5)
                        queries(b * 4 + 5, 2)
                    if j == 2 and not last(b):
                        pe.wait_ge(router.logits_ready, b + 2)
                        keys_of(b + 1)
                    if not (first(b) and j < 2):
                        if j == 2:
                            pe.wait_ge(s["v_ready"], b + 1)
                        heads(u - 2)

            over_batches(pe, batch)
            n = BATCH * STEPS
            project(BATCH - 1, n - 3, 1)
            turn_probs(n - 2, 0)
            heads(n - 2)
            project(BATCH - 1, n - 2, 2)
            turn_probs(n - 1, 1)
            heads(n - 1)
            project(BATCH - 1, n - 1, 3)



EF, FH = 16, 64
FF_CHUNKS = EF * FH // P
RUN = 4
RUNS = TILES // RUN
WIDE = RUN * P
LOW_ROWS = 32


def mixture_of_experts(nc, x_sb, y_sb, w, consts, loaded, loads):
    ident, half_pow, experts, select, low_mask = consts
    ctx = ExitStack()
    with ctx:
        def sb(name, shape, dt=F32):
            return ctx.enter_context(nc.sbuf_tensor(f"moe_{name}", shape, dt))

        def pb(name, shape):
            return ctx.enter_context(nc.psum_tensor(f"moe_{name}", shape, F32))

        semaphores = []

        def sem(name):
            semaphores.append(ctx.enter_context(nc.semaphore(f"moe_{name}")))
            return semaphores[-1]

        w1 = [sb("w1_hi", [P, EF * FH], F32R), sb("w1_lo", [P, EF * FH], F32R)]
        stats = sb("stats", [P, RUN, 6])
        moments = sb("moments", [P, RUN, 2])
        var_eps = sb("var_eps", [P, RUN])
        rstd = sb("rstd", [P, RUN])
        tn = sb("tn", [P, RUN, DIM])
        xt = sb("xt", [P, WIDE])
        xt_hi = sb("xt_hi", [P, WIDE], F32R)
        xt_lo = sb("xt_lo", [P, WIDE], F32R)
        router = Router(lambda n, s, d=F32: sb("r_" + n, s, d), lambda n: sem("r_" + n), RUN, EF, experts)
        gates = sb("gates", [P, RUN, LOW_ROWS + EF])
        gates_hi = sb("gates_hi", [LOW_ROWS + EF, WIDE], F32R)
        gates_t = sb("gates_t", [P, WIDE], F32R)
        sel = sb("sel", [P, FF_CHUNKS * P], F32R)
        active = [sb(f"active{i}", [P, WIDE]) for i in range(2)]
        scaled = [sb(f"scaled{i}", [P, WIDE]) for i in range(2)]
        total = sb("total", [P, WIDE])

        hidden_ps = [pb(f"hidden_ps{i}", [P, WIDE]) for i in range(2)]
        gate_ps = [pb(f"gate_ps{i}", [P, WIDE]) for i in range(2)]
        out_ps = pb("out_ps", [P, WIDE])
        misc = pb("misc", [P, WIDE])

        names = """waited cleared halved split stats_ready var_ready eps_added rstd_ready tn_ready tn_turned xt_ready
            xt_hi_ready xt_lo_ready logits_done gates_ready gates_copied gates_turned gates_hi_ready gates_t_ready
            hidden_done spread_done active_ready scaled_ready out_done total_ready x_ready""".split()
        s = {n: sem(n) for n in names}
        C = FF_CHUNKS

        def first(n):
            return isinstance(n, int) and n == 0

        def last(n):
            return isinstance(n, int) and n == RUNS - 1

        def over_runs(eng, body):
            body(0)
            with eng.Fori(1, RUNS - 1) as n:
                body(n)
            body(RUNS - 1)

        def tile(t, n, i):
            return t[:, bass.ds((n * RUN + i) * DIM, DIM)]

        cleared_at_exit(nc, ctx, semaphores)
        block = ctx.enter_context(nc.Block())

        @block.gpsimd
        def _(pool):
            pool.memset(gates_t[:, :].bitcast(F32), 0.0).then_inc(s["cleared"], 1)
            pool.memset(gates[:, :, :], 0.0).then_inc(s["cleared"], 1)

            def deviations(n):
                pool.wait_ge(s["var_ready"], n + 1)
                pool.sem_inc(s["waited"], 1)
                pool.tensor_scalar(var_eps[:, :], moments[:, :, 1], EPS, None, ALU.add).then_inc(s["eps_added"], 1)
                pool.wait_ge(s["eps_added"], n + 1)
                pool.tensor_tensor(rstd[:, :], var_eps[:, :], half_pow[:, 0:RUN], ALU.pow).then_inc(s["rstd_ready"], 1)

            deviations(0)
            with pool.Fori(1, RUNS) as n:
                deviations(n)

        @block.scalar
        def _(act):
            act.wait_ge(loaded, loads)
            act.activation(w1[0][:, :], w["ff_w1"][:, :], ACT.Copy).then_inc(s["halved"], 1)
            act.activation(sel[:, :], select[:, :], ACT.Copy).then_inc(s["halved"], 1)

            def turned_y(n):
                act.wait_ge(s["tn_turned"], n + 1)
                act.activation(xt[:, :], misc[:, :], ACT.Identity, bias=w["ln2_b"][:, 0:1],
                               scale=w["ln2_w"][:, 0:1]).then_inc(s["xt_ready"], 1)

            def high_halves(n):
                act.wait_ge(s["xt_ready"], n + 1)
                if not first(n):
                    act.wait_ge(s["hidden_done"], n * C)
                act.activation(xt_hi[:, :], xt[:, :], ACT.Copy).then_inc(s["xt_hi_ready"], 1)
                act.wait_ge(s["gates_turned"], n + 1)
                act.activation(gates_hi[:, :], misc[0:LOW_ROWS + EF, :], ACT.Copy).then_inc(s["gates_hi_ready"], 1)

            def gap(n):
                act.wait_ge(router.gap_ready, n + 1)
                act.activation(router.gap_exp[:, :], router.gap[:, :], ACT.Exp).then_inc(router.gap_exp_ready, 1)

            turned_y(0)
            gap(0)
            high_halves(0)

            def run(n):
                for c in range(C):
                    u = n * C + c
                    act.wait_ge(s["hidden_done"], u + 1)
                    if not (first(n) and c < 2):
                        act.wait_ge(s["scaled_ready"], u - 1)
                    act.activation(active[c % 2][:, :], hidden_ps[c % 2][:, :], ACT.Relu,
                                   bias=w["ff_b1"][:, c:c + 1]).then_inc(s["active_ready"], 1)
                    if not last(n):
                        if c == 2:
                            turned_y(n + 1)
                        if c == 3:
                            gap(n + 1)
                        if c == C - 1:
                            high_halves(n + 1)

            over_runs(act, run)

        @block.vector
        def _(dve):
            dve.wait_ge(s["halved"], 2)
            dve.wait_ge(s["cleared"], 2)
            dve.tensor_tensor(w1[1][:, :], w["ff_w1"][:, :], w1[0][:, :].bitcast(F32), ALU.subtract).then_inc(s["split"], 1)

            def norm_y(n):
                for i in range(RUN):
                    ins = dve.bn_stats(stats[:, i, :], tile(y_sb, n, i))
                ins.then_inc(s["stats_ready"], 1)
                dve.wait_ge(s["stats_ready"], n + 1)
                dve.sem_inc(s["waited"], 1)
                for i in range(RUN):
                    ins = dve.bn_aggr(moments[:, i, :], stats[:, i, :])
                ins.then_inc(s["var_ready"], 1)

            def norm_out(n):
                dve.wait_ge(s["rstd_ready"], n + 1)
                dve.wait_ge(s["var_ready"], n + 1)
                for i in range(RUN):
                    ins = dve.tensor_scalar(tn[:, i, :], tile(y_sb, n, i), moments[:, i, 0:1], rstd[:, i:i + 1],
                                            ALU.subtract, ALU.mult)
                ins.then_inc(s["tn_ready"], 1)

            def low_halves(n):
                dve.wait_ge(s["xt_hi_ready"], n + 1)
                dve.tensor_tensor(xt_lo[:, :], xt[:, :], xt_hi[:, :].bitcast(F32), ALU.subtract).then_inc(s["xt_lo_ready"], 1)
                dve.wait_ge(s["gates_hi_ready"], n + 1)
                if not first(n):
                    dve.wait_ge(s["spread_done"], n * C)
                rows = slice(0, LOW_ROWS + EF)
                dve.scalar_tensor_tensor(out=gates_t[rows, :], in0=gates_hi[:, :].bitcast(F32), scalar=low_mask[rows, 0:1],
                                         in1=misc[rows, :], op0=ALU.mult, op1=ALU.add).then_inc(s["gates_t_ready"], 1)

            def logits(n):
                dve.wait_ge(s["logits_done"], n + 1)
                route_logits(dve, router, n, RUN, misc[:, 0:RUN * EF].rearrange("p (h e) -> p h e", h=RUN), None, None)

            def gates_of(n):
                route_gates(dve, router, n, RUN, gates[:, :, 0:EF]).then_inc(s["gates_ready"], 1)
                dve.wait_ge(s["gates_ready"], n + 1)
                dve.tensor_copy(gates[:, :, LOW_ROWS:LOW_ROWS + EF], gates[:, :, 0:EF]).then_inc(s["gates_copied"], 1)

            def add_to_x(n):
                dve.wait_ge(s["out_done"], (n + 1) * C)
                dve.tensor_tensor(total[:, :], y_sb[:, bass.ds(n * WIDE, WIDE)], out_ps[:, :], ALU.add).then_inc(s["total_ready"], 1)
                dve.wait_ge(s["total_ready"], n + 1)
                dst = x_sb[:, bass.ds(n * WIDE, WIDE)]
                dve.tensor_tensor(dst, dst, total[:, :], ALU.add).then_inc(s["x_ready"], 1)

            norm_y(0)
            norm_out(0)
            logits(0)
            gates_of(0)
            low_halves(0)

            def run(n):
                for c in range(C):
                    u = n * C + c
                    dve.wait_ge(s["active_ready"], u + 1)
                    dve.wait_ge(s["spread_done"], u + 1)
                    if not (first(n) and c < 2):
                        dve.wait_ge(s["out_done"], u - 1)
                    dve.tensor_tensor(scaled[c % 2][:, :], active[c % 2][:, :], gate_ps[c % 2][:, :],
                                      ALU.mult).then_inc(s["scaled_ready"], 1)
                    if c == 0 and not first(n):
                        add_to_x(n - 1)
                    if not last(n):
                        if c == 0:
                            norm_y(n + 1)
                        if c == 1:
                            norm_out(n + 1)
                        if c == 3:
                            logits(n + 1)
                        if c == 4:
                            gates_of(n + 1)
                        if c == C - 1:
                            low_halves(n + 1)

            over_runs(dve, run)
            add_to_x(RUNS - 1)

        @block.tensor
        def _(pe):
            pe.wait_ge(loaded, loads)
            pe.wait_ge(s["split"], 1)

            def turn_y(n):
                pe.wait_ge(s["tn_ready"], n + 1)
                if not first(n):
                    pe.wait_ge(s["gates_t_ready"], n)
                for i in range(RUN):
                    mm = pe.transpose(misc[:, i * P:(i + 1) * P], tn[:, i, :], ident[:, :])
                mm.then_inc(s["tn_turned"], 1)

            def logits(n):
                pe.wait_ge(s["xt_ready"], n + 1)
                for i in range(RUN):
                    mm = pe.matmul(misc[:, i * EF:(i + 1) * EF], xt[:, i * P:(i + 1) * P], w["ff_gate_w"][:, :],
                                   start=True, stop=True)
                mm.then_inc(s["logits_done"], 1)

            def turn_gates(n):
                pe.wait_ge(s["gates_copied"], n + 1)
                pe.sem_inc(s["waited"], 1)
                for i in range(RUN):
                    mm = pe.transpose(misc[0:LOW_ROWS + EF, i * P:(i + 1) * P], gates[:, i, :], ident[:, :])
                mm.then_inc(s["gates_turned"], 1)

            def hidden(n, c):
                u = n * C + c
                if c == 0:
                    pe.wait_ge(s["xt_lo_ready"], n + 1)
                    pe.wait_ge(s["gates_t_ready"], n + 1)
                if not (first(n) and c < 2):
                    pe.wait_ge(s["active_ready"], u - 1)
                    pe.wait_ge(s["scaled_ready"], u - 1)
                cols = slice(c * P, (c + 1) * P)
                out = hidden_ps[c % 2][:, :]
                pe.matmul(out, w1[1][:, cols], xt_hi[:, :], start=True, stop=False)
                pe.matmul(out, w1[0][:, cols], xt_lo[:, :], start=False, stop=False)
                pe.matmul(out, w1[0][:, cols], xt_hi[:, :], start=False, stop=True).then_inc(s["hidden_done"], 1)
                pe.matmul(gate_ps[c % 2][:, :], sel[:, cols], gates_t[:, :], start=True, stop=True).then_inc(s["spread_done"], 1)

            def out(n, c):
                u = n * C + c
                if c == 0:
                    if not first(n):
                        pe.wait_ge(s["total_ready"], n)
                    for i in range(RUN):
                        pe.matmul(out_ps[:, i * P:(i + 1) * P], gates_t[:, i * P:(i + 1) * P].bitcast(F32), w["ff_b2"][:, :],
                                  start=(i == 0), stop=False, skip_group_check=True)
                pe.wait_ge(s["scaled_ready"], u + 1)
                for i in range(RUN):
                    mm = pe.matmul(out_ps[:, i * P:(i + 1) * P], scaled[c % 2][:, i * P:(i + 1) * P],
                                   w["ff_w2"][:, c * DIM:(c + 1) * DIM], start=False, stop=(c == C - 1), skip_group_check=True)
                mm.then_inc(s["out_done"], 1)
                return mm

            turn_y(0)
            logits(0)
            turn_gates(0)

            def run(n):
                for c in range(C):
                    hidden(n, c)
                    if c > 0:
                        out(n, c - 1)
                    if not last(n):
                        if c == 2:
                            turn_y(n + 1)
                        if c == 3:
                            logits(n + 1)
                        if c == 6:
                            turn_gates(n + 1)
                out(n, C - 1)

            over_runs(pe, run)


EX, FX = 8, 344
PARTS = -(-FX // P)


def gated_experts(nc, x_sb, out_dram, w, consts, loaded, loads):
    ident, half_pow, experts = consts
    ctx = ExitStack()
    with ctx:
        def sb(name, shape, dt=F32):
            return ctx.enter_context(nc.sbuf_tensor(f"ffn_{name}", shape, dt))

        def pb(name, shape):
            return ctx.enter_context(nc.psum_tensor(f"ffn_{name}", shape, F32))

        semaphores = []

        def sem(name):
            semaphores.append(ctx.enter_context(nc.semaphore(f"ffn_{name}")))
            return semaphores[-1]

        C = EX * PARTS
        wg = [sb("wg_hi", [P, C * P], F32R), sb("wg_lo", [P, C * P], F32R)]
        wu = [sb("wu_hi", [P, C * P], F32R), sb("wu_lo", [P, C * P], F32R)]
        stats = sb("stats", [P, RUN, 6])
        moments = sb("moments", [P, RUN, 2])
        var_eps = sb("var_eps", [P, RUN])
        rstd = sb("rstd", [P, RUN])
        tn = sb("tn", [P, RUN, DIM])
        xt = sb("xt", [P, WIDE])
        xt_hi = sb("xt_hi", [P, WIDE], F32R)
        xt_lo = sb("xt_lo", [P, WIDE], F32R)
        router = Router(lambda n, s, d=F32: sb("r_" + n, s, d), lambda n: sem("r_" + n), RUN, EX, experts)
        euler = sb("euler", [P, RUN])
        gates_next = sb("gates_next", [P, RUN, EX])
        gates = sb("gates", [P, RUN, EX])
        gated = [sb(f"gated{i}", [P, WIDE]) for i in range(2)]
        hidden = [sb(f"hidden{i}", [P, WIDE]) for i in range(2)]

        gate_ps = [pb(f"gate_ps{i}", [P, WIDE]) for i in range(2)]
        up_ps = [pb(f"up_ps{i}", [P, WIDE]) for i in range(2)]
        down_ps = [pb(f"down_ps{i}", [P, WIDE]) for i in range(2)]
        misc = pb("misc", [P, WIDE])

        names = """waited cleared halved split stats_ready var_ready eps_added rstd_ready tn_ready tn_turned xt_ready
            xt_hi_ready xt_lo_ready logits_done gates_next_ready gates_ready
            gate_done up_done gated_ready hidden_ready down_done x_ready stored""".split()
        s = {n: sem(n) for n in names}

        def first(n):
            return isinstance(n, int) and n == 0

        def last(n):
            return isinstance(n, int) and n == RUNS - 1

        def over_runs(eng, body):
            body(0)
            with eng.Fori(1, RUNS - 1) as n:
                body(n)
            body(RUNS - 1)

        def tile(t, n, i):
            return t[:, bass.ds((n * RUN + i) * DIM, DIM)]

        cleared_at_exit(nc, ctx, semaphores)
        block = ctx.enter_context(nc.Block())

        @block.sync
        def _(sp):
            def store(n):
                sp.wait_ge(s["x_ready"], (n + 1) * EX)
                sp.dma_start(out_dram[:, bass.ds(n * RUN, RUN), :],
                             x_sb[:, bass.ds(n * WIDE, WIDE)].rearrange("p (t c) -> p t c", c=DIM)).then_inc(s["stored"], 16)

            store(0)
            with sp.Fori(1, RUNS) as n:
                store(n)
            sp.wait_ge(s["stored"], RUNS * 16)

        @block.gpsimd
        def _(pool):
            def deviations(n):
                pool.wait_ge(s["var_ready"], n + 1)
                pool.sem_inc(s["waited"], 1)
                pool.tensor_scalar(var_eps[:, :], moments[:, :, 1], EPS, None, ALU.add).then_inc(s["eps_added"], 1)
                pool.wait_ge(s["eps_added"], n + 1)
                pool.tensor_tensor(rstd[:, :], var_eps[:, :], half_pow[:, 0:RUN], ALU.pow).then_inc(s["rstd_ready"], 1)

            def gap_exp(n):
                pool.wait_ge(router.gap_ready, n + 1)
                pool.tensor_tensor(router.gap_exp[:, :], euler[:, :], router.gap[:, :],
                                   ALU.pow).then_inc(router.gap_exp_ready, 1)

            pool.memset(euler[:, :], math.e).then_inc(s["cleared"], 1)
            pool.wait_ge(s["cleared"], 1)
            deviations(0)
            gap_exp(0)
            with pool.Fori(1, RUNS) as n:
                deviations(n)
                gap_exp(n)

        @block.scalar
        def _(act):
            act.wait_ge(loaded, loads)

            def turned_x(n):
                act.wait_ge(s["tn_turned"], n + 1)
                act.activation(xt[:, :], misc[:, :], ACT.Copy).then_inc(s["xt_ready"], 1)

            def high_half(n):
                act.wait_ge(s["xt_ready"], n + 1)
                if not first(n):
                    act.wait_ge(s["up_done"], n * C)
                act.activation(xt_hi[:, :], xt[:, :], ACT.Copy).then_inc(s["xt_hi_ready"], 1)

            for e in range(EX):
                cols = slice(e * PARTS * P, (e + 1) * PARTS * P)
                act.activation(wg[0][:, cols], w["Wg"][:, cols], ACT.Copy).then_inc(s["halved"], 1)
                act.activation(wu[0][:, cols], w["Wu"][:, cols], ACT.Copy).then_inc(s["halved"], 1)
                if e == 0:
                    turned_x(0)
                    high_half(0)

            def run(n):
                for c in range(C):
                    u = n * C + c
                    act.wait_ge(s["gate_done"], u + 1)
                    if not (first(n) and c < 2):
                        act.wait_ge(s["hidden_ready"], u - 1)
                    act.activation(gated[c % 2][:, :], gate_ps[c % 2][:, :], ACT.Silu).then_inc(s["gated_ready"], 1)
                    if not last(n):
                        if c == 4:
                            turned_x(n + 1)
                        if c == C - 1:
                            high_half(n + 1)

            over_runs(act, run)

        @block.vector
        def _(dve):
            def norm_x(n):
                for i in range(RUN):
                    ins = dve.bn_stats(stats[:, i, :], tile(x_sb, n, i))
                ins.then_inc(s["stats_ready"], 1)
                dve.wait_ge(s["stats_ready"], n + 1)
                dve.sem_inc(s["waited"], 1)
                for i in range(RUN):
                    ins = dve.bn_aggr(moments[:, i, :], stats[:, i, :])
                ins.then_inc(s["var_ready"], 1)

            def norm_out(n):
                dve.wait_ge(s["rstd_ready"], n + 1)
                dve.wait_ge(s["var_ready"], n + 1)
                for i in range(RUN):
                    ins = dve.tensor_scalar(tn[:, i, :], tile(x_sb, n, i), moments[:, i, 0:1], rstd[:, i:i + 1],
                                            ALU.subtract, ALU.mult)
                ins.then_inc(s["tn_ready"], 1)

            def low_half(n):
                dve.wait_ge(s["xt_hi_ready"], n + 1)
                dve.tensor_tensor(xt_lo[:, :], xt[:, :], xt_hi[:, :].bitcast(F32), ALU.subtract).then_inc(s["xt_lo_ready"], 1)

            def logits(n):
                dve.wait_ge(s["logits_done"], n + 1)
                route_logits(dve, router, n, RUN, misc[:, 0:RUN * EX].rearrange("p (h e) -> p h e", h=RUN),
                             w["bs"][:, :].unsqueeze(1).broadcast_to([P, RUN, EX]), None)

            def gates_of(n):
                route_gates(dve, router, n, RUN, gates_next[:, :, :]).then_inc(s["gates_next_ready"], 1)

            def take_gates(n):
                dve.wait_ge(s["gates_next_ready"], n + 1)
                if not first(n):
                    dve.wait_ge(s["x_ready"], n * EX)
                dve.tensor_copy(gates[:, :, :], gates_next[:, :, :]).then_inc(s["gates_ready"], 1)

            def low_weights(e):
                cols = slice(e * PARTS * P, (e + 1) * PARTS * P)
                dve.wait_ge(s["halved"], 2 * e + 2)
                for t, name in ((wg, "Wg"), (wu, "Wu")):
                    ins = dve.tensor_tensor(t[1][:, cols], w[name][:, cols], t[0][:, cols].bitcast(F32), ALU.subtract)
                ins.then_inc(s["split"], 1)

            def combine(n, e):
                dve.wait_ge(s["down_done"], (n * EX + e + 1) * PARTS)
                if not (first(n) and e == 0):
                    dve.wait_ge(s["x_ready"], n * EX + e)
                if e == 0:
                    dve.wait_ge(s["gates_ready"], n + 1)
                for i in range(RUN):
                    dst = tile(x_sb, n, i)
                    ins = dve.scalar_tensor_tensor(out=dst, in0=down_ps[e % 2][:, i * DIM:(i + 1) * DIM],
                                                   scalar=gates[:, i, e:e + 1], in1=dst, op0=ALU.mult, op1=ALU.add)
                ins.then_inc(s["x_ready"], 1)

            norm_x(0)
            norm_out(0)
            low_weights(0)
            low_half(0)
            logits(0)
            gates_of(0)
            take_gates(0)

            def run(n):
                for c in range(C):
                    u = n * C + c
                    e, part = c // PARTS, c % PARTS
                    if first(n) and part == 0 and e + 1 < EX:
                        low_weights(e + 1)
                    dve.wait_ge(s["gated_ready"], u + 1)
                    dve.wait_ge(s["up_done"], u + 1)
                    if not (first(n) and c < 2):
                        dve.wait_ge(s["down_done"], u - 1)
                    dve.tensor_tensor(hidden[c % 2][:, :], gated[c % 2][:, :], up_ps[c % 2][:, :],
                                      ALU.mult).then_inc(s["hidden_ready"], 1)
                    if part == 1 and e > 0:
                        combine(n, e - 1)
                    if c == 1 and not first(n):
                        combine(n - 1, EX - 1)
                        take_gates(n)
                    if not last(n):
                        if c == 2:
                            norm_x(n + 1)
                        if c == 3:
                            norm_out(n + 1)
                        if c == 5:
                            logits(n + 1)
                        if c == 8:
                            gates_of(n + 1)
                        if c == C - 1:
                            low_half(n + 1)

            over_runs(dve, run)
            combine(RUNS - 1, EX - 1)

        @block.tensor
        def _(pe):
            pe.wait_ge(loaded, loads)

            def turn_x(n):
                pe.wait_ge(s["tn_ready"], n + 1)
                if not first(n):
                    pe.wait_ge(router.logits_ready, n)
                for i in range(RUN):
                    mm = pe.transpose(misc[:, i * P:(i + 1) * P], tn[:, i, :], ident[:, :])
                mm.then_inc(s["tn_turned"], 1)

            def logits(n):
                pe.wait_ge(s["xt_ready"], n + 1)
                for i in range(RUN):
                    mm = pe.matmul(misc[:, i * EX:(i + 1) * EX], xt[:, i * P:(i + 1) * P], w["Ws"][:, :],
                                   start=True, stop=True)
                mm.then_inc(s["logits_done"], 1)

            def gate_up(n, c):
                u = n * C + c
                cols = slice(c * P, (c + 1) * P)
                if c == 0:
                    pe.wait_ge(s["xt_lo_ready"], n + 1)
                if first(n) and c % PARTS == 0:
                    pe.wait_ge(s["split"], c // PARTS + 1)
                if not (first(n) and c < 2):
                    pe.wait_ge(s["gated_ready"], u - 1)
                    pe.wait_ge(s["hidden_ready"], u - 1)
                for t, ps, done in ((wg, gate_ps, "gate_done"), (wu, up_ps, "up_done")):
                    out = ps[c % 2][:, :]
                    pe.matmul(out, t[1][:, cols], xt_hi[:, :], start=True, stop=False)
                    pe.matmul(out, t[0][:, cols], xt_lo[:, :], start=False, stop=False)
                    pe.matmul(out, t[0][:, cols], xt_hi[:, :], start=False, stop=True).then_inc(s[done], 1)

            def down(n, c):
                u = n * C + c
                e, part = c // PARTS, c % PARTS
                if part == 0 and not (first(n) and e < 2):
                    pe.wait_ge(s["x_ready"], n * EX + e - 1)
                pe.wait_ge(s["hidden_ready"], u + 1)
                for i in range(RUN):
                    mm = pe.matmul(down_ps[e % 2][:, i * P:(i + 1) * P], hidden[c % 2][:, i * P:(i + 1) * P],
                                   w["Wd"][:, c * DIM:(c + 1) * DIM], start=(part == 0 and i == 0), stop=(part == PARTS - 1),
                                   skip_group_check=True)
                mm.then_inc(s["down_done"], 1)
                return mm

            turn_x(0)
            logits(0)

            def run(n):
                for c in range(C):
                    gate_up(n, c)
                    if c > 0:
                        down(n, c - 1)
                    if not last(n):
                        if c == 4:
                            turn_x(n + 1)
                        if c == 5:
                            logits(n + 1)
                down(n, C - 1)

            over_runs(pe, run)



def _alibi_slopes():
    return np.power(np.float32(2.0), (np.float32(-8.0) * np.arange(1, HEADS + 1, dtype=np.float32)) / np.float32(HEADS))


def _masks(window):
    token = np.arange(SEQ)
    back = token[:, None] - token[None, :]
    seen = (back >= 0) & (back <= window)
    rows = np.where(seen, 0.0, MASKED).astype(np.float32).reshape(HALVES, P, SEQ).transpose(1, 0, 2)
    cols = np.where(seen, 0.0, MASKED).astype(np.float32).T[0:P, :]
    return rows.reshape(P, HALVES * SEQ), cols


def _stack_columns(w):
    out = np.zeros((DIM, HEADS, STRIP), w.dtype)
    for at in (ROW_A, ROW_B, ROW_C):
        out[:, :, at:at + HEAD_DIM] = w.reshape(DIM, HEADS, HEAD_DIM)
    return out.reshape(DIM, HEADS * STRIP)


def _row_masks():
    m = np.zeros((HEADS // GROUPS, STRIP, 2), np.float32)
    m[:, [ROW_SLOPE_LO, ROW_MAX_LO], 0] = -1.0
    m[:, ROW_C:ROW_C + HEAD_DIM, 0] = -1.0
    m[:, ROW_B:ROW_B + HEAD_DIM, 1] = -1.0
    return m.reshape(P, 2)


def _constant_rows(alibi, q_bias=None, k_bias=None):
    q = np.zeros((2, HEADS, STRIP), np.float32)
    k = np.zeros((2, HEADS, STRIP), np.float32)
    k[0, :, [ROW_MAX_HI, ROW_MAX_LO]] = 1.0
    if alibi:
        q[0, :, [ROW_SLOPE_HI, ROW_SLOPE_LO]] = _alibi_slopes()
        k[1, :, [ROW_SLOPE_HI, ROW_SLOPE_LO]] = 1.0
    if q_bias is not None:
        for at in (ROW_A, ROW_B, ROW_C):
            q[0, :, at:at + HEAD_DIM] = q_bias.reshape(HEADS, HEAD_DIM)
            k[0, :, at:at + HEAD_DIM] = k_bias.reshape(HEADS, HEAD_DIM)
    return np.concatenate([q.reshape(2, -1), k.reshape(2, -1)], axis=1)


def _ramp():
    m = np.zeros((P, SEQ), np.float32)
    m[0] = m[32] = 1.0
    m[64] = np.arange(SEQ)
    return m


def _far_mask():
    at = np.arange(P)
    return (at[:, None] + at[None, :] >= P).astype(np.float32)


def _select():
    m = np.zeros((P, FF_CHUNKS * P), np.float32)
    col = np.arange(FF_CHUNKS * P)
    m[col // FH, col] = 1.0
    m[LOW_ROWS + col // FH, col] = 1.0
    return m


def _low_mask():
    m = np.zeros((P, 1), np.float32)
    m[LOW_ROWS:] = -1.0
    return m


def _twice(b2):
    m = np.zeros((P, DIM), b2.dtype)
    m[0:EF] = m[LOW_ROWS:LOW_ROWS + EF] = b2
    return m


def _up_columns(w):
    out = np.zeros((DIM, EX, PARTS * P), w.dtype)
    out[:, :, 0:FX] = w.transpose(1, 0, 2)
    return out.reshape(DIM, EX * PARTS * P)


def _down_rows(w):
    out = np.zeros((EX, PARTS * P, DIM), w.dtype)
    out[:, 0:FX] = w
    return np.ascontiguousarray(out.reshape(EX * PARTS, P, DIM).transpose(1, 0, 2)).reshape(P, EX * PARTS * DIM)



def two_layers(nc, d, out):
    scratch = [nc.dram_tensor(f"band_scratch{i}", [QUAD, SLAB], F32).ap() for i in range(STEPS)]
    out_tiles = out.rearrange("b (h p) c -> p (b h) c", p=P)
    with ExitStack() as ctx:
        def sb(name, shape, dt=F32):
            return ctx.enter_context(nc.sbuf_tensor(name, shape, dt))

        def sem(name):
            return ctx.enter_context(nc.semaphore(name))

        def loaded_tile(name):
            return sb("w_" + name, list(d[name].shape))

        x_sb = sb("x_sb", [P, TILES * DIM])
        y_sb = sb("y_sb", [P, TILES * DIM])
        ident = loaded_tile("ident")
        ident_bf = sb("ident_bf", [P, P], BF16)
        half_pow = sb("half_pow", [P, RUN])
        row_masks = loaded_tile("row_masks")
        ramp = sb("ramp", [P, SEQ], F32R)
        layers = ("a0", "a1")
        mask_rows = {n: sb(f"{n}_mask_rows", [P, HALVES, SEQ]) for n in layers}
        mask_cols = {n: sb(f"{n}_mask_cols", [P, SEQ], BF16) for n in layers}
        stacks = {n: [loaded_tile(f"{n}_{k}") for k in ("wq", "wk", "wv", "wo")] for n in layers}
        const_rows = {n: sb(f"{n}_const_rows", [P, 2 * HEADS * STRIP]) for n in layers}
        a1_bias = loaded_tile("a1_bias")
        head_names = ("ln1_w", "ln1_b", "gate_w", "q_w", "q_b", "k_w", "k_b", "v_w", "v_b", "o_w", "o_b", "rel_t")
        expert_names = ("ln2_w", "ln2_b", "ff_gate_w", "ff_w1", "ff_b1", "ff_w2", "ff_b2", "select", "low_mask", "experts")
        w = {n: loaded_tile(n) for n in head_names + expert_names}

        far_mask = sb("far_mask", [P, P], U8)

        first_loaded = sem("first_loaded")
        later_loaded = sem("later_loaded")
        last_loaded = sem("last_loaded")
        zeros_set = sem("zeros_set")
        scratch_zeroed = sem("scratch_zeroed")
        constants = sem("constants")

        with ExitStack() as prep:
            ramp_in = prep.enter_context(nc.sbuf_tensor("ramp_in", [P, SEQ], F32))
            far_in = prep.enter_context(nc.sbuf_tensor("far_in", [P, P], F32))
            cols_in = {n: prep.enter_context(nc.sbuf_tensor(f"{n}_cols_in", [P, SEQ], F32)) for n in layers}

            with nc.Block() as block:
                @block.sync
                def _(sp):
                    def load(dst, src, done=first_loaded):
                        sp.dma_start(dst, src).then_inc(done, 16)

                    load(x_sb[:, :].rearrange("p (t c) -> p t c", c=DIM), d["x"].rearrange("b (h p) c -> p (b h) c", p=P))
                    for name, dst in (("ident", ident), ("row_masks", row_masks), ("ramp", ramp_in), ("far_mask", far_in)):
                        load(dst[:, :], d[name])
                    for n in layers:
                        load(mask_rows[n][:, :, :], d[f"{n}_mask_rows"].rearrange("p (h k) -> p h k", h=HALVES))
                        load(cols_in[n][:, :], d[f"{n}_mask_cols"])
                        for at, row in ((0, 0), (32, 0), (64, 1)):
                            load(const_rows[n][at:at + 1, :], d[f"{n}_const_rows"][row:row + 1, :])
                    for dst, k in zip(stacks["a0"], ("wq", "wk", "wv", "wo")):
                        load(dst[:, :], d[f"a0_{k}"])
                    for dst, k in zip(stacks["a1"], ("wq", "wk", "wv", "wo")):
                        load(dst[:, :], d[f"a1_{k}"], later_loaded)
                    load(a1_bias[:, :], d["a1_bias"], later_loaded)
                    for n in head_names + expert_names:
                        load(w[n][:, :], d[n], later_loaded)

                @block.gpsimd
                def _(pool):
                    pool.memset(half_pow[:, :], -0.5).then_inc(constants, 1)
                    pool.memset(y_sb[:, 0:QUAD * SLAB // P], 0.0).then_inc(zeros_set, 1)
                    pool.wait_ge(zeros_set, 1)
                    for t in scratch:
                        pool.dma_start(t.rearrange("e s -> (e s)").rearrange("(p s) -> p s", p=P),
                                       y_sb[:, 0:QUAD * SLAB // P]).then_inc(scratch_zeroed, 16)

                @block.vector
                def _(dve):
                    dve.wait_ge(first_loaded, 16 * (1 + 4 + 2 * 5 + 4))
                    dve.tensor_copy(ident_bf[:, :], ident[:, :]).then_inc(constants, 1)
                    dve.tensor_copy(ramp[:, :], ramp_in[:, :]).then_inc(constants, 1)
                    dve.tensor_copy(far_mask[:, :], far_in[:, :]).then_inc(constants, 1)
                    for n in layers:
                        dve.tensor_copy(mask_cols[n][:, :], cols_in[n][:, :]).then_inc(constants, 1)
                    dve.wait_ge(constants, 6)

        def attention_phase(name, bias):
            attention(nc, Attention(name, name == "a0"), x_sb, stacks[name] + [const_rows[name], bias],
                      (ident, ident_bf, mask_rows[name], mask_cols[name], row_masks, ramp, half_pow[:, 0:HALVES]), constants, 6)

        attention_phase("a0", None)
        mixture_of_heads(nc, x_sb, y_sb, w, (ident, half_pow[:, 0:HALVES], w["experts"][:, 0:EA], far_mask),
                         scratch, later_loaded, 16 * (5 + len(w)))
        mixture_of_experts(nc, x_sb, y_sb, w, (ident, half_pow, w["experts"], w["select"], w["low_mask"]),
                           later_loaded, 16 * (5 + len(w)))
        last_names = ("Ws", "bs", "Wg", "Wu", "Wd")
        w_last = {n: loaded_tile(n) for n in last_names}
        with nc.Block() as block:
            @block.sync
            def _(sp):
                for n in last_names:
                    sp.dma_start(w_last[n][:, :], d[n]).then_inc(last_loaded, 16)

        attention_phase("a1", a1_bias)
        gated_experts(nc, x_sb, out_tiles, w_last, (ident, half_pow, w["experts"][:, 0:EX]), last_loaded, 16 * len(w_last))



def _laid_out(i):
    rows_of = lambda a: np.ascontiguousarray(np.broadcast_to(a[None], (P,) + a.shape))
    column = lambda a: a[:, None]
    d = {"x": i["L0_attn_x"], "ident": np.eye(P, dtype=np.float32), "row_masks": _row_masks(), "ramp": _ramp()}
    qkv = i["L1_attn_W_attn"]
    q_b, k_b, v_b = np.split(i["L1_attn_b_attn"], 3)
    projections = {"a0": [i["L0_attn_" + k].T for k in ("Wq", "Wk", "Wv", "Wo")],
                   "a1": [qkv[:, 0:DIM], qkv[:, DIM:2 * DIM], qkv[:, 2 * DIM:], i["L1_attn_W_proj"]]}
    for n, window in (("a0", SEQ), ("a1", LOCAL_WINDOW)):
        wq, wk, wv, wo = projections[n]
        d[f"{n}_mask_rows"], d[f"{n}_mask_cols"] = _masks(window)
        d[f"{n}_wq"], d[f"{n}_wk"], d[f"{n}_wv"], d[f"{n}_wo"] = _stack_columns(wq), _stack_columns(wk), wv, wo
    d["a0_const_rows"] = _constant_rows(True)
    d["a1_const_rows"] = _constant_rows(False, q_b, k_b)
    d["a1_bias"] = rows_of(np.concatenate([v_b, i["L1_attn_b_proj"]]))
    f = {k[len("L0_ffn_"):]: a for k, a in i.items() if k.startswith("L0_ffn_")}
    for n in ("ln1_w", "ln1_b", "ln2_w", "ln2_b", "k_b"):
        d[n] = column(f[n])
    d.update(gate_w=f["attn_gate_w"], k_w=f["k_w"], v_w=f["v_w"], o_b=f["o_b"], v_b=rows_of(f["v_b"]),
             q_w=f["q_w"].transpose(1, 0, 2).reshape(DIM, EA * HD), q_b=f["q_b"].T,
             o_w=f["o_w"].transpose(1, 0, 2).reshape(HD, EA * DIM), rel_t=f["rel_table"].T, far_mask=_far_mask(),
             ff_gate_w=f["ff_gate_w"], ff_w1=f["ff_w1"].transpose(1, 0, 2).reshape(DIM, EF * FH),
             ff_b1=f["ff_b1"].reshape(FF_CHUNKS, P).T,
             ff_w2=f["ff_w2"].reshape(FF_CHUNKS, P, DIM).transpose(1, 0, 2).reshape(P, FF_CHUNKS * DIM),
             ff_b2=_twice(f["ff_b2"]), select=_select(), low_mask=_low_mask(),
             experts=rows_of(np.arange(EF, dtype=np.float32)))
    d.update(Ws=i["L1_ffn_Ws"], bs=rows_of(i["L1_ffn_bs"]), Wg=_up_columns(i["L1_ffn_Wg"]), Wu=_up_columns(i["L1_ffn_Wu"]),
             Wd=_down_rows(i["L1_ffn_Wd"]))
    return {n: np.ascontiguousarray(a) for n, a in d.items()}


def kernel(**inputs):
    import concourse.bacc as bacc
    from concourse.bass_utils import run_bass_kernel_spmd

    nc = bacc.Bacc("TRN2", target_bir_lowering=False, num_devices=1)
    data = _laid_out({n: np.asarray(a) for n, a in inputs.items()})
    arrays, d = {}, {}
    for name, a in data.items():
        arrays[f"in_{name}"] = a
        d[name] = nc.dram_tensor(f"in_{name}", a.shape, mybir.dt.from_np(a.dtype), kind="ExternalInput").ap()
    out = nc.dram_tensor("out", (BATCH, SEQ, DIM), F32, kind="ExternalOutput").ap()
    two_layers(nc, d, out)
    return run_bass_kernel_spmd(nc, [arrays], core_ids=[0]).results[0]["out"]
```

```python
import math
from contextlib import ExitStack

import concourse.bass as bass
from concourse import mybir
import numpy as np

F32 = mybir.dt.float32
F32R = mybir.dt.float32r
BF16 = mybir.dt.bfloat16
U8 = mybir.dt.uint8
ALU = mybir.AluOpType
ACT = mybir.ActivationFunctionType

P = 128
BATCH, SEQ, DIM = 16, 256, 128
HALVES = SEQ // P
TILES = BATCH * HALVES
EPS = 1e-5
MASKED = -1e30
LOWEST = -3e38

HEADS, HEAD_DIM = 16, 8
GROUP = 4
GROUPS = HEADS // GROUP
PAIRS = GROUP // 2
STRIP = P // GROUP
ROW_SLOPE_HI, ROW_MAX_HI, ROW_SLOPE_LO, ROW_MAX_LO = 0, 1, 2, 3
ROW_A, ROW_B, ROW_C = 4, 12, 20
LOCAL_WINDOW = 32


class Attention:

    def __init__(self, name, alibi):
        self.name = name
        self.alibi = alibi
        self.keys = ((0, P), (0 if alibi else P - LOCAL_WINDOW, SEQ))
        self.early_queries = SEQ if alibi else P + LOCAL_WINDOW


def cleared_at_exit(nc, ctx, semaphores):
    def clear():
        with nc.Block() as block:
            @block.sync
            def _(sp):
                for semaphore in semaphores:
                    sp.sem_clear(semaphore)

    ctx.callback(clear)



def attention(nc, cfg, x_sb, weights, consts, loaded, loads, x_loaded=None):
    wq_stack, wk_stack, wv, wo, const_rows, bias_rows = weights
    ident, ident_bf, mask_rows, mask_cols, row_masks, ramp, half_pow = consts
    n0 = cfg.name
    ctx = ExitStack()
    with ctx:
        def sb(name, shape, dt=F32):
            return ctx.enter_context(nc.sbuf_tensor(f"{n0}_{name}", shape, dt))

        def pb(name, shape):
            return ctx.enter_context(nc.psum_tensor(f"{n0}_{name}", shape, F32))

        semaphores = []

        def sem(name):
            semaphores.append(ctx.enter_context(nc.semaphore(f"{n0}_{name}")))
            return semaphores[-1]

        w_hi = {k: sb(f"w{k}_hi", [P, HEADS * STRIP], F32R) for k in "qk"}
        w_lo = {k: sb(f"w{k}_lo", [P, HEADS * STRIP], F32R) for k in "qk"}
        c_rows = {k: sb(f"c{k}", [P, HEADS * STRIP], F32R) for k in "qk"}
        c_tmp = sb("c_tmp", [P, 2 * HEADS * STRIP], F32R)
        stats = sb("stats", [P, HALVES, 6])
        moments = sb("moments", [P, HALVES, 2])
        var_eps = sb("var_eps", [P, HALVES])
        rstd = sb("rstd", [P, HALVES])
        xn = sb("xn", [P, HALVES, DIM])
        xt = sb("xt", [P, SEQ])
        xt_hi = sb("xt_hi", [P, SEQ], F32R)
        xt_lo = sb("xt_lo", [P, SEQ], F32R)
        qk_hi = sb("qk_hi", [P, 2 * SEQ], F32R)
        q_max_hi = sb("q_max_hi", [P, SEQ], F32R)
        k_stack = [sb(f"k_stack{i}", [P, SEQ], F32R) for i in range(2)]
        q_stack = [sb(f"q_stack{i}", [P, SEQ], F32R) for i in range(2)]
        k_heads = [sb(f"k_heads{i}", [P, GROUP, SEQ], F32R) for i in range(GROUPS)]
        q_full = [sb(f"q_full{i}", [P, SEQ + P], F32R) for i in range(2)]
        row_max = sb("row_max", [P, HALVES, GROUP])
        neg_max = sb("neg_max", [P, HALVES, P])
        if cfg.alibi:
            pieces, width = 1, SEQ + P
        else:
            pieces, width = 2, P + LOCAL_WINDOW
        probs = sb("probs", [P, GROUP, pieces * width])
        v_aug = sb("v_aug", [P, HALVES, HEADS, STRIP])
        o_t = [sb(f"o_t{i}", [P, SEQ]) for i in range(2)]
        inv_sum = sb("inv_sum", [P, HALVES * GROUP])
        attn = sb("attn", [P, HALVES, DIM])
        attn_t = sb("attn_t", [P, SEQ])

        qk_ps = [pb(f"qk_ps{i}", [P, 2 * SEQ]) for i in range(2)]
        score_ps = pb("score_ps", [P, GROUP, 2 * SEQ])
        o_ps = pb("o_ps", [P, 2 * SEQ])
        misc = pb("misc", [P, 2 * SEQ])

        zeroed = sem("zeroed")
        waited = sem("waited")
        halved = sem("halved")
        split = sem("split")
        stats_done = sem("stats_done")
        var_ready = sem("var_ready")
        eps_added = sem("eps_added")
        rstd_ready = sem("rstd_ready")
        xn_ready = sem("xn_ready")
        xn_turned = sem("xn_turned")
        xt_hi_ready = sem("xt_hi_ready")
        xt_ready = sem("xt_ready")
        v_done = sem("v_done")
        v_ready = sem("v_ready")
        qk_done = sem("qk_done")
        qk_hi_ready = sem("qk_hi_ready")
        stacks_ready = sem("stacks_ready")
        k_stack_ready = sem("k_stack_ready")
        k_heads_zeroed = sem("k_heads_zeroed")
        k_heads_act = sem("k_heads_act")
        k_heads_pool = sem("k_heads_pool")
        scores_done = sem("scores_done")
        max_part = sem("max_part")
        max_ready = sem("max_ready")
        max_added = sem("max_added")
        q_hi_ready = sem("q_hi_ready")
        q_full_ready = sem("q_full_ready")
        scores_t_done = sem("scores_t_done")
        probs_ready = sem("probs_ready")
        pv_done = sem("pv_done")
        o_t_ready = sem("o_t_ready")
        out_turned = sem("out_turned")
        inv_ready = sem("inv_ready")
        attn_ready = sem("attn_ready")
        attn_turned = sem("attn_turned")
        attn_t_ready = sem("attn_t_ready")
        projected = sem("projected")
        x_added = sem("x_added")
        x_biased = sem("x_biased")

        def over_batches(eng, body):
            body(0)
            with eng.Fori(1, BATCH - 1) as b:
                body(b)
            body(BATCH - 1)

        def is_first(b):
            return isinstance(b, int) and b == 0

        def is_last(b):
            return isinstance(b, int) and b == BATCH - 1

        def x_half(b, h):
            return x_sb[:, bass.ds((b * HALVES + h) * DIM, DIM)]

        cleared_at_exit(nc, ctx, semaphores)
        block = ctx.enter_context(nc.Block())

        @block.gpsimd
        def _(pool):
            for k in "qk":
                pool.memset(c_rows[k][:, :].bitcast(F32), 0.0).then_inc(zeroed, 1)
            for t in q_full:
                pool.memset(t[:, SEQ:].bitcast(F32), 0.0).then_inc(zeroed, 1)
            pool.memset(neg_max[:, :, :], 0.0).then_inc(zeroed, 1)
            pool.memset(v_aug[:, :, :, :], 0.0).then_inc(zeroed, 1)
            pool.wait_ge(zeroed, 6)
            pool.memset(v_aug[:, :, :, HEAD_DIM:HEAD_DIM + 1], 1.0).then_inc(zeroed, 1)

            def inverse_deviation(b):
                pool.wait_ge(var_ready, b + 1)
                pool.sem_inc(waited, 1)
                pool.tensor_scalar(var_eps[:, :], moments[:, :, 1], EPS, None, ALU.add).then_inc(eps_added, 1)
                pool.wait_ge(eps_added, b + 1)
                pool.tensor_tensor(rstd[:, :], var_eps[:, :], half_pow[:, :], ALU.pow).then_inc(rstd_ready, 1)

            def spread_keys(u, g):
                pool.wait_ge(k_stack_ready, u + 1)
                heads = slice(GROUP // 2, GROUP)
                pool.tensor_tensor(k_heads[g][:, heads, :],
                                   k_stack[g % 2][:, :].bitcast(F32).unsqueeze(1).broadcast_to([P, GROUP // 2, SEQ]),
                                   row_masks[:, 2 + GROUP // 2:2 + GROUP].unsqueeze(2).broadcast_to([P, GROUP // 2, SEQ]),
                                   ALU.mult).then_inc(k_heads_pool, 1)

            inverse_deviation(0)
            spread_keys(0, 0)
            spread_keys(1, 1)

            def batch(b):
                for g in range(GROUPS):
                    if not (is_last(b) and g >= 2):
                        spread_keys(b * GROUPS + g + 2, (g + 2) % GROUPS)
                    if g == 0 and not is_last(b):
                        inverse_deviation(b + 1)

            over_batches(pool, batch)

        @block.scalar
        def _(act):
            act.wait_ge(loaded, loads)
            scale = HEAD_DIM ** -0.5
            act.activation(w_hi["q"][:, :], wq_stack[:, :], ACT.Copy, scale=scale).then_inc(halved, 1)
            act.activation(w_hi["k"][:, :], wk_stack[:, :], ACT.Copy).then_inc(halved, 1)

            def turned_x(b):
                act.wait_ge(xn_turned, b + 1)
                act.activation(xt[:, :], misc[:, 0:SEQ], ACT.Copy)
                act.activation(xt_hi[:, :], misc[:, 0:SEQ], ACT.Copy).then_inc(xt_hi_ready, 1)

            def high_half(u, parity):
                act.wait_ge(qk_done, u + 1)
                if not (isinstance(u, int) and u == 0):
                    act.wait_ge(stacks_ready, u)
                act.activation(qk_hi[:, :], qk_ps[parity][:, :], ACT.Copy).then_inc(qk_hi_ready, 1)

            def high_half_with_max(u, parity):
                act.wait_ge(max_added, u + 1)
                act.activation(q_max_hi[:, :], qk_ps[parity][:, 0:SEQ], ACT.Copy).then_inc(q_hi_ready, 1)

            def spread_keys(u, g):
                act.wait_ge(k_stack_ready, u + 1)
                for i in range(GROUP // 2):
                    rows = slice(i * STRIP, (i + 1) * STRIP)
                    ins = act.activation(k_heads[g][rows, i, :], k_stack[g % 2][rows, :].bitcast(F32), ACT.Copy)
                ins.then_inc(k_heads_act, 1)

            def output_copied(u, parity):
                act.wait_ge(pv_done, u + 1)
                act.activation(o_t[parity][:, :], o_ps[:, 0:SEQ], ACT.Copy).then_inc(o_t_ready, 1)

            turned_x(0)
            act.wait_ge(zeroed, 7)
            act.wait_ge(k_heads_zeroed, GROUPS)
            row_scale = 1.0 if cfg.alibi else scale
            for j, k in enumerate("qk"):
                cols = slice(j * 512, j * 512 + 512)
                s = row_scale if k == "q" else 1.0
                act.activation(c_rows[k][0:1, :], const_rows[0:1, cols], ACT.Copy, scale=s).then_inc(halved, 1)
                act.activation(c_tmp[32:33, cols], const_rows[32:33, cols], ACT.Copy, scale=s).then_inc(halved, 1)
                act.activation(c_rows[k][64:65, :], const_rows[64:65, cols], ACT.Copy).then_inc(halved, 1)
            high_half(0, 0)
            spread_keys(0, 0)
            high_half(1, 1)
            spread_keys(1, 1)
            high_half_with_max(0, 0)

            def unit(b, g):
                u = b * GROUPS + g
                if not (is_first(b) and g == 0):
                    output_copied(u - 1, (g - 1) % 2)
                if not (is_last(b) and g >= 2):
                    high_half(u + 2, g % 2)
                if g == 1 and not is_last(b):
                    turned_x(b + 1)
                for pair in range(PAIRS):
                    act.wait_ge(scores_t_done, u * PAIRS + pair + 1)
                    banks = score_ps[:, 2 * pair:2 * pair + 2, :]
                    if pieces == 1:
                        src, dst = banks[:, :, 0:width], probs[:, 2 * pair:2 * pair + 2, :]
                    else:
                        src = banks.rearrange("p h (k q) -> p h k q", k=2)[:, :, :, 0:width]
                        dst = probs[:, 2 * pair:2 * pair + 2, :].rearrange("p h (k q) -> p h k q", k=2)
                    act.activation(dst, src, ACT.Exp).then_inc(probs_ready, 1)
                    if pair == 0 and not (is_last(b) and g >= 2):
                        spread_keys(u + 2, (g + 2) % GROUPS)
                if not (is_last(b) and g == 3):
                    high_half_with_max(u + 1, (g + 1) % 2)
                if g == 1 and not is_first(b):
                    attention_turned(b - 1)

            def attention_turned(b):
                act.wait_ge(attn_turned, b + 1)
                act.activation(attn_t[:, :], misc[:, 0:SEQ], ACT.Copy).then_inc(attn_t_ready, 1)

            def batch(b):
                for g in range(GROUPS):
                    unit(b, g)

            over_batches(act, batch)
            output_copied(BATCH * GROUPS - 1, (GROUPS - 1) % 2)
            attention_turned(BATCH - 1)

        @block.vector
        def _(dve):
            dve.wait_ge(loaded, loads)

            def moments_of(b):
                for h in range(HALVES):
                    dve.bn_stats(stats[:, h, :], x_half(b, h)).then_inc(stats_done, 1)
                dve.wait_ge(stats_done, b * HALVES + HALVES)
                dve.sem_inc(waited, 1)
                for h in range(HALVES):
                    ins = dve.bn_aggr(moments[:, h, :], stats[:, h, :])
                ins.then_inc(var_ready, 1)

            def normalise(b):
                dve.wait_ge(rstd_ready, b + 1)
                dve.wait_ge(var_ready, b + 1)
                for h in range(HALVES):
                    ins = dve.tensor_scalar(xn[:, h, :], x_half(b, h), moments[:, h, 0:1], rstd[:, h:h + 1],
                                            ALU.subtract, ALU.mult)
                ins.then_inc(xn_ready, 1)

            def turned_x_low(b):
                dve.wait_ge(xt_hi_ready, b + 1)
                dve.tensor_tensor(xt_lo[:, :], misc[:, 0:SEQ], xt_hi[:, :].bitcast(F32),
                                  ALU.subtract).then_inc(xt_ready, 1)

            def stacks(u, parity):
                dve.wait_ge(qk_hi_ready, u + 1)
                ps = qk_ps[parity]
                for dst, at, mask, done in ((k_stack[parity], SEQ, 1, k_stack_ready), (q_stack[parity], 0, 0, stacks_ready)):
                    dve.scalar_tensor_tensor(
                        out=dst[:, :], in0=qk_hi[:, at:at + SEQ].bitcast(F32), scalar=row_masks[:, mask:mask + 1],
                        in1=ps[:, at:at + SEQ], op0=ALU.mult, op1=ALU.add).then_inc(done, 1)

            def maxima(u, parity):
                for pair in range(PAIRS):
                    dve.wait_ge(scores_done, u * PAIRS + pair + 1)
                    dve.sem_inc(waited, 1)
                    for h in range(HALVES):
                        lo, hi = cfg.keys[h]
                        for i in range(2):
                            n = 2 * pair + i
                            banked = score_ps[:, 2 * pair + h, i * (hi - lo):(i + 1) * (hi - lo)]
                            ins = dve.tensor_tensor_reduce(banked, banked, mask_rows[:, h, lo:hi], 1.0, LOWEST,
                                                           ALU.add, ALU.max, row_max[:, h, n:n + 1])
                    ins.then_inc(max_part, 1)
                dve.wait_ge(max_part, u * PAIRS + PAIRS)
                cols = neg_max[:, :, :].rearrange("q h (i r two) -> q (h i) r two", r=STRIP // 2, two=2)
                src = row_max[:, :, :].rearrange("q h i -> q (h i)").unsqueeze(2).broadcast_to([P, HALVES * GROUP, 2])
                dve.tensor_scalar(cols[:, :, 0:2, 1], src, -1.0, None, ALU.mult).then_inc(max_ready, 1)

            def queries_with_max(u, parity):
                dve.wait_ge(q_hi_ready, u + 1)
                dve.scalar_tensor_tensor(
                    out=q_full[parity][:, 0:SEQ], in0=q_max_hi[:, :].bitcast(F32), scalar=row_masks[:, 0:1],
                    in1=qk_ps[parity][:, 0:SEQ], op0=ALU.mult, op1=ALU.add).then_inc(q_full_ready, 1)

            def output_rows(u, g):
                dve.wait_ge(out_turned, u + 1)
                o = o_ps[:, SEQ:].rearrange("q (i r) -> q i r", r=STRIP)
                dve.reciprocal(inv_sum[:, :], o[:, :, HEAD_DIM]).then_inc(inv_ready, 1)
                dve.wait_ge(inv_ready, u + 1)
                for h in range(HALVES):
                    ins = dve.tensor_tensor(
                        attn[:, h, g * GROUP * HEAD_DIM:(g + 1) * GROUP * HEAD_DIM].rearrange("q (i d) -> q i d", d=HEAD_DIM),
                        o[:, h * GROUP:(h + 1) * GROUP, 0:HEAD_DIM],
                        inv_sum[:, h * GROUP:(h + 1) * GROUP].unsqueeze(2).broadcast_to([P, GROUP, HEAD_DIM]), ALU.mult)
                    if h == HALVES - 1:
                        ins.then_inc(attn_ready, 1)

            def add_to_x(b):
                dve.wait_ge(projected, b + 1)
                dst = x_sb[:, bass.ds(b * SEQ, SEQ)]
                dve.tensor_tensor(dst, dst, misc[:, 0:SEQ], ALU.add).then_inc(x_added, 1)
                if bias_rows is not None:
                    dve.wait_ge(x_added, b + 1)
                    dve.tensor_tensor(dst.rearrange("p (h c) -> p h c", h=HALVES), dst.rearrange("p (h c) -> p h c", h=HALVES),
                                      bias_rows[:, DIM:2 * DIM].unsqueeze(1).broadcast_to([P, HALVES, DIM]),
                                      ALU.add).then_inc(x_biased, 1)

            moments_of(0)
            for t in k_heads:
                dve.memset(t[:, 0:GROUP // 2, :].bitcast(F32), 0.0).then_inc(k_heads_zeroed, 1)
            normalise(0)
            scale = HEAD_DIM ** -0.5
            dve.wait_ge(halved, 2)
            for k, src, s in (("q", wq_stack, scale), ("k", wk_stack, 1.0)):
                dve.scalar_tensor_tensor(out=w_lo[k][:, :], in0=src[:, :], scalar=s,
                                         in1=w_hi[k][:, :].bitcast(F32), op0=ALU.mult,
                                         op1=ALU.subtract).then_inc(split, 1)
            turned_x_low(0)
            dve.wait_ge(halved, 8)
            row_scale = 1.0 if cfg.alibi else scale
            for j, k in enumerate("qk"):
                cols = slice(j * 512, j * 512 + 512)
                dve.scalar_tensor_tensor(out=c_rows[k][32:33, :], in0=const_rows[32:33, cols],
                                         scalar=row_scale if k == "q" else 1.0,
                                         in1=c_tmp[32:33, cols].bitcast(F32), op0=ALU.mult,
                                         op1=ALU.subtract).then_inc(split, 1)
            dve.wait_ge(zeroed, 7)
            stacks(0, 0)
            stacks(1, 1)
            maxima(0, 0)
            queries_with_max(0, 0)

            def values_in(b):
                dve.wait_ge(v_done, b + 1)
                src = misc[:, 0:SEQ].rearrange("p (n d) -> p n d", d=HEAD_DIM)
                dst = v_aug[:, :, :, :].rearrange("p k h r -> p (k h) r")[:, :, 0:HEAD_DIM]
                if bias_rows is None:
                    dve.tensor_copy(dst, src).then_inc(v_ready, 1)
                else:
                    for h in range(HALVES):
                        ins = dve.tensor_tensor(dst[:, h * HEADS:(h + 1) * HEADS, :], src[:, h * HEADS:(h + 1) * HEADS, :],
                                                bias_rows[:, 0:DIM].rearrange("p (n d) -> p n d", d=HEAD_DIM), ALU.add)
                    ins.then_inc(v_ready, 1)

            def unit(b, g):
                u = b * GROUPS + g
                if not (is_last(b) and g == 3):
                    maxima(u + 1, (g + 1) % 2)
                if not (is_last(b) and g >= 2):
                    stacks(u + 2, g % 2)
                if g == 0:
                    values_in(b)
                    if not is_last(b):
                        moments_of(b + 1)
                if g == 1 and not is_last(b):
                    turned_x_low(b + 1)
                if not (is_first(b) and g == 0):
                    output_rows(u - 1, (g - 1) % GROUPS)
                if not (is_last(b) and g == 3):
                    queries_with_max(u + 1, (g + 1) % 2)
                if g == 0 and not is_last(b):
                    normalise(b + 1)
                if g == 2 and not is_first(b):
                    add_to_x(b - 1)

            def batch(b):
                for g in range(GROUPS):
                    unit(b, g)

            if x_loaded is not None:
                dve.wait_ge(*x_loaded)
            over_batches(dve, batch)
            output_rows(BATCH * GROUPS - 1, GROUPS - 1)
            add_to_x(BATCH - 1)

        @block.tensor
        def _(pe):
            pe.wait_ge(loaded, loads)

            def turn_x(b):
                pe.wait_ge(xn_ready, b + 1)
                for h in range(HALVES):
                    mm = pe.transpose(misc[:, h * P:(h + 1) * P], xn[:, h, :], ident[:, :])
                mm.then_inc(xn_turned, 1)

            def values(b):
                for h in range(HALVES):
                    mm = pe.matmul(misc[:, h * DIM:(h + 1) * DIM], xt[:, h * P:(h + 1) * P], wv[:, :],
                                   start=True, stop=True)
                mm.then_inc(v_done, 1)

            def queries_keys(g, parity):
                for k, at, ramp_or_one in (("q", 0, 0), ("k", SEQ, 0)):
                    out = qk_ps[parity][:, at:at + SEQ]
                    cols = slice(g * P, (g + 1) * P)
                    pe.matmul(out, c_rows[k][:, cols], ramp[:, :], start=(k == "q"), stop=False, skip_group_check=True)
                    pe.matmul(out, w_hi[k][:, cols], xt_lo[:, :], start=False, stop=False, skip_group_check=True)
                    pe.matmul(out, w_lo[k][:, cols], xt_hi[:, :], start=False, stop=False, skip_group_check=True)
                    mm = pe.matmul(out, w_hi[k][:, cols], xt_hi[:, :], start=False, stop=True, skip_group_check=True)
                mm.then_inc(qk_done, 1)

            def scores(b, g):
                u, parity = b * GROUPS + g, g % 2
                pe.wait_ge(stacks_ready, u + 1)
                pe.wait_ge(k_heads_act, u + 1)
                for pair in range(PAIRS):
                    if pair > 0:
                        pe.wait_ge(k_heads_pool, u + 1)
                    if isinstance(u, int) and u == 1:
                        pe.wait_ge(max_part, pair + 1)
                    elif not (isinstance(u, int) and u == 0):
                        pe.wait_ge(probs_ready, (u - 2) * PAIRS + pair + 1)
                    for h in range(HALVES):
                        lo, hi = cfg.keys[h]
                        mm = pe.matmul(score_ps[:, 2 * pair + h, 0:2 * (hi - lo)], q_stack[parity][:, h * P:(h + 1) * P],
                                       k_heads[g][:, 2 * pair:2 * pair + 2, lo:hi], start=True, stop=True)
                    mm.then_inc(scores_done, 1)

            def add_max(u, parity):
                pe.wait_ge(max_ready, u + 1)
                for h in range(HALVES):
                    mm = pe.matmul(qk_ps[parity][:, h * P:(h + 1) * P], neg_max[:, h, :], ident[:, :],
                                   start=False, stop=True, skip_group_check=True)
                mm.then_inc(max_added, 1)

            def scores_turned(u, g, pair, last):
                if last:
                    pe.wait_ge(probs_ready, (u - 1) * PAIRS + pair + 1)
                else:
                    pe.wait_ge(max_part, (u + 1) * PAIRS + pair + 1)
                heads = range(2 * pair, 2 * pair + 2)
                for i in heads:
                    for h in range(HALVES):
                        n = (P if cfg.alibi else P + LOCAL_WINDOW) if h == 0 else P
                        pe.matmul(score_ps[:, i, h * SEQ:h * SEQ + n], ident_bf[:, :], mask_cols[:, 0:n],
                                  start=(h == 0), stop=False, skip_group_check=True)
                for i in heads:
                    for h in range(HALVES):
                        mm = pe.matmul(score_ps[:, i, h * SEQ:(h + 1) * SEQ], k_heads[g][:, i, h * P:(h + 1) * P],
                                       q_full[g % 2][:, h * P:h * P + SEQ], start=False, stop=True, skip_group_check=True)
                mm.then_inc(scores_t_done, 1)

            def probs_values(u, g):
                pe.wait_ge(probs_ready, (u + 1) * PAIRS)
                if not (isinstance(u, int) and u == 0):
                    pe.wait_ge(attn_ready, u)
                for h in range(HALVES):
                    n = cfg.early_queries if h == 0 else P
                    at = 0 if h == 0 else (SEQ if cfg.alibi else width)
                    for i in range(GROUP):
                        mm = pe.matmul(o_ps[i * STRIP:(i + 1) * STRIP, h * P:h * P + n],
                                       v_aug[:, h, g * GROUP + i, :], probs[:, i, at:at + n],
                                       start=(h == 0), stop=(h == HALVES - 1), skip_group_check=True)
                mm.then_inc(pv_done, 1)

            def turn_output(u, parity):
                pe.wait_ge(o_t_ready, u + 1)
                for h in range(HALVES):
                    mm = pe.transpose(o_ps[:, SEQ + h * P:SEQ + (h + 1) * P], o_t[parity][:, h * P:(h + 1) * P], ident[:, :])
                mm.then_inc(out_turned, 1)

            def turn_attention(b):
                pe.wait_ge(attn_ready, (b + 1) * GROUPS)
                for h in range(HALVES):
                    mm = pe.transpose(misc[:, h * P:(h + 1) * P], attn[:, h, :], ident[:, :])
                mm.then_inc(attn_turned, 1)

            def project(b):
                pe.wait_ge(attn_t_ready, b + 1)
                for h in range(HALVES):
                    mm = pe.matmul(misc[:, h * DIM:(h + 1) * DIM], attn_t[:, h * P:(h + 1) * P], wo[:, :],
                                   start=True, stop=True)
                mm.then_inc(projected, 1)

            turn_x(0)
            pe.wait_ge(split, 4)
            pe.wait_ge(halved, 8)
            pe.wait_ge(xt_ready, 1)
            queries_keys(0, 0)
            queries_keys(1, 1)
            scores(0, 0)
            add_max(0, 0)

            def unit(b, g):
                u = b * GROUPS + g
                last = is_last(b) and g == 3
                if not last:
                    scores(b + (g + 1) // GROUPS, (g + 1) % GROUPS)
                if not (is_first(b) and g == 0):
                    if g == 1:
                        pe.wait_ge(v_ready, b + 1)
                    probs_values(u - 1, (g - 1) % GROUPS)
                pe.wait_ge(q_full_ready, u + 1)
                if not (is_last(b) and g >= 2):
                    if g == 2:
                        pe.wait_ge(xt_ready, b + 2)
                    queries_keys((g + 2) % GROUPS, g % 2)
                if g == 0:
                    values(b)
                if g == 1 and not is_last(b):
                    pe.wait_ge(v_ready, b + 1)
                    turn_x(b + 1)
                if g == 2 and not is_first(b):
                    project(b - 1)
                for pair in range(PAIRS):
                    scores_turned(u, g, pair, last)
                if not last:
                    add_max(u + 1, (g + 1) % 2)
                if g == 1 and not is_first(b):
                    if not is_last(b):
                        pe.wait_ge(xt_ready, b + 2)
                    turn_attention(b - 1)
                if not (is_first(b) and g == 0):
                    turn_output(u - 1, (g - 1) % 2)

            def batch(b):
                for g in range(GROUPS):
                    unit(b, g)

            over_batches(pe, batch)
            probs_values(BATCH * GROUPS - 1, GROUPS - 1)
            turn_output(BATCH * GROUPS - 1, 1)
            turn_attention(BATCH - 1)
            project(BATCH - 1)



def route_logits(dve, t, count, n_tiles, logits_ps, bias, done):
    if bias is None:
        dve.tensor_copy(t.logits[:, :, :], logits_ps).then_inc(t.logits_ready, 1)
    else:
        dve.tensor_tensor(t.logits[:, :, :], logits_ps, bias, ALU.add).then_inc(t.logits_ready, 1)
    dve.wait_ge(t.logits_ready, count + 1)
    dve.sem_inc(t.waited, 1)
    for n in range(n_tiles):
        ins = dve.max(t.top[:, n, :], t.logits[:, n, :])
    ins.then_inc(t.top_ready, 1)
    dve.wait_ge(t.top_ready, count + 1)
    dve.tensor_tensor(t.gap[:, :], t.top[:, :, 1], t.top[:, :, 0], ALU.subtract).then_inc(t.gap_ready, 1)
    for n in range(n_tiles):
        ins = dve.max_index(t.index[:, n, :], t.top[:, n, :], t.logits[:, n, :])
    ins.then_inc(t.index_ready, 1)
    dve.wait_ge(t.index_ready, count + 1)
    dve.tensor_copy(t.chosen[:, :, :], t.index[:, :, 0:2]).then_inc(t.chosen_ready, 1)


def route_shares(dve, t, count):
    dve.wait_ge(t.gap_exp_ready, count + 1)
    dve.tensor_scalar(t.total[:, :], t.gap_exp[:, :], 1.0, None, ALU.add).then_inc(t.total_ready, 1)
    dve.wait_ge(t.total_ready, count + 1)
    dve.reciprocal(t.share[:, :, 0], t.total[:, :]).then_inc(t.first_ready, 1)
    dve.wait_ge(t.first_ready, count + 1)
    dve.tensor_tensor(t.share[:, :, 1], t.gap_exp[:, :], t.share[:, :, 0], ALU.mult).then_inc(t.share_ready, 1)


def route_gates(eng, t, count, n_tiles, gates):
    eng.wait_ge(t.share_ready, count + 1)
    eng.wait_ge(t.chosen_ready, count + 1)
    eng.sem_inc(t.waited, 1)
    for n in range(n_tiles):
        for k in range(2):
            ins = eng.tensor_scalar(t.placed[:, n, k, :], t.experts[:, :], t.chosen[:, n, k:k + 1],
                                    t.share[:, n, k:k + 1], ALU.is_equal, ALU.mult)
    ins.then_inc(t.placed_ready, 1)
    eng.wait_ge(t.placed_ready, count + 1)
    first, second = t.placed[:, :, 0, :], t.placed[:, :, 1, :]
    return eng.tensor_tensor(gates, first, second, ALU.add)


class Router:

    def __init__(self, sb, sem, n_tiles, n_experts, experts):
        self.experts = experts
        self.logits = sb("logits", [P, n_tiles, n_experts])
        self.top = sb("top", [P, n_tiles, 8])
        self.index = sb("index", [P, n_tiles, 8], mybir.dt.uint32)
        self.chosen = sb("chosen", [P, n_tiles, 2])
        self.gap = sb("gap", [P, n_tiles])
        self.gap_exp = sb("gap_exp", [P, n_tiles])
        self.total = sb("total", [P, n_tiles])
        self.share = sb("share", [P, n_tiles, 2])
        self.placed = sb("placed", [P, n_tiles, 2, n_experts])
        self.waited = sem("waited")
        self.logits_ready = sem("logits_ready")
        self.top_ready = sem("top_ready")
        self.gap_ready = sem("gap_ready")
        self.index_ready = sem("index_ready")
        self.chosen_ready = sem("chosen_ready")
        self.gap_exp_ready = sem("gap_exp_ready")
        self.total_ready = sem("total_ready")
        self.first_ready = sem("first_ready")
        self.share_ready = sem("share_ready")
        self.placed_ready = sem("placed_ready")


HD = 128
EA = 8
MAXP = 64
QUAD = 4
STEPS = (EA // QUAD) * HALVES
SLAB = P * (SEQ + 1)


def mixture_of_heads(nc, x_sb, y_sb, w, consts, scratch, scratch_zeroed, loaded, loads):
    ident, half_pow, experts, far_mask = consts
    ctx = ExitStack()
    with ctx:
        def sb(name, shape, dt=F32):
            return ctx.enter_context(nc.sbuf_tensor(f"moa_{name}", shape, dt))

        def pb(name, shape):
            return ctx.enter_context(nc.psum_tensor(f"moa_{name}", shape, F32))

        semaphores = []

        def sem(name):
            semaphores.append(ctx.enter_context(nc.semaphore(f"moa_{name}")))
            return semaphores[-1]

        qw = [sb("qw_hi", [P, EA * HD], F32R), sb("qw_lo", [P, EA * HD], F32R)]
        kw = [sb("kw_hi", [P, HD], F32R), sb("kw_lo", [P, HD], F32R)]
        rel = [sb("rel_hi", [P, 2 * P], F32R), sb("rel_lo", [P, 2 * P], F32R)]
        rel_near = sb("rel_near", [P, 2 * P])
        k_bias = sb("k_bias", [P, 2])
        stats = sb("stats", [P, HALVES, 6])
        stats2 = sb("stats2", [P, HALVES, 6])
        moments = sb("moments", [P, HALVES, 2])
        moments2 = sb("moments2", [P, HALVES, 2])
        var_eps = sb("var_eps", [P, HALVES])
        var_eps2 = sb("var_eps2", [P, HALVES])
        rstd = sb("rstd", [P, HALVES])
        rstd2 = sb("rstd2", [P, HALVES])
        tn = sb("tn", [P, HALVES, DIM])
        xt = sb("xt", [P, SEQ])
        xt_hi = sb("xt_hi", [P, SEQ], F32R)
        xt_lo = sb("xt_lo", [P, SEQ], F32R)
        router = Router(lambda n, s, d=F32: sb("r_" + n, s, d), lambda n: sem("r_" + n), HALVES, EA, experts)
        gates = sb("gates", [P, BATCH, HALVES, EA])
        gates_now = sb("gates_now", [P, HALVES, EA])
        gates_t = sb("gates_t", [EA, SEQ])
        q_hi = [sb(f"q_hi{i}", [P, QUAD, SEQ], F32R) for i in range(2)]
        q_lo = [sb(f"q_lo{i}", [P, QUAD, SEQ], F32R) for i in range(2)]
        keys = sb("keys", [P, HALVES, SEQ])
        keys_hi = sb("keys_hi", [P, HALVES, SEQ], F32R)
        keys_lo = sb("keys_lo", [P, HALVES, SEQ], F32R)
        v_next = sb("v_next", [P, HALVES, HD])
        v = sb("v", [P, HALVES, HD])
        band = [sb(f"band{i}", [P, QUAD, P]) for i in range(2)]
        band_in = [sb(f"band_in{i}", [P, QUAD, SEQ]) for i in range(STEPS)]
        row_max = sb("row_max", [P, QUAD])
        neg_max = sb("neg_max", [P, QUAD])
        sums = sb("sums", [P, QUAD])
        inv = sb("inv", [P, QUAD])
        factor = [sb(f"factor{i}", [P, QUAD]) for i in range(2)]
        probs = [sb(f"probs{i}", [P, QUAD, SEQ]) for i in range(2)]
        weighted = [sb(f"weighted{i}", [P, QUAD, SEQ]) for i in range(2)]
        probs_t = sb("probs_t", [P, HALVES, QUAD * P])
        heads_t = sb("heads_t", [P, QUAD * P])

        rel_ps = pb("rel_ps", [P, 2, 2 * P])
        score_ps = pb("score_ps", [P, QUAD, SEQ])
        turn_ps = pb("turn_ps", [P, HALVES, QUAD * P])
        heads_ps = pb("heads_ps", [P, QUAD * P])
        out_ps = pb("out_ps", [P, 4 * P])
        misc = pb("misc", [P, 4 * P])

        names = """waited cleared rel_ready halved split stats_ready var_ready eps_added rstd_ready s_ready stats2_ready
            var2_ready eps2_added rstd2_ready tn_ready tn_turned xt_ready xt_hi_ready xt_lo_ready
            q_done q_hi_ready q_ready v_done v_next_ready v_ready keys_done keys_added keys_hi_ready keys_ready
            logits_done gates_ready gates_kept gates_turned gates_t_ready rel_done band_left_ready band_ready
            band_written band_read scores_done max_found neg_max_ready probs_ready inv_ready factor_ready
            weighted_ready turned probs_t_left probs_t_right heads_done heads_ready out_done y_ready""".split()
        s = {n: sem(n) for n in names}
        scale = HD ** -0.5

        score_cols = score_ps[:, :, :].rearrange("p e s -> p (e s)")
        turn_halves = [turn_ps[:, h, :].rearrange("p (e w) -> p e w", e=2) for h in range(HALVES)]
        early_bands = [rel_ps[:, :, :], *turn_halves, rel_ps[:, :, :]]
        early = [score_cols[:, 0:4 * P], score_cols[:, 4 * P:8 * P], turn_ps[:, 0, :], turn_ps[:, 1, :]]

        def over_batches(eng, body):
            body(0)
            with eng.Fori(1, BATCH - 1) as b:
                body(b)
            body(BATCH - 1)

        def first(b):
            return isinstance(b, int) and b == 0

        def last(b):
            return isinstance(b, int) and b == BATCH - 1

        def started(u):
            return not isinstance(u, int) or 0 <= u < BATCH * STEPS

        def tile(t, b, h):
            return t[:, bass.ds((b * HALVES + h) * DIM, DIM)]

        cleared_at_exit(nc, ctx, semaphores)
        block = ctx.enter_context(nc.Block())

        @block.sync
        def _(sp):
            def shift_band(u, j):
                sp.wait_ge(s["band_ready"], (u + 1) * 2)
                half = j % HALVES
                slab = scratch[j]
                rows = slab[:, :].rearrange("e (q w) -> q e w", w=SEQ + 1)
                sp.dma_start(rows[:, :, 0:P], band[j % 2][:, :, :]).then_inc(s["band_written"], 16)
                sp.wait_ge(s["band_written"], (u + 1) * 16)
                rows = slab[:, 0:P * SEQ].rearrange("e (q w) -> q e w", w=SEQ)
                if half == 0:
                    dst, src = band_in[j][:, :, 0:SEQ - MAXP], rows[:, :, MAXP:SEQ]
                else:
                    dst, src = band_in[j][:, :, MAXP:SEQ], rows[:, :, 0:SEQ - MAXP]
                sp.dma_start(dst, src).then_inc(s["band_read"], 16)

            sp.wait_ge(scratch_zeroed, 16 * STEPS)
            sp.wait_ge(s["cleared"], STEPS)
            shift_band(0, 0)
            shift_band(1, 1)

            def batch(b):
                for j in range(STEPS):
                    if not (last(b) and j >= 2):
                        shift_band(b * STEPS + j + 2, (j + 2) % STEPS)

            over_batches(sp, batch)
            sp.wait_ge(s["band_read"], BATCH * STEPS * 16)

        @block.gpsimd
        def _(pool):
            for j in range(STEPS):
                gone = slice(SEQ - MAXP, SEQ) if j % HALVES == 0 else slice(0, MAXP)
                pool.memset(band_in[j][:, :, gone], 0.0).then_inc(s["cleared"], 1)

            def deviations(b):
                for m, ve, r, ready, added, done in ((moments, var_eps, rstd, "var_ready", "eps_added", "rstd_ready"),
                                                     (moments2, var_eps2, rstd2, "var2_ready", "eps2_added", "rstd2_ready")):
                    pool.wait_ge(s[ready], b + 1)
                    pool.sem_inc(s["waited"], 1)
                    pool.tensor_scalar(ve[:, :], m[:, :, 1], EPS, None, ALU.add).then_inc(s[added], 1)
                    pool.wait_ge(s[added], b + 1)
                    pool.tensor_tensor(r[:, :], ve[:, :], half_pow[:, :], ALU.pow).then_inc(s[done], 1)

            def gates_of(b):
                route_gates(pool, router, b, HALVES, gates_now[:, :, :]).then_inc(s["gates_ready"], 1)
                pool.wait_ge(s["gates_ready"], b + 1)
                pool.sem_inc(s["waited"], 1)
                dst = gates[:, bass.ds(b, 1), :, :].rearrange("p a h e -> p (a h) e")
                pool.tensor_copy(dst, gates_now[:, :, :]).then_inc(s["gates_kept"], 1)

            deviations(0)
            gates_of(0)

            def batch(b):
                for j in range(STEPS):
                    u = b * STEPS + j
                    if j == 3 and not last(b):
                        gates_of(b + 1)
                    if j == 0 and not last(b):
                        deviations(b + 1)
                    pool.wait_ge(s["factor_ready"], u + 1)
                    if not (first(b) and j < 2):
                        pool.wait_ge(s["turned"], u - 1)
                    pool.tensor_tensor(weighted[j % 2][:, :, :], probs[j % 2][:, :, :],
                                       factor[j % 2][:, :].unsqueeze(2).broadcast_to([P, QUAD, SEQ]),
                                       ALU.mult).then_inc(s["weighted_ready"], 1)
                    if j == 1:
                        pool.wait_ge(s["v_next_ready"], b + 1)
                        if not first(b):
                            pool.wait_ge(s["heads_done"], b * STEPS)
                        pool.sem_inc(s["waited"], 1)
                        pool.tensor_copy(v[:, :, :], v_next[:, :, :]).then_inc(s["v_ready"], 1)

            over_batches(pool, batch)

        @block.scalar
        def _(act):
            act.wait_ge(loaded, loads)
            act.wait_ge(s["rel_ready"], 4)
            act.activation(qw[0][:, :], w["q_w"][:, :], ACT.Copy).then_inc(s["halved"], 1)
            act.activation(kw[0][:, :], w["k_w"][:, :], ACT.Copy).then_inc(s["halved"], 1)
            act.activation(rel[0][:, :], rel_near[:, :], ACT.Copy).then_inc(s["halved"], 1)

            def turned_x(b):
                act.wait_ge(s["tn_turned"], b + 1)
                act.activation(xt[:, :], misc[:, 0:SEQ], ACT.Identity, bias=w["ln1_b"][:, 0:1],
                               scale=w["ln1_w"][:, 0:1]).then_inc(s["xt_ready"], 1)
                act.wait_ge(s["xt_ready"], b + 1)
                act.activation(xt_hi[:, :], xt[:, :], ACT.Copy).then_inc(s["xt_hi_ready"], 1)

            def queries_high(n, e0, bank=misc):
                act.wait_ge(s["q_done"], n + 1)
                for i in range(2):
                    e = e0 + i
                    ins = act.activation(q_hi[e // QUAD][:, e % QUAD, :], bank[:, i * SEQ:(i + 1) * SEQ], ACT.Identity,
                                         bias=w["q_b"][:, e:e + 1])
                ins.then_inc(s["q_hi_ready"], 1)

            def band_left(u, j, part, bank=rel_ps):
                act.wait_ge(s["rel_done"], u * 2 + part + 1)
                if started(u - 2) and part == 0:
                    act.wait_ge(s["band_written"], (u - 1) * 16)
                act.activation(band[j % 2][:, 2 * part:2 * part + 2, :], bank[:, :, 0:P],
                               ACT.Copy).then_inc(s["band_left_ready"], 1)

            def keys_in(b, bank=misc):
                act.wait_ge(s["keys_done"], b + 1)
                if not first(b):
                    act.wait_ge(s["keys_ready"], b)
                for half, cut in ((0, MAXP), (1, SEQ - MAXP)):
                    for side, (lo, hi) in enumerate(((0, cut), (cut, SEQ))):
                        ins = act.activation(keys[:, half, lo:hi], bank[:, lo:hi], ACT.Identity,
                                             bias=k_bias[:, side:side + 1])
                ins.then_inc(s["keys_added"], 1)

            def keys_high(b):
                act.wait_ge(s["keys_added"], b + 1)
                if not first(b):
                    act.wait_ge(s["scores_done"], b * STEPS)
                act.activation(keys_hi[:, :, :], keys[:, :, :], ACT.Copy).then_inc(s["keys_hi_ready"], 1)

            def gap(b):
                act.wait_ge(router.gap_ready, b + 1)
                act.activation(router.gap_exp[:, :], router.gap[:, :], ACT.Exp).then_inc(router.gap_exp_ready, 1)

            turned_x(0)
            queries_high(0, 0, early[0])
            queries_high(1, 2, early[1])
            keys_in(0)
            keys_high(0)
            queries_high(2, 4, early[2])
            queries_high(3, 6, early[3])
            for u in range(2):
                for part in range(2):
                    band_left(u, u, part, early_bands[2 * u + part])
            gap(0)

            def turned_left(u):
                act.wait_ge(s["turned"], u + 1)
                act.activation(probs_t[:, 0, :], turn_ps[:, 0, :], ACT.Copy).then_inc(s["probs_t_left"], 1)

            def batch(b):
                for j in range(STEPS):
                    u = b * STEPS + j
                    if not (last(b) and j >= 2):
                        band_left(u + 2, j, 0)
                    if j == 1 and not last(b):
                        turned_x(b + 1)
                    if j == 3 and not last(b):
                        queries_high(b * 4 + 6, 4)
                    if not (first(b) and j < 2):
                        turned_left(u - 2)
                    if j == 1 and not last(b):
                        queries_high(b * 4 + 4, 0)
                    if j == 3 and not last(b):
                        keys_high(b + 1)
                        queries_high(b * 4 + 7, 6)
                    act.wait_ge(s["neg_max_ready"], u + 1)
                    if not (first(b) and j < 2):
                        act.wait_ge(s["weighted_ready"], u - 1)
                    for e in range(QUAD):
                        ins = act.activation(probs[j % 2][:, e, :], score_ps[:, e, :], ACT.Exp, bias=neg_max[:, e:e + 1],
                                             scale=scale, accum_out=sums[:, e:e + 1])
                    ins.then_inc(s["probs_ready"], 1)
                    if not (last(b) and j >= 2):
                        band_left(u + 2, j, 1)
                    if not (first(b) and j < 2):
                        heads_out(u - 2)
                    if j == 1 and not last(b):
                        queries_high(b * 4 + 5, 2)
                    if j == 2 and not last(b):
                        gap(b + 1)
                        keys_in(b + 1)

            def heads_out(u):
                act.wait_ge(s["heads_done"], u + 1)
                act.activation(heads_t[:, :], heads_ps[:, :], ACT.Copy).then_inc(s["heads_ready"], 1)

            over_batches(act, batch)
            for u in range(BATCH * STEPS - 2, BATCH * STEPS):
                turned_left(u)
                heads_out(u)

        @block.vector
        def _(dve):
            dve.wait_ge(loaded, loads)
            dve.wait_ge(scratch_zeroed, 16 * STEPS)
            def norm_x(b):
                for h in range(HALVES):
                    ins = dve.bn_stats(stats[:, h, :], tile(x_sb, b, h))
                ins.then_inc(s["stats_ready"], 1)
                dve.wait_ge(s["stats_ready"], b + 1)
                dve.sem_inc(s["waited"], 1)
                for h in range(HALVES):
                    ins = dve.bn_aggr(moments[:, h, :], stats[:, h, :])
                ins.then_inc(s["var_ready"], 1)

            def norm_s(b):
                dve.wait_ge(s["rstd_ready"], b + 1)
                dve.wait_ge(s["var_ready"], b + 1)
                for h in range(HALVES):
                    ins = dve.tensor_scalar(tile(y_sb, b, h), tile(x_sb, b, h), moments[:, h, 0:1], rstd[:, h:h + 1],
                                            ALU.subtract, ALU.mult)
                ins.then_inc(s["s_ready"], 1)
                dve.wait_ge(s["s_ready"], b + 1)
                dve.sem_inc(s["waited"], 1)
                for h in range(HALVES):
                    ins = dve.bn_stats(stats2[:, h, :], tile(y_sb, b, h))
                ins.then_inc(s["stats2_ready"], 1)
                dve.wait_ge(s["stats2_ready"], b + 1)
                dve.sem_inc(s["waited"], 1)
                for h in range(HALVES):
                    ins = dve.bn_aggr(moments2[:, h, :], stats2[:, h, :])
                ins.then_inc(s["var2_ready"], 1)

            def norm_out(b):
                dve.wait_ge(s["rstd2_ready"], b + 1)
                dve.wait_ge(s["var2_ready"], b + 1)
                for h in range(HALVES):
                    ins = dve.tensor_scalar(tn[:, h, :], tile(y_sb, b, h), moments2[:, h, 0:1], rstd2[:, h:h + 1],
                                            ALU.subtract, ALU.mult)
                ins.then_inc(s["tn_ready"], 1)

            def turned_x_low(b):
                dve.wait_ge(s["xt_hi_ready"], b + 1)
                dve.tensor_tensor(xt_lo[:, :], xt[:, :], xt_hi[:, :].bitcast(F32), ALU.subtract).then_inc(s["xt_lo_ready"], 1)

            def queries_low(n, e0, bank=misc):
                dve.wait_ge(s["q_hi_ready"], n + 1)
                for i in range(2):
                    e = e0 + i
                    ins = dve.scalar_tensor_tensor(
                        out=q_lo[e // QUAD][:, e % QUAD, :], in0=bank[:, i * SEQ:(i + 1) * SEQ], scalar=w["q_b"][:, e:e + 1],
                        in1=q_hi[e // QUAD][:, e % QUAD, :].bitcast(F32), op0=ALU.add, op1=ALU.subtract)
                ins.then_inc(s["q_ready"], 1)

            def values(b, bank=misc):
                dve.wait_ge(s["v_done"], b + 1)
                if not first(b):
                    dve.wait_ge(s["v_ready"], b)
                dve.tensor_tensor(v_next[:, :, :], bank[:, 0:SEQ].rearrange("p (h d) -> p h d", h=HALVES),
                                  w["v_b"][:, :].unsqueeze(1).broadcast_to([P, HALVES, HD]),
                                  ALU.add).then_inc(s["v_next_ready"], 1)

            def keys_low(b):
                dve.wait_ge(s["keys_hi_ready"], b + 1)
                dve.tensor_tensor(keys_lo[:, :, :], keys[:, :, :], keys_hi[:, :, :].bitcast(F32),
                                  ALU.subtract).then_inc(s["keys_ready"], 1)

            def logits(b, bank=misc):
                dve.wait_ge(s["logits_done"], b + 1)
                route_logits(dve, router, b, HALVES, bank[:, 0:HALVES * EA].rearrange("p (h e) -> p h e", h=HALVES), None, None)

            def band_right(u, j, part, bank=rel_ps):
                dve.wait_ge(s["band_left_ready"], u * 2 + part + 1)
                dve.sem_inc(s["waited"], 1)
                dve.copy_predicated(band[j % 2][:, 2 * part:2 * part + 2, :],
                                    far_mask[:, :].unsqueeze(1).broadcast_to([P, 2, P]),
                                    bank[:, :, P:2 * P]).then_inc(s["band_ready"], 1)

            for i, at in enumerate((0, 2 * MAXP)):
                dve.tensor_scalar(rel_near[:, i * P:(i + 1) * P], w["rel_t"][:, 0:P], w["rel_t"][:, at:at + 1], None,
                                  ALU.subtract).then_inc(s["rel_ready"], 1)
                dve.tensor_tensor(k_bias[:, i:i + 1], w["k_b"][:, 0:1], w["rel_t"][:, at:at + 1],
                                  ALU.add).then_inc(s["rel_ready"], 1)
            norm_x(0)
            norm_s(0)
            dve.wait_ge(s["halved"], 3)
            dve.wait_ge(s["rel_ready"], 4)
            for full, (hi, lo) in ((w["q_w"], qw), (w["k_w"], kw), (rel_near, rel)):
                dve.tensor_tensor(lo[:, :], full[:, :], hi[:, :].bitcast(F32), ALU.subtract).then_inc(s["split"], 1)
            norm_out(0)
            turned_x_low(0)
            queries_low(0, 0, early[0])
            queries_low(1, 2, early[1])
            values(0, heads_ps)
            keys_low(0)
            queries_low(2, 4, early[2])
            queries_low(3, 6, early[3])
            for u in range(2):
                for part in range(2):
                    band_right(u, u, part, early_bands[2 * u + part])
            logits(0, out_ps)
            route_shares(dve, router, 0)

            def turned_right(u):
                dve.wait_ge(s["turned"], u + 1)
                dve.tensor_copy(probs_t[:, 1, :], turn_ps[:, 1, :]).then_inc(s["probs_t_right"], 1)

            def add_to_y(b):
                dve.wait_ge(s["out_done"], b + 1)
                dst = y_sb[:, bass.ds(b * SEQ, SEQ)]
                dve.tensor_tensor(dst, dst, out_ps[:, 0:SEQ], ALU.add).then_inc(s["y_ready"], 1)

            def batch(b):
                for j in range(STEPS):
                    u = b * STEPS + j
                    if j == 0 and not last(b):
                        norm_x(b + 1)
                    dve.wait_ge(s["scores_done"], u + 1)
                    dve.wait_ge(s["band_read"], (u + 1) * 16)
                    dve.sem_inc(s["waited"], 1)
                    for e in range(QUAD):
                        ins = dve.tensor_tensor_reduce(score_ps[:, e, :], score_ps[:, e, :], band_in[j][:, e, :], 1.0, LOWEST,
                                                       ALU.add, ALU.max, row_max[:, e:e + 1])
                    ins.then_inc(s["max_found"], 1)
                    dve.wait_ge(s["max_found"], u + 1)
                    dve.tensor_scalar(neg_max[:, :], row_max[:, :], -scale, None, ALU.mult).then_inc(s["neg_max_ready"], 1)
                    if j == 0:
                        dve.wait_ge(s["gates_turned"], b + 1)
                        dve.tensor_copy(gates_t[:, :], misc[0:EA, 0:SEQ]).then_inc(s["gates_t_ready"], 1)
                    if j == 2 and not last(b):
                        values(b + 1)
                    if j == 3 and not last(b):
                        queries_low(b * 4 + 6, 4)
                    if not (last(b) and j >= 2):
                        band_right(u + 2, j, 0)
                    if j == 1 and not last(b):
                        turned_x_low(b + 1)
                    if not (first(b) and j < 2):
                        turned_right(u - 2)
                    if j == 0 and not last(b):
                        norm_s(b + 1)
                    if j == 1 and not last(b):
                        queries_low(b * 4 + 4, 0)
                    if j == 2 and not last(b):
                        logits(b + 1)
                    if j == 3 and not last(b):
                        keys_low(b + 1)
                        queries_low(b * 4 + 7, 6)
                    if not (last(b) and j >= 2):
                        band_right(u + 2, j, 1)
                    dve.wait_ge(s["probs_ready"], u + 1)
                    dve.reciprocal(inv[:, :], sums[:, :]).then_inc(s["inv_ready"], 1)
                    dve.wait_ge(s["inv_ready"], u + 1)
                    dve.wait_ge(s["gates_kept"], b + 1)
                    eg, half = j // HALVES, j % HALVES
                    g = gates[:, bass.ds(b, 1), half, eg * QUAD:(eg + 1) * QUAD].rearrange("p a e -> p (a e)")
                    dve.tensor_tensor(factor[j % 2][:, :], inv[:, :], g, ALU.mult).then_inc(s["factor_ready"], 1)
                    if j == 0 and not last(b):
                        norm_out(b + 1)
                    if j == 1 and not last(b):
                        queries_low(b * 4 + 5, 2)
                    if j == 2 and not last(b):
                        route_shares(dve, router, b + 1)
                    if j == 2 and not first(b):
                        add_to_y(b - 1)

            over_batches(dve, batch)
            for u in range(BATCH * STEPS - 2, BATCH * STEPS):
                turned_right(u)
            add_to_y(BATCH - 1)

        @block.tensor
        def _(pe):
            pe.wait_ge(loaded, loads)

            def turn_x(b):
                pe.wait_ge(s["tn_ready"], b + 1)
                for h in range(HALVES):
                    mm = pe.transpose(misc[:, h * P:(h + 1) * P], tn[:, h, :], ident[:, :])
                mm.then_inc(s["tn_turned"], 1)

            def three(out, lhs, rhs, begin, end):
                pe.matmul(out, lhs[1], rhs[0], start=begin, stop=False)
                pe.matmul(out, lhs[0], rhs[1], start=False, stop=False)
                return pe.matmul(out, lhs[0], rhs[0], start=False, stop=end)

            def queries(n, e0, bank=misc):
                for i in range(2):
                    cols = slice((e0 + i) * HD, (e0 + i + 1) * HD)
                    mm = three(bank[:, i * SEQ:(i + 1) * SEQ], [t[:, cols] for t in qw], [xt_hi[:, :], xt_lo[:, :]], True, True)
                mm.then_inc(s["q_done"], 1)

            def values(b, bank=misc):
                for h in range(HALVES):
                    mm = pe.matmul(bank[:, h * HD:(h + 1) * HD], xt[:, h * P:(h + 1) * P], w["v_w"][:, :],
                                   start=True, stop=True)
                mm.then_inc(s["v_done"], 1)

            def keys_of(b, bank=misc):
                three(bank[:, 0:SEQ], [t[:, :] for t in kw], [xt_hi[:, :], xt_lo[:, :]], True, True).then_inc(s["keys_done"], 1)

            def logits(b, bank=misc):
                for h in range(HALVES):
                    mm = pe.matmul(bank[:, h * EA:(h + 1) * EA], xt[:, h * P:(h + 1) * P], w["gate_w"][:, :],
                                   start=True, stop=True)
                mm.then_inc(s["logits_done"], 1)

            def turn_gates(b):
                for h in range(HALVES):
                    mm = pe.transpose(misc[0:EA, h * P:(h + 1) * P], gates_now[:, h, :], ident[:, :])
                mm.then_inc(s["gates_turned"], 1)

            def near(u, j, part, bank=rel_ps):
                if not (isinstance(u, int) and u < 2):
                    pe.wait_ge(s["band_ready"], u * 2 + part)
                eg, half = j // HALVES, j % HALVES
                for i in range(2):
                    e = 2 * part + i
                    cols = slice(half * P, (half + 1) * P)
                    mm = three(bank[:, i, :], [q_hi[eg][:, e, cols], q_lo[eg][:, e, cols]], [rel[0][:, :], rel[1][:, :]],
                               True, True)
                mm.then_inc(s["rel_done"], 1)

            def scores(u, j):
                if not (isinstance(u, int) and u == 0):
                    pe.wait_ge(s["probs_ready"], u)
                eg, half = j // HALVES, j % HALVES
                for e in range(QUAD):
                    cols = slice(half * P, (half + 1) * P)
                    mm = three(score_ps[:, e, :], [q_hi[eg][:, e, cols], q_lo[eg][:, e, cols]],
                               [keys_hi[:, half, :], keys_lo[:, half, :]], True, True)
                mm.then_inc(s["scores_done"], 1)

            def turn_probs(u, parity):
                pe.wait_ge(s["weighted_ready"], u + 1)
                if not (isinstance(u, int) and u == 0):
                    pe.wait_ge(s["probs_t_left"], u)
                    pe.wait_ge(s["probs_t_right"], u)
                for h in range(HALVES):
                    for e in range(QUAD):
                        mm = pe.transpose(turn_ps[:, h, e * P:(e + 1) * P], weighted[parity][:, e, h * P:(h + 1) * P], ident[:, :])
                mm.then_inc(s["turned"], 1)

            def heads(u):
                pe.wait_ge(s["probs_t_left"], u + 1)
                pe.wait_ge(s["probs_t_right"], u + 1)
                if not (isinstance(u, int) and u == 0):
                    pe.wait_ge(s["heads_ready"], u)
                for h in range(HALVES):
                    mm = pe.matmul(heads_ps[:, :], v[:, h, :], probs_t[:, h, :], start=(h == 0), stop=(h == HALVES - 1))
                mm.then_inc(s["heads_done"], 1)

            def project(b, u, j):
                pe.wait_ge(s["heads_ready"], u + 1)
                eg, half = j // HALVES, j % HALVES
                if j == 0:
                    pe.wait_ge(s["gates_t_ready"], b + 1)
                    if not first(b):
                        pe.wait_ge(s["y_ready"], b)
                    for h in range(HALVES):
                        pe.matmul(out_ps[:, h * P:(h + 1) * P], gates_t[:, h * P:(h + 1) * P], w["o_b"][:, :],
                                  start=(h == 0), stop=False, skip_group_check=True)
                for e in range(QUAD):
                    n = eg * QUAD + e
                    mm = pe.matmul(out_ps[:, half * P:(half + 1) * P], heads_t[:, e * P:(e + 1) * P],
                                   w["o_w"][:, n * DIM:(n + 1) * DIM], start=False, stop=(eg == 1 and e == QUAD - 1),
                                   skip_group_check=True)
                if j == STEPS - 1:
                    mm.then_inc(s["out_done"], 1)

            turn_x(0)
            pe.wait_ge(s["split"], 3)
            pe.wait_ge(s["xt_lo_ready"], 1)
            queries(0, 0, early[0])
            queries(1, 2, early[1])
            values(0, heads_ps)
            keys_of(0)
            queries(2, 4, early[2])
            queries(3, 6, early[3])
            logits(0, out_ps)
            pe.wait_ge(s["q_ready"], 3)
            for u in range(2):
                for part in range(2):
                    if (u, part) == (1, 0):
                        pe.wait_ge(s["q_ready"], 4)
                    if (u, part) == (1, 1):
                        pe.wait_ge(s["band_ready"], 1)
                    near(u, u, part, early_bands[2 * u + part])

            def batch(b):
                for j in range(STEPS):
                    u = b * STEPS + j
                    if j == 0:
                        pe.wait_ge(s["keys_ready"], b + 1)
                    scores(u, j)
                    if not (last(b) and j >= 2):
                        near(u + 2, (j + 2) % STEPS, 0)
                    if j == 0:
                        pe.wait_ge(s["q_ready"], b * 4 + 4)
                        pe.wait_ge(s["gates_ready"], b + 1)
                        turn_gates(b)
                    if j == 1 and not last(b):
                        pe.wait_ge(s["gates_t_ready"], b + 1)
                        turn_x(b + 1)
                    if j == 2 and not last(b):
                        pe.wait_ge(s["q_ready"], b * 4 + 6)
                        values(b + 1)
                    if j == 3 and not last(b):
                        pe.wait_ge(s["keys_added"], b + 2)
                        queries(b * 4 + 6, 4)
                    if not (first(b) and j < 2):
                        turn_probs(u - 2, j % 2)
                    if not (first(b) and j < 3):
                        project(b if j == 3 else b - 1, u - 3, (j - 3) % STEPS)
                    if j == 1 and not last(b):
                        pe.wait_ge(s["xt_lo_ready"], b + 2)
                        queries(b * 4 + 4, 0)
                    if j == 2 and not last(b):
                        pe.wait_ge(s["v_next_ready"], b + 2)
                        logits(b + 1)
                    if j == 3 and not last(b):
                        pe.wait_ge(s["q_ready"], b * 4 + 7)
                        queries(b * 4 + 7, 6)
                    if not (last(b) and j >= 2):
                        near(u + 2, (j + 2) % STEPS, 1)
                    if not (first(b) and j < 2):
                        if j == 2:
                            pe.wait_ge(s["v_ready"], b + 1)
                        heads(u - 2)
                    if j == 1 and not last(b):
                        pe.wait_ge(s["q_ready"], b * 4 + 5)
                        queries(b * 4 + 5, 2)
                    if j == 2 and not last(b):
                        pe.wait_ge(router.logits_ready, b + 2)
                        keys_of(b + 1)

            over_batches(pe, batch)
            n = BATCH * STEPS
            project(BATCH - 1, n - 3, 1)
            turn_probs(n - 2, 0)
            heads(n - 2)
            project(BATCH - 1, n - 2, 2)
            turn_probs(n - 1, 1)
            heads(n - 1)
            project(BATCH - 1, n - 1, 3)



EF, FH = 16, 64
FF_CHUNKS = EF * FH // P
RUN = 4
RUNS = TILES // RUN
WIDE = RUN * P
LOW_ROWS = 32


def mixture_of_experts(nc, x_sb, y_sb, w, consts, loaded, loads):
    ident, half_pow, experts, select, low_mask = consts
    ctx = ExitStack()
    with ctx:
        def sb(name, shape, dt=F32):
            return ctx.enter_context(nc.sbuf_tensor(f"moe_{name}", shape, dt))

        def pb(name, shape):
            return ctx.enter_context(nc.psum_tensor(f"moe_{name}", shape, F32))

        semaphores = []

        def sem(name):
            semaphores.append(ctx.enter_context(nc.semaphore(f"moe_{name}")))
            return semaphores[-1]

        w1 = [sb("w1_hi", [P, EF * FH], F32R), sb("w1_lo", [P, EF * FH], F32R)]
        stats = sb("stats", [P, RUN, 6])
        moments = sb("moments", [P, RUN, 2])
        var_eps = sb("var_eps", [P, RUN])
        rstd = sb("rstd", [P, RUN])
        tn = sb("tn", [P, RUN, DIM])
        xt = sb("xt", [P, WIDE])
        xt_hi = sb("xt_hi", [P, WIDE], F32R)
        xt_lo = sb("xt_lo", [P, WIDE], F32R)
        router = Router(lambda n, s, d=F32: sb("r_" + n, s, d), lambda n: sem("r_" + n), RUN, EF, experts)
        gates = sb("gates", [P, RUN, LOW_ROWS + EF])
        gates_hi = sb("gates_hi", [LOW_ROWS + EF, WIDE], F32R)
        gates_t = sb("gates_t", [P, WIDE], F32R)
        sel = sb("sel", [P, FF_CHUNKS * P], F32R)
        active = [sb(f"active{i}", [P, WIDE]) for i in range(2)]
        scaled = [sb(f"scaled{i}", [P, WIDE]) for i in range(2)]
        total = sb("total", [P, WIDE])

        hidden_ps = [pb(f"hidden_ps{i}", [P, WIDE]) for i in range(2)]
        gate_ps = [pb(f"gate_ps{i}", [P, WIDE]) for i in range(2)]
        out_ps = pb("out_ps", [P, WIDE])
        misc = pb("misc", [P, WIDE])

        names = """waited cleared halved split stats_ready var_ready eps_added rstd_ready tn_ready tn_turned xt_ready
            xt_hi_ready xt_lo_ready logits_done gates_ready gates_copied gates_turned gates_hi_ready gates_t_ready
            hidden_done spread_done active_ready scaled_ready out_done total_ready x_ready""".split()
        s = {n: sem(n) for n in names}
        C = FF_CHUNKS

        def first(n):
            return isinstance(n, int) and n == 0

        def last(n):
            return isinstance(n, int) and n == RUNS - 1

        def over_runs(eng, body):
            body(0)
            with eng.Fori(1, RUNS - 1) as n:
                body(n)
            body(RUNS - 1)

        def tile(t, n, i):
            return t[:, bass.ds((n * RUN + i) * DIM, DIM)]

        cleared_at_exit(nc, ctx, semaphores)
        block = ctx.enter_context(nc.Block())

        @block.gpsimd
        def _(pool):
            pool.memset(gates_t[:, :].bitcast(F32), 0.0).then_inc(s["cleared"], 1)
            pool.memset(gates[:, :, :], 0.0).then_inc(s["cleared"], 1)

            def deviations(n):
                pool.wait_ge(s["var_ready"], n + 1)
                pool.sem_inc(s["waited"], 1)
                pool.tensor_scalar(var_eps[:, :], moments[:, :, 1], EPS, None, ALU.add).then_inc(s["eps_added"], 1)
                pool.wait_ge(s["eps_added"], n + 1)
                pool.tensor_tensor(rstd[:, :], var_eps[:, :], half_pow[:, 0:RUN], ALU.pow).then_inc(s["rstd_ready"], 1)

            deviations(0)
            with pool.Fori(1, RUNS) as n:
                deviations(n)

        @block.scalar
        def _(act):
            act.wait_ge(loaded, loads)
            act.activation(w1[0][:, :], w["ff_w1"][:, :], ACT.Copy).then_inc(s["halved"], 1)

            def turned_y(n):
                act.wait_ge(s["tn_turned"], n + 1)
                act.activation(xt[:, :], misc[:, :], ACT.Identity, bias=w["ln2_b"][:, 0:1],
                               scale=w["ln2_w"][:, 0:1]).then_inc(s["xt_ready"], 1)

            def high_halves(n):
                act.wait_ge(s["xt_ready"], n + 1)
                if not first(n):
                    act.wait_ge(s["hidden_done"], n * C)
                act.activation(xt_hi[:, :], xt[:, :], ACT.Copy).then_inc(s["xt_hi_ready"], 1)
                act.wait_ge(s["gates_turned"], n + 1)
                act.activation(gates_hi[:, :], misc[0:LOW_ROWS + EF, :], ACT.Copy).then_inc(s["gates_hi_ready"], 1)

            def gap(n):
                act.wait_ge(router.gap_ready, n + 1)
                act.activation(router.gap_exp[:, :], router.gap[:, :], ACT.Exp).then_inc(router.gap_exp_ready, 1)

            turned_y(0)
            act.activation(sel[:, :], select[:, :], ACT.Copy).then_inc(s["halved"], 1)
            gap(0)
            high_halves(0)

            def run(n):
                for c in range(C):
                    u = n * C + c
                    act.wait_ge(s["hidden_done"], u + 1)
                    if not (first(n) and c < 2):
                        act.wait_ge(s["scaled_ready"], u - 1)
                    act.activation(active[c % 2][:, :], hidden_ps[c % 2][:, :], ACT.Relu,
                                   bias=w["ff_b1"][:, c:c + 1]).then_inc(s["active_ready"], 1)
                    if not last(n):
                        if c == 2:
                            turned_y(n + 1)
                        if c == 3:
                            gap(n + 1)
                        if c == C - 1:
                            high_halves(n + 1)

            over_runs(act, run)

        @block.vector
        def _(dve):
            def norm_y(n):
                for i in range(RUN):
                    ins = dve.bn_stats(stats[:, i, :], tile(y_sb, n, i))
                ins.then_inc(s["stats_ready"], 1)
                dve.wait_ge(s["stats_ready"], n + 1)
                dve.sem_inc(s["waited"], 1)
                for i in range(RUN):
                    ins = dve.bn_aggr(moments[:, i, :], stats[:, i, :])
                ins.then_inc(s["var_ready"], 1)

            def norm_out(n):
                dve.wait_ge(s["rstd_ready"], n + 1)
                dve.wait_ge(s["var_ready"], n + 1)
                for i in range(RUN):
                    ins = dve.tensor_scalar(tn[:, i, :], tile(y_sb, n, i), moments[:, i, 0:1], rstd[:, i:i + 1],
                                            ALU.subtract, ALU.mult)
                ins.then_inc(s["tn_ready"], 1)

            def low_halves(n):
                dve.wait_ge(s["xt_hi_ready"], n + 1)
                dve.tensor_tensor(xt_lo[:, :], xt[:, :], xt_hi[:, :].bitcast(F32), ALU.subtract).then_inc(s["xt_lo_ready"], 1)
                dve.wait_ge(s["gates_hi_ready"], n + 1)
                if not first(n):
                    dve.wait_ge(s["spread_done"], n * C)
                rows = slice(0, LOW_ROWS + EF)
                dve.scalar_tensor_tensor(out=gates_t[rows, :], in0=gates_hi[:, :].bitcast(F32), scalar=low_mask[rows, 0:1],
                                         in1=misc[rows, :], op0=ALU.mult, op1=ALU.add).then_inc(s["gates_t_ready"], 1)

            def logits(n):
                dve.wait_ge(s["logits_done"], n + 1)
                route_logits(dve, router, n, RUN, misc[:, 0:RUN * EF].rearrange("p (h e) -> p h e", h=RUN), None, None)

            def gates_of(n):
                route_shares(dve, router, n)
                route_gates(dve, router, n, RUN, gates[:, :, 0:EF]).then_inc(s["gates_ready"], 1)
                dve.wait_ge(s["gates_ready"], n + 1)
                dve.tensor_copy(gates[:, :, LOW_ROWS:LOW_ROWS + EF], gates[:, :, 0:EF]).then_inc(s["gates_copied"], 1)

            def add_to_x(n):
                dve.wait_ge(s["out_done"], (n + 1) * C)
                dve.tensor_tensor(total[:, :], y_sb[:, bass.ds(n * WIDE, WIDE)], out_ps[:, :], ALU.add).then_inc(s["total_ready"], 1)
                dve.wait_ge(s["total_ready"], n + 1)
                dst = x_sb[:, bass.ds(n * WIDE, WIDE)]
                dve.tensor_tensor(dst, dst, total[:, :], ALU.add).then_inc(s["x_ready"], 1)

            norm_y(0)
            norm_out(0)
            dve.wait_ge(s["halved"], 1)
            dve.tensor_tensor(w1[1][:, :], w["ff_w1"][:, :], w1[0][:, :].bitcast(F32), ALU.subtract).then_inc(s["split"], 1)
            dve.wait_ge(s["cleared"], 2)
            logits(0)
            gates_of(0)
            low_halves(0)

            def run(n):
                for c in range(C):
                    u = n * C + c
                    dve.wait_ge(s["active_ready"], u + 1)
                    dve.wait_ge(s["spread_done"], u + 1)
                    if not (first(n) and c < 2):
                        dve.wait_ge(s["out_done"], u - 1)
                    dve.tensor_tensor(scaled[c % 2][:, :], active[c % 2][:, :], gate_ps[c % 2][:, :],
                                      ALU.mult).then_inc(s["scaled_ready"], 1)
                    if c == 0 and not first(n):
                        add_to_x(n - 1)
                    if not last(n):
                        if c == 0:
                            norm_y(n + 1)
                        if c == 1:
                            norm_out(n + 1)
                        if c == 3:
                            logits(n + 1)
                        if c == 4:
                            gates_of(n + 1)
                        if c == C - 1:
                            low_halves(n + 1)

            over_runs(dve, run)
            add_to_x(RUNS - 1)

        @block.tensor
        def _(pe):
            pe.wait_ge(loaded, loads)

            def turn_y(n):
                pe.wait_ge(s["tn_ready"], n + 1)
                if not first(n):
                    pe.wait_ge(s["gates_t_ready"], n)
                for i in range(RUN):
                    mm = pe.transpose(misc[:, i * P:(i + 1) * P], tn[:, i, :], ident[:, :])
                mm.then_inc(s["tn_turned"], 1)

            def logits(n):
                pe.wait_ge(s["xt_ready"], n + 1)
                for i in range(RUN):
                    mm = pe.matmul(misc[:, i * EF:(i + 1) * EF], xt[:, i * P:(i + 1) * P], w["ff_gate_w"][:, :],
                                   start=True, stop=True)
                mm.then_inc(s["logits_done"], 1)

            def turn_gates(n):
                pe.wait_ge(s["gates_copied"], n + 1)
                pe.sem_inc(s["waited"], 1)
                for i in range(RUN):
                    mm = pe.transpose(misc[0:LOW_ROWS + EF, i * P:(i + 1) * P], gates[:, i, :], ident[:, :])
                mm.then_inc(s["gates_turned"], 1)

            def hidden(n, c):
                u = n * C + c
                if c == 0:
                    pe.wait_ge(s["xt_lo_ready"], n + 1)
                    pe.wait_ge(s["gates_t_ready"], n + 1)
                if not (first(n) and c < 2):
                    pe.wait_ge(s["active_ready"], u - 1)
                    pe.wait_ge(s["scaled_ready"], u - 1)
                cols = slice(c * P, (c + 1) * P)
                out = hidden_ps[c % 2][:, :]
                pe.matmul(out, w1[1][:, cols], xt_hi[:, :], start=True, stop=False)
                pe.matmul(out, w1[0][:, cols], xt_lo[:, :], start=False, stop=False)
                pe.matmul(out, w1[0][:, cols], xt_hi[:, :], start=False, stop=True).then_inc(s["hidden_done"], 1)
                pe.matmul(gate_ps[c % 2][:, :], sel[:, cols], gates_t[:, :], start=True, stop=True).then_inc(s["spread_done"], 1)

            def out(n, c):
                u = n * C + c
                if c == 0:
                    if not first(n):
                        pe.wait_ge(s["total_ready"], n)
                    for i in range(RUN):
                        pe.matmul(out_ps[:, i * P:(i + 1) * P], gates_t[:, i * P:(i + 1) * P].bitcast(F32), w["ff_b2"][:, :],
                                  start=(i == 0), stop=False, skip_group_check=True)
                pe.wait_ge(s["scaled_ready"], u + 1)
                for i in range(RUN):
                    mm = pe.matmul(out_ps[:, i * P:(i + 1) * P], scaled[c % 2][:, i * P:(i + 1) * P],
                                   w["ff_w2"][:, c * DIM:(c + 1) * DIM], start=False, stop=(c == C - 1), skip_group_check=True)
                mm.then_inc(s["out_done"], 1)
                return mm

            turn_y(0)
            logits(0)
            turn_gates(0)
            pe.wait_ge(s["halved"], 2)
            pe.wait_ge(s["split"], 1)

            def run(n):
                for c in range(C):
                    hidden(n, c)
                    if c > 0:
                        out(n, c - 1)
                    if not last(n):
                        if c == 2:
                            turn_y(n + 1)
                        if c == 3:
                            logits(n + 1)
                        if c == 6:
                            turn_gates(n + 1)
                out(n, C - 1)

            over_runs(pe, run)


EX, FX = 8, 344
PARTS = -(-FX // P)


def gated_experts(nc, x_sb, out_dram, w, consts, loaded, loads):
    ident, half_pow, experts = consts
    ctx = ExitStack()
    with ctx:
        def sb(name, shape, dt=F32):
            return ctx.enter_context(nc.sbuf_tensor(f"ffn_{name}", shape, dt))

        def pb(name, shape):
            return ctx.enter_context(nc.psum_tensor(f"ffn_{name}", shape, F32))

        semaphores = []

        def sem(name):
            semaphores.append(ctx.enter_context(nc.semaphore(f"ffn_{name}")))
            return semaphores[-1]

        C = EX * PARTS
        wg = [sb("wg_hi", [P, C * P], F32R), sb("wg_lo", [P, C * P], F32R)]
        wu = [sb("wu_hi", [P, C * P], F32R), sb("wu_lo", [P, C * P], F32R)]
        stats = sb("stats", [P, RUN, 6])
        moments = sb("moments", [P, RUN, 2])
        var_eps = sb("var_eps", [P, RUN])
        rstd = sb("rstd", [P, RUN])
        tn = sb("tn", [P, RUN, DIM])
        xt = sb("xt", [P, WIDE])
        xt_hi = sb("xt_hi", [P, WIDE], F32R)
        xt_lo = sb("xt_lo", [P, WIDE], F32R)
        router = Router(lambda n, s, d=F32: sb("r_" + n, s, d), lambda n: sem("r_" + n), RUN, EX, experts)
        euler = sb("euler", [P, RUN])
        gates_next = sb("gates_next", [P, RUN, EX])
        gates = sb("gates", [P, RUN, EX])
        gated = [sb(f"gated{i}", [P, WIDE]) for i in range(2)]
        hidden = [sb(f"hidden{i}", [P, WIDE]) for i in range(2)]

        gate_ps = [pb(f"gate_ps{i}", [P, WIDE]) for i in range(2)]
        up_ps = [pb(f"up_ps{i}", [P, WIDE]) for i in range(2)]
        down_ps = [pb(f"down_ps{i}", [P, WIDE]) for i in range(2)]
        misc = pb("misc", [P, WIDE])

        names = """waited cleared halved split stats_ready var_ready eps_added rstd_ready tn_ready tn_turned xt_ready
            xt_hi_ready xt_lo_ready logits_done gates_next_ready gates_ready
            gate_done up_done gated_ready hidden_ready down_done x_ready stored""".split()
        s = {n: sem(n) for n in names}

        def first(n):
            return isinstance(n, int) and n == 0

        def last(n):
            return isinstance(n, int) and n == RUNS - 1

        def over_runs(eng, body):
            body(0)
            with eng.Fori(1, RUNS - 1) as n:
                body(n)
            body(RUNS - 1)

        def tile(t, n, i):
            return t[:, bass.ds((n * RUN + i) * DIM, DIM)]

        cleared_at_exit(nc, ctx, semaphores)
        block = ctx.enter_context(nc.Block())

        @block.sync
        def _(sp):
            def store(n):
                sp.wait_ge(s["x_ready"], (n + 1) * EX)
                sp.dma_start(out_dram[:, bass.ds(n * RUN, RUN), :],
                             x_sb[:, bass.ds(n * WIDE, WIDE)].rearrange("p (t c) -> p t c", c=DIM)).then_inc(s["stored"], 16)

            store(0)
            with sp.Fori(1, RUNS) as n:
                store(n)
            sp.wait_ge(s["stored"], RUNS * 16)

        @block.gpsimd
        def _(pool):
            def deviations(n):
                pool.wait_ge(s["var_ready"], n + 1)
                pool.sem_inc(s["waited"], 1)
                pool.tensor_scalar(var_eps[:, :], moments[:, :, 1], EPS, None, ALU.add).then_inc(s["eps_added"], 1)
                pool.wait_ge(s["eps_added"], n + 1)
                pool.tensor_tensor(rstd[:, :], var_eps[:, :], half_pow[:, 0:RUN], ALU.pow).then_inc(s["rstd_ready"], 1)

            def gap_exp(n):
                pool.wait_ge(router.gap_ready, n + 1)
                pool.tensor_tensor(router.gap_exp[:, :], euler[:, :], router.gap[:, :],
                                   ALU.pow).then_inc(router.gap_exp_ready, 1)

            pool.memset(euler[:, :], math.e).then_inc(s["cleared"], 1)
            pool.wait_ge(s["cleared"], 1)
            deviations(0)
            gap_exp(0)
            with pool.Fori(1, RUNS) as n:
                deviations(n)
                gap_exp(n)

        @block.scalar
        def _(act):
            act.wait_ge(loaded, loads)

            def turned_x(n):
                act.wait_ge(s["tn_turned"], n + 1)
                act.activation(xt[:, :], misc[:, :], ACT.Copy).then_inc(s["xt_ready"], 1)

            def high_half(n):
                act.wait_ge(s["xt_ready"], n + 1)
                if not first(n):
                    act.wait_ge(s["up_done"], n * C)
                act.activation(xt_hi[:, :], xt[:, :], ACT.Copy).then_inc(s["xt_hi_ready"], 1)

            for e in range(EX):
                cols = slice(e * PARTS * P, (e + 1) * PARTS * P)
                act.activation(wg[0][:, cols], w["Wg"][:, cols], ACT.Copy).then_inc(s["halved"], 1)
                act.activation(wu[0][:, cols], w["Wu"][:, cols], ACT.Copy).then_inc(s["halved"], 1)
                if e == 0:
                    turned_x(0)
                    high_half(0)

            def run(n):
                for c in range(C):
                    u = n * C + c
                    act.wait_ge(s["gate_done"], u + 1)
                    if not (first(n) and c < 2):
                        act.wait_ge(s["hidden_ready"], u - 1)
                    act.activation(gated[c % 2][:, :], gate_ps[c % 2][:, :], ACT.Silu).then_inc(s["gated_ready"], 1)
                    if not last(n):
                        if c == 4:
                            turned_x(n + 1)
                        if c == C - 1:
                            high_half(n + 1)

            over_runs(act, run)

        @block.vector
        def _(dve):
            def norm_x(n):
                for i in range(RUN):
                    ins = dve.bn_stats(stats[:, i, :], tile(x_sb, n, i))
                ins.then_inc(s["stats_ready"], 1)
                dve.wait_ge(s["stats_ready"], n + 1)
                dve.sem_inc(s["waited"], 1)
                for i in range(RUN):
                    ins = dve.bn_aggr(moments[:, i, :], stats[:, i, :])
                ins.then_inc(s["var_ready"], 1)

            def norm_out(n):
                dve.wait_ge(s["rstd_ready"], n + 1)
                dve.wait_ge(s["var_ready"], n + 1)
                for i in range(RUN):
                    ins = dve.tensor_scalar(tn[:, i, :], tile(x_sb, n, i), moments[:, i, 0:1], rstd[:, i:i + 1],
                                            ALU.subtract, ALU.mult)
                ins.then_inc(s["tn_ready"], 1)

            def low_half(n):
                dve.wait_ge(s["xt_hi_ready"], n + 1)
                dve.tensor_tensor(xt_lo[:, :], xt[:, :], xt_hi[:, :].bitcast(F32), ALU.subtract).then_inc(s["xt_lo_ready"], 1)

            def logits(n):
                dve.wait_ge(s["logits_done"], n + 1)
                route_logits(dve, router, n, RUN, misc[:, 0:RUN * EX].rearrange("p (h e) -> p h e", h=RUN),
                             w["bs"][:, :].unsqueeze(1).broadcast_to([P, RUN, EX]), None)

            def gates_of(n):
                route_shares(dve, router, n)
                route_gates(dve, router, n, RUN, gates_next[:, :, :]).then_inc(s["gates_next_ready"], 1)

            def take_gates(n):
                dve.wait_ge(s["gates_next_ready"], n + 1)
                if not first(n):
                    dve.wait_ge(s["x_ready"], n * EX)
                dve.tensor_copy(gates[:, :, :], gates_next[:, :, :]).then_inc(s["gates_ready"], 1)

            def low_weights(e):
                cols = slice(e * PARTS * P, (e + 1) * PARTS * P)
                dve.wait_ge(s["halved"], 2 * e + 2)
                for t, name in ((wg, "Wg"), (wu, "Wu")):
                    ins = dve.tensor_tensor(t[1][:, cols], w[name][:, cols], t[0][:, cols].bitcast(F32), ALU.subtract)
                ins.then_inc(s["split"], 1)

            def combine(n, e):
                dve.wait_ge(s["down_done"], (n * EX + e + 1) * PARTS)
                if not (first(n) and e == 0):
                    dve.wait_ge(s["x_ready"], n * EX + e)
                if e == 0:
                    dve.wait_ge(s["gates_ready"], n + 1)
                for i in range(RUN):
                    dst = tile(x_sb, n, i)
                    ins = dve.scalar_tensor_tensor(out=dst, in0=down_ps[e % 2][:, i * DIM:(i + 1) * DIM],
                                                   scalar=gates[:, i, e:e + 1], in1=dst, op0=ALU.mult, op1=ALU.add)
                ins.then_inc(s["x_ready"], 1)

            norm_x(0)
            norm_out(0)
            low_weights(0)
            low_half(0)
            logits(0)
            def run(n):
                for c in range(C):
                    u = n * C + c
                    e, part = c // PARTS, c % PARTS
                    if first(n) and part == 0 and e + 1 < EX:
                        low_weights(e + 1)
                    dve.wait_ge(s["gated_ready"], u + 1)
                    dve.wait_ge(s["up_done"], u + 1)
                    if not (first(n) and c < 2):
                        dve.wait_ge(s["down_done"], u - 1)
                    dve.tensor_tensor(hidden[c % 2][:, :], gated[c % 2][:, :], up_ps[c % 2][:, :],
                                      ALU.mult).then_inc(s["hidden_ready"], 1)
                    if first(n) and c == 1:
                        gates_of(0)
                        take_gates(0)
                    if part == 1 and e > 0:
                        combine(n, e - 1)
                    if c == 1 and not first(n):
                        combine(n - 1, EX - 1)
                        take_gates(n)
                    if not last(n):
                        if c == 2:
                            norm_x(n + 1)
                        if c == 3:
                            norm_out(n + 1)
                        if c == 5:
                            logits(n + 1)
                        if c == 8:
                            gates_of(n + 1)
                        if c == C - 1:
                            low_half(n + 1)

            over_runs(dve, run)
            combine(RUNS - 1, EX - 1)

        @block.tensor
        def _(pe):
            pe.wait_ge(loaded, loads)

            def turn_x(n):
                pe.wait_ge(s["tn_ready"], n + 1)
                if not first(n):
                    pe.wait_ge(router.logits_ready, n)
                for i in range(RUN):
                    mm = pe.transpose(misc[:, i * P:(i + 1) * P], tn[:, i, :], ident[:, :])
                mm.then_inc(s["tn_turned"], 1)

            def logits(n):
                pe.wait_ge(s["xt_ready"], n + 1)
                for i in range(RUN):
                    mm = pe.matmul(misc[:, i * EX:(i + 1) * EX], xt[:, i * P:(i + 1) * P], w["Ws"][:, :],
                                   start=True, stop=True)
                mm.then_inc(s["logits_done"], 1)

            def gate_up(n, c):
                u = n * C + c
                cols = slice(c * P, (c + 1) * P)
                if c == 0:
                    pe.wait_ge(s["xt_lo_ready"], n + 1)
                if first(n) and c % PARTS == 0:
                    pe.wait_ge(s["split"], c // PARTS + 1)
                if not (first(n) and c < 2):
                    pe.wait_ge(s["gated_ready"], u - 1)
                    pe.wait_ge(s["hidden_ready"], u - 1)
                for t, ps, done in ((wg, gate_ps, "gate_done"), (wu, up_ps, "up_done")):
                    out = ps[c % 2][:, :]
                    pe.matmul(out, t[1][:, cols], xt_hi[:, :], start=True, stop=False)
                    pe.matmul(out, t[0][:, cols], xt_lo[:, :], start=False, stop=False)
                    pe.matmul(out, t[0][:, cols], xt_hi[:, :], start=False, stop=True).then_inc(s[done], 1)

            def down(n, c):
                u = n * C + c
                e, part = c // PARTS, c % PARTS
                if part == 0 and not (first(n) and e < 2):
                    pe.wait_ge(s["x_ready"], n * EX + e - 1)
                pe.wait_ge(s["hidden_ready"], u + 1)
                for i in range(RUN):
                    mm = pe.matmul(down_ps[e % 2][:, i * P:(i + 1) * P], hidden[c % 2][:, i * P:(i + 1) * P],
                                   w["Wd"][:, c * DIM:(c + 1) * DIM], start=(part == 0 and i == 0), stop=(part == PARTS - 1),
                                   skip_group_check=True)
                mm.then_inc(s["down_done"], 1)
                return mm

            turn_x(0)
            logits(0)

            def run(n):
                for c in range(C):
                    gate_up(n, c)
                    if c > 0:
                        down(n, c - 1)
                    if not last(n):
                        if c == 4:
                            turn_x(n + 1)
                        if c == 5:
                            logits(n + 1)
                down(n, C - 1)

            over_runs(pe, run)



def _alibi_slopes():
    return np.power(np.float32(2.0), (np.float32(-8.0) * np.arange(1, HEADS + 1, dtype=np.float32)) / np.float32(HEADS))


def _masks(window):
    token = np.arange(SEQ)
    back = token[:, None] - token[None, :]
    seen = (back >= 0) & (back <= window)
    rows = np.where(seen, 0.0, MASKED).astype(np.float32).reshape(HALVES, P, SEQ).transpose(1, 0, 2)
    cols = np.where(seen, 0.0, MASKED).astype(np.float32).T[0:P, :]
    return rows.reshape(P, HALVES * SEQ), cols


def _stack_columns(w):
    out = np.zeros((DIM, HEADS, STRIP), w.dtype)
    for at in (ROW_A, ROW_B, ROW_C):
        out[:, :, at:at + HEAD_DIM] = w.reshape(DIM, HEADS, HEAD_DIM)
    return out.reshape(DIM, HEADS * STRIP)


def _row_masks():
    m = np.zeros((GROUP, STRIP, 2 + GROUP), np.float32)
    m[:, [ROW_SLOPE_LO, ROW_MAX_LO], 0] = -1.0
    m[:, ROW_C:ROW_C + HEAD_DIM, 0] = -1.0
    m[:, ROW_B:ROW_B + HEAD_DIM, 1] = -1.0
    m[range(GROUP), :, range(2, 2 + GROUP)] = 1.0
    return m.reshape(P, 2 + GROUP)


def _constant_rows(alibi, q_bias=None, k_bias=None):
    q = np.zeros((2, HEADS, STRIP), np.float32)
    k = np.zeros((2, HEADS, STRIP), np.float32)
    k[0, :, [ROW_MAX_HI, ROW_MAX_LO]] = 1.0
    if alibi:
        q[0, :, [ROW_SLOPE_HI, ROW_SLOPE_LO]] = _alibi_slopes()
        k[1, :, [ROW_SLOPE_HI, ROW_SLOPE_LO]] = 1.0
    if q_bias is not None:
        for at in (ROW_A, ROW_B, ROW_C):
            q[0, :, at:at + HEAD_DIM] = q_bias.reshape(HEADS, HEAD_DIM)
            k[0, :, at:at + HEAD_DIM] = k_bias.reshape(HEADS, HEAD_DIM)
    return np.concatenate([q.reshape(2, -1), k.reshape(2, -1)], axis=1)


def _ramp():
    m = np.zeros((P, SEQ), np.float32)
    m[0] = m[32] = 1.0
    m[64] = np.arange(SEQ)
    return m


def _far_mask():
    at = np.arange(P)
    return (at[:, None] + at[None, :] >= P).astype(np.float32)


def _select():
    m = np.zeros((P, FF_CHUNKS * P), np.float32)
    col = np.arange(FF_CHUNKS * P)
    m[col // FH, col] = 1.0
    m[LOW_ROWS + col // FH, col] = 1.0
    return m


def _low_mask():
    m = np.zeros((P, 1), np.float32)
    m[LOW_ROWS:] = -1.0
    return m


def _twice(b2):
    m = np.zeros((P, DIM), b2.dtype)
    m[0:EF] = m[LOW_ROWS:LOW_ROWS + EF] = b2
    return m


def _up_columns(w):
    out = np.zeros((DIM, EX, PARTS * P), w.dtype)
    out[:, :, 0:FX] = w.transpose(1, 0, 2)
    return out.reshape(DIM, EX * PARTS * P)


def _down_rows(w):
    out = np.zeros((EX, PARTS * P, DIM), w.dtype)
    out[:, 0:FX] = w
    return np.ascontiguousarray(out.reshape(EX * PARTS, P, DIM).transpose(1, 0, 2)).reshape(P, EX * PARTS * DIM)


CONSTANTS = 8


def two_layers(nc, d, out):
    scratch = [nc.dram_tensor(f"band_scratch{i}", [QUAD, SLAB], F32).ap() for i in range(STEPS)]
    out_tiles = out.rearrange("b (h p) c -> p (b h) c", p=P)
    with ExitStack() as ctx:
        def sb(name, shape, dt=F32):
            return ctx.enter_context(nc.sbuf_tensor(name, shape, dt))

        def sem(name):
            return ctx.enter_context(nc.semaphore(name))

        def loaded_tile(name):
            return sb("w_" + name, list(d[name].shape))

        x_sb = sb("x_sb", [P, TILES * DIM])
        y_sb = sb("y_sb", [P, TILES * DIM])
        ident = sb("ident", [P, P])
        ident_bf = sb("ident_bf", [P, P], BF16)
        half_pow = sb("half_pow", [P, RUN])
        row_masks = sb("row_masks", [P, 2 + GROUP])
        ramp = sb("ramp", [P, SEQ], F32R)
        layers = ("a0", "a1")
        mask_rows = {n: sb(f"{n}_mask_rows", [P, HALVES, SEQ]) for n in layers}
        mask_cols = {n: sb(f"{n}_mask_cols", [P, SEQ], BF16) for n in layers}
        stacks = {n: [loaded_tile(f"{n}_{k}") for k in ("wq", "wk", "wv", "wo")] for n in layers}
        const_rows = {n: sb(f"{n}_const_rows", [P, 2 * HEADS * STRIP]) for n in layers}
        a1_bias = loaded_tile("a1_bias")
        head_names = ("ln1_w", "ln1_b", "gate_w", "q_w", "q_b", "k_w", "k_b", "v_w", "v_b", "o_w", "o_b", "rel_t")
        expert_names = ("ln2_w", "ln2_b", "ff_gate_w", "ff_w1", "ff_b1", "ff_w2", "ff_b2", "select", "low_mask", "experts")
        w = {n: loaded_tile(n) for n in head_names + expert_names}

        far_mask = sb("far_mask", [P, P], U8)

        first_loaded = sem("first_loaded")
        x_loaded = sem("x_loaded")
        later_loaded = sem("later_loaded")
        last_loaded = sem("last_loaded")
        zeros_set = sem("zeros_set")
        scratch_zeroed = sem("scratch_zeroed")
        constants = sem("constants")
        first_batches = 2

        with ExitStack() as prep:
            pack = prep.enter_context(nc.sbuf_tensor("pack", [P, d["pack"].shape[1]], F32))
            cut = np.cumsum([0, P, 2 + GROUP, SEQ, P, SEQ, SEQ])
            ident_in, masks_in, ramp_in, far_in, cols0_in, cols1_in = (pack[:, a:b] for a, b in zip(cut, cut[1:]))

            def load_attention(eng, n, done):
                for dst, k in zip(stacks[n], ("wq", "wk", "wv", "wo")):
                    eng.dma_start(dst[:, :], d[f"{n}_{k}"]).then_inc(done, 16)
                for at, row in ((0, 0), (32, 0), (64, 1)):
                    eng.dma_start(const_rows[n][at:at + 1, :], d[f"{n}_const_rows"][row:row + 1, :]).then_inc(done, 16)
                eng.dma_start(mask_rows[n][:, :, :], d[f"{n}_mask_rows"].rearrange("p (h k) -> p h k", h=HALVES)).then_inc(done, 16)

            with nc.Block() as block:
                @block.sync
                def _(sp):
                    def load_x(lo, hi, done):
                        sp.dma_start(x_sb[:, lo * SEQ:hi * SEQ].rearrange("p (t c) -> p t c", c=DIM),
                                     d["x"][lo:hi].rearrange("b (h p) c -> p (b h) c", p=P)).then_inc(done, 16)

                    load_x(0, first_batches, first_loaded)
                    sp.dma_start(pack[:, :], d["pack"]).then_inc(first_loaded, 16)
                    load_x(first_batches, BATCH, x_loaded)
                    load_attention(sp, "a1", later_loaded)
                    sp.dma_start(a1_bias[:, :], d["a1_bias"]).then_inc(later_loaded, 16)
                    for n in head_names + expert_names:
                        sp.dma_start(w[n][:, :], d[n]).then_inc(later_loaded, 16)

                @block.scalar
                def _(act):
                    load_attention(act, "a0", first_loaded)

                @block.gpsimd
                def _(pool):
                    pool.memset(half_pow[:, :], -0.5).then_inc(constants, 1)
                    pool.memset(y_sb[:, 0:QUAD * SLAB // P], 0.0).then_inc(zeros_set, 1)
                    pool.wait_ge(zeros_set, 1)
                    for t in scratch:
                        pool.dma_start(t.rearrange("e s -> (e s)").rearrange("(p s) -> p s", p=P),
                                       y_sb[:, 0:QUAD * SLAB // P]).then_inc(scratch_zeroed, 16)

                @block.vector
                def _(dve):
                    dve.wait_ge(first_loaded, 16 * (2 + 8))
                    for dst, src in ((ident, ident_in), (ident_bf, ident_in), (row_masks, masks_in), (ramp, ramp_in),
                                     (far_mask, far_in), (mask_cols["a0"], cols0_in), (mask_cols["a1"], cols1_in)):
                        dve.tensor_copy(dst[:, :], src).then_inc(constants, 1)
                    dve.wait_ge(constants, CONSTANTS)

        def attention_phase(name, bias):
            attention(nc, Attention(name, name == "a0"), x_sb, stacks[name] + [const_rows[name], bias],
                      (ident, ident_bf, mask_rows[name], mask_cols[name], row_masks, ramp, half_pow[:, 0:HALVES]), constants, CONSTANTS,
                      (x_loaded, 16) if name == "a0" else None)

        attention_phase("a0", None)
        mixture_of_heads(nc, x_sb, y_sb, w, (ident, half_pow[:, 0:HALVES], w["experts"][:, 0:EA], far_mask),
                         scratch, scratch_zeroed, later_loaded, 16 * (9 + len(w)))
        mixture_of_experts(nc, x_sb, y_sb, w, (ident, half_pow, w["experts"], w["select"], w["low_mask"]),
                           later_loaded, 16 * (9 + len(w)))
        last_names = ("Ws", "bs", "Wg", "Wu", "Wd")
        w_last = {n: loaded_tile(n) for n in last_names}
        with nc.Block() as block:
            @block.sync
            def _(sp):
                for n in last_names:
                    sp.dma_start(w_last[n][:, :], d[n]).then_inc(last_loaded, 16)

        attention_phase("a1", a1_bias)
        gated_experts(nc, x_sb, out_tiles, w_last, (ident, half_pow, w["experts"][:, 0:EX]), last_loaded, 16 * len(w_last))



def _laid_out(i):
    rows_of = lambda a: np.ascontiguousarray(np.broadcast_to(a[None], (P,) + a.shape))
    column = lambda a: a[:, None]
    d = {"x": i["L0_attn_x"]}
    qkv = i["L1_attn_W_attn"]
    q_b, k_b, v_b = np.split(i["L1_attn_b_attn"], 3)
    projections = {"a0": [i["L0_attn_" + k].T for k in ("Wq", "Wk", "Wv", "Wo")],
                   "a1": [qkv[:, 0:DIM], qkv[:, DIM:2 * DIM], qkv[:, 2 * DIM:], i["L1_attn_W_proj"]]}
    columns = []
    for n, window in (("a0", SEQ), ("a1", LOCAL_WINDOW)):
        wq, wk, wv, wo = projections[n]
        d[f"{n}_mask_rows"], mask = _masks(window)
        columns.append(mask)
        d[f"{n}_wq"], d[f"{n}_wk"], d[f"{n}_wv"], d[f"{n}_wo"] = _stack_columns(wq), _stack_columns(wk), wv, wo
    d["pack"] = np.concatenate([np.eye(P, dtype=np.float32), _row_masks(), _ramp(), _far_mask(), *columns], axis=1)
    d["a0_const_rows"] = _constant_rows(True)
    d["a1_const_rows"] = _constant_rows(False, q_b, k_b)
    d["a1_bias"] = rows_of(np.concatenate([v_b, i["L1_attn_b_proj"]]))
    f = {k[len("L0_ffn_"):]: a for k, a in i.items() if k.startswith("L0_ffn_")}
    for n in ("ln1_w", "ln1_b", "ln2_w", "ln2_b", "k_b"):
        d[n] = column(f[n])
    d.update(gate_w=f["attn_gate_w"], k_w=f["k_w"], v_w=f["v_w"], o_b=f["o_b"], v_b=rows_of(f["v_b"]),
             q_w=f["q_w"].transpose(1, 0, 2).reshape(DIM, EA * HD), q_b=f["q_b"].T,
             o_w=f["o_w"].transpose(1, 0, 2).reshape(HD, EA * DIM), rel_t=f["rel_table"].T,
             ff_gate_w=f["ff_gate_w"], ff_w1=f["ff_w1"].transpose(1, 0, 2).reshape(DIM, EF * FH),
             ff_b1=f["ff_b1"].reshape(FF_CHUNKS, P).T,
             ff_w2=f["ff_w2"].reshape(FF_CHUNKS, P, DIM).transpose(1, 0, 2).reshape(P, FF_CHUNKS * DIM),
             ff_b2=_twice(f["ff_b2"]), select=_select(), low_mask=_low_mask(),
             experts=rows_of(np.arange(EF, dtype=np.float32)))
    d.update(Ws=i["L1_ffn_Ws"], bs=rows_of(i["L1_ffn_bs"]), Wg=_up_columns(i["L1_ffn_Wg"]), Wu=_up_columns(i["L1_ffn_Wu"]),
             Wd=_down_rows(i["L1_ffn_Wd"]))
    return {n: np.ascontiguousarray(a) for n, a in d.items()}


def kernel(**inputs):
    import concourse.bacc as bacc
    from concourse.bass_utils import run_bass_kernel_spmd

    nc = bacc.Bacc("TRN2", target_bir_lowering=False, num_devices=1)
    data = _laid_out({n: np.asarray(a) for n, a in inputs.items()})
    arrays, d = {}, {}
    for name, a in data.items():
        arrays[f"in_{name}"] = a
        d[name] = nc.dram_tensor(f"in_{name}", a.shape, mybir.dt.from_np(a.dtype), kind="ExternalInput").ap()
    out = nc.dram_tensor("out", (BATCH, SEQ, DIM), F32, kind="ExternalOutput").ap()
    two_layers(nc, d, out)
    return run_bass_kernel_spmd(nc, [arrays], core_ids=[0]).results[0]["out"]
```
